# Optimizing a Trainium2 kernel written in Bass

```python
import numpy as np
import jax
import jax.numpy as jnp

def _softmax(x, axis=-1):
    return jax.nn.softmax(x, axis=axis)

def _gelu(x):
    return jax.nn.gelu(x, approximate=True)

def _silu(x):
    return jax.nn.silu(x)

def _sigmoid(x):
    return jax.nn.sigmoid(x)

def _layernorm(x, axis=-1, eps=1e-05):
    m = jnp.mean(x, axis=axis, keepdims=True)
    v = jnp.var(x, axis=axis, keepdims=True)
    return (x - m) / jnp.sqrt(v + eps)

def _scatter_add(tgt, idx, src, axis=0):
    return tgt.at[idx].add(src)

def _segment_sum(src, seg, n):
    return jax.ops.segment_sum(src, seg, n)
kernel_name = 'mk_gnn_resnorm_d2_gnn_r8_3ed26a'

def setup_inputs(seed: int=0):
    np.random.seed(seed)
    _w = jnp.asarray

    def _rec_inputs():
        import jax
        import jax.numpy as jnp
        _gk = jax.random.key(seed)
        x = -0.0002949 + 1 * jax.random.normal(jax.random.fold_in(_gk, 1), (1250, 512), jnp.float32)
        _s = jax.random.randint(jax.random.fold_in(_gk, 2), (10000,), 0, 1250, jnp.int32)
        _d = jax.random.randint(jax.random.fold_in(_gk, 3), (10000,), 0, 1250, jnp.int32)
        _loop = jnp.arange(1250, dtype=jnp.int32)
        src = jnp.concatenate([_s, _d, _loop])
        dst = jnp.concatenate([_d, _s, _loop])
        _o = jnp.argsort(dst, stable=True)
        src = src[_o]
        dst = dst[_o]
        edge_type_32 = jax.random.randint(jax.random.fold_in(_gk, 13), (21250,), 0, 32, jnp.int32)
        edge_weight1 = jax.random.uniform(jax.random.fold_in(_gk, 14), (21250, 1), jnp.float32, 0.0, 0.999996)
        node_vec1 = jax.random.uniform(jax.random.fold_in(_gk, 15), (1250, 1), jnp.float32, 0.0, 0.999957)
        return (x, src, dst, edge_type_32, edge_weight1, node_vec1)
    x, src, dst, edge_type_32, edge_weight1, node_vec1 = _rec_inputs()

    def _L0_gnn_setup():
        import jax, jax.numpy as jnp
        import numpy as np
        N_NODES = 40962
        LATENT_DIM = 512
        N_EDGES = 81924
        NUM_BLOCKS = 4
        NUM_HEADS = 4
        NUM_FREQ = 32
        BASE_PERIOD = 16
        NOISE_EMB_DIM = 16
        EPS = 1e-05

        def _cond_layer_norm(x, cond, sw, sb, bw, bb):
            mu = jnp.mean(x, axis=-1, keepdims=True)
            var = jnp.var(x, axis=-1, keepdims=True)
            xn = (x - mu) * jax.lax.rsqrt(var + EPS)
            scale = cond @ sw + sb
            bias = cond @ bw + bb
            return xn * (1.0 + scale) + bias

        def _sparse_attention(x, src, dst, wq, bq, wk, bk, wv, bv, wo, bo):
            N, D = x.shape
            H, Dh = (NUM_HEADS, D // NUM_HEADS)
            q = (x @ wq + bq).reshape(N, H, Dh) * Dh ** (-0.5)
            k = (x @ wk + bk).reshape(N, H, Dh)
            v = (x @ wv + bv).reshape(N, H, Dh)
            scores = jnp.einsum('ehd,ehd->eh', q[src], k[dst])
            smax = jax.ops.segment_max(scores, src, num_segments=N)
            ex = jnp.exp(scores - smax[src])
            denom = jax.ops.segment_sum(ex, src, num_segments=N)
            attn = ex / denom[src]
            out = jax.ops.segment_sum(attn[:, :, None] * v[dst], src, num_segments=N)
            return out.reshape(N, D) @ wo + bo

        def _forward(x, edge_index, noise_levels, f_w1, f_b1, f_w2, f_b2, s1_w, s1_b, b1_w, b1_b, wq, bq, wk, bk, wv, bv, wo, bo, s2_w, s2_b, b2_w, b2_b, m_w1, m_b1, m_w2, m_b2):
            src, dst = (edge_index[0], edge_index[1])
            freqs = jnp.arange(1, NUM_FREQ + 1, dtype=x.dtype) * (2.0 * np.pi / BASE_PERIOD)
            ph = noise_levels * freqs
            emb = jnp.concatenate([jnp.sin(ph), jnp.cos(ph)], axis=-1)
            cond = jax.nn.silu(emb @ f_w1 + f_b1) @ f_w2 + f_b2
            for i in range(NUM_BLOCKS):
                y = _cond_layer_norm(x, cond, s1_w[i], s1_b[i], b1_w[i], b1_b[i])
                y = _sparse_attention(y, src, dst, wq[i], bq[i], wk[i], bk[i], wv[i], bv[i], wo[i], bo[i])
                x = x + y
                y = _cond_layer_norm(x, cond, s2_w[i], s2_b[i], b2_w[i], b2_b[i])
                y = jax.nn.relu(y @ m_w1[i] + m_b1[i]) @ m_w2[i] + m_b2[i]
                x = x + y
            return x
        key = jax.random.key(seed)
        ks = jax.random.split(key, 20)

        def w(k, shape, s=0.02):
            return jax.random.normal(k, shape, dtype=jnp.float32) * s
        D, B, C = (LATENT_DIM, NUM_BLOCKS, NOISE_EMB_DIM)
        z = lambda *s: jnp.zeros(s, jnp.float32)
        return {'latent_mesh_nodes': jax.random.normal(ks[0], (N_NODES, D), dtype=jnp.float32), 'edge_index': jax.random.randint(ks[1], (2, N_EDGES), 0, N_NODES, dtype=jnp.int32), 'noise_levels': jax.random.uniform(ks[2], (N_NODES, 1), dtype=jnp.float32), 'f_w1': w(ks[3], (2 * NUM_FREQ, C)), 'f_b1': z(C), 'f_w2': w(ks[4], (C, C)), 'f_b2': z(C), 's1_w': w(ks[5], (B, C, D)), 's1_b': z(B, D), 'b1_w': w(ks[6], (B, C, D)), 'b1_b': z(B, D), 'wq': w(ks[7], (B, D, D)), 'bq': z(B, D), 'wk': w(ks[8], (B, D, D)), 'bk': z(B, D), 'wv': w(ks[9], (B, D, D)), 'bv': z(B, D), 'wo': w(ks[10], (B, D, D)), 'bo': z(B, D), 's2_w': w(ks[11], (B, C, D)), 's2_b': z(B, D), 'b2_w': w(ks[12], (B, C, D)), 'b2_b': z(B, D), 'm_w1': w(ks[13], (B, D, D)), 'm_b1': z(B, D), 'm_w2': w(ks[14], (B, D, D)), 'm_b2': z(B, D)}
    _L0_gnn_all = _L0_gnn_setup()
    _L0_gnn_in = {k: v for k, v in _L0_gnn_all.items() if k in ('f_w1', 'f_b1', 'f_w2', 'f_b2', 's1_w', 's1_b', 'b1_w', 'b1_b', 'wq', 'bq', 'wk', 'bk', 'wv', 'bv', 'wo', 'bo', 's2_w', 's2_b', 'b2_w', 'b2_b', 'm_w1', 'm_b1', 'm_w2', 'm_b2')}
    del _L0_gnn_all

    def _L1_gnn_setup():
        import jax, jax.numpy as jnp
        import numpy as np
        N_NODES = 2500
        N_EDGES = 40000
        IN_FEAT = 512
        OUT_FEAT = 512
        NUM_RELS = 32
        NUM_BASES = 8
        key = jax.random.key(seed)
        ks = jax.random.split(key, 8)
        x = jax.random.normal(ks[0], (N_NODES, IN_FEAT), dtype=jnp.float32)
        bases = jax.random.normal(ks[1], (NUM_BASES, IN_FEAT, OUT_FEAT), dtype=jnp.float32) * (1.0 / np.sqrt(IN_FEAT))
        w_comp = jax.random.normal(ks[2], (NUM_RELS, NUM_BASES), dtype=jnp.float32) * (1.0 / np.sqrt(NUM_BASES))
        h_bias = jnp.zeros((OUT_FEAT,), dtype=jnp.float32)
        norm = jax.random.uniform(ks[3], (N_EDGES, 1), dtype=jnp.float32)
        src = jax.random.randint(ks[4], (N_EDGES,), 0, N_NODES, dtype=jnp.int32)
        dst = jax.random.randint(ks[5], (N_EDGES,), 0, N_NODES, dtype=jnp.int32)
        etype = jnp.sort(jax.random.randint(ks[6], (N_EDGES,), 0, NUM_RELS, dtype=jnp.int32))
        return {'x': x, 'bases': bases, 'w_comp': w_comp, 'h_bias': h_bias, 'norm': norm, 'src': src, 'dst': dst, 'etype': etype}
    _L1_gnn_all = _L1_gnn_setup()
    _L1_gnn_in = {k: v for k, v in _L1_gnn_all.items() if k in ('bases', 'w_comp', 'h_bias')}
    del _L1_gnn_all
    return {'x': x, 'src': src, 'dst': dst, 'edge_type_32': edge_type_32, 'edge_weight1': edge_weight1, 'node_vec1': node_vec1, 'L0_gnn_f_w1': _L0_gnn_in['f_w1'], 'L0_gnn_f_b1': _L0_gnn_in['f_b1'], 'L0_gnn_f_w2': _L0_gnn_in['f_w2'], 'L0_gnn_f_b2': _L0_gnn_in['f_b2'], 'L0_gnn_s1_w': _L0_gnn_in['s1_w'], 'L0_gnn_s1_b': _L0_gnn_in['s1_b'], 'L0_gnn_b1_w': _L0_gnn_in['b1_w'], 'L0_gnn_b1_b': _L0_gnn_in['b1_b'], 'L0_gnn_wq': _L0_gnn_in['wq'], 'L0_gnn_bq': _L0_gnn_in['bq'], 'L0_gnn_wk': _L0_gnn_in['wk'], 'L0_gnn_bk': _L0_gnn_in['bk'], 'L0_gnn_wv': _L0_gnn_in['wv'], 'L0_gnn_bv': _L0_gnn_in['bv'], 'L0_gnn_wo': _L0_gnn_in['wo'], 'L0_gnn_bo': _L0_gnn_in['bo'], 'L0_gnn_s2_w': _L0_gnn_in['s2_w'], 'L0_gnn_s2_b': _L0_gnn_in['s2_b'], 'L0_gnn_b2_w': _L0_gnn_in['b2_w'], 'L0_gnn_b2_b': _L0_gnn_in['b2_b'], 'L0_gnn_m_w1': _L0_gnn_in['m_w1'], 'L0_gnn_m_b1': _L0_gnn_in['m_b1'], 'L0_gnn_m_w2': _L0_gnn_in['m_w2'], 'L0_gnn_m_b2': _L0_gnn_in['m_b2'], 'L1_gnn_bases': _L1_gnn_in['bases'], 'L1_gnn_w_comp': _L1_gnn_in['w_comp'], 'L1_gnn_h_bias': _L1_gnn_in['h_bias']}

def reference(x, src, dst, edge_type_32, edge_weight1, node_vec1, L0_gnn_f_w1, L0_gnn_f_b1, L0_gnn_f_w2, L0_gnn_f_b2, L0_gnn_s1_w, L0_gnn_s1_b, L0_gnn_b1_w, L0_gnn_b1_b, L0_gnn_wq, L0_gnn_bq, L0_gnn_wk, L0_gnn_bk, L0_gnn_wv, L0_gnn_bv, L0_gnn_wo, L0_gnn_bo, L0_gnn_s2_w, L0_gnn_s2_b, L0_gnn_b2_w, L0_gnn_b2_b, L0_gnn_m_w1, L0_gnn_m_b1, L0_gnn_m_w2, L0_gnn_m_b2, L1_gnn_bases, L1_gnn_w_comp, L1_gnn_h_bias):
    import jax
    import jax.numpy as jnp

    def _L0_gnn_ref(latent_mesh_nodes, edge_index, noise_levels, f_w1, f_b1, f_w2, f_b2, s1_w, s1_b, b1_w, b1_b, wq, bq, wk, bk, wv, bv, wo, bo, s2_w, s2_b, b2_w, b2_b, m_w1, m_b1, m_w2, m_b2):
        import jax, jax.numpy as jnp
        import numpy as np
        N_NODES = 40962
        LATENT_DIM = 512
        N_EDGES = 81924
        NUM_BLOCKS = 4
        NUM_HEADS = 4
        NUM_FREQ = 32
        BASE_PERIOD = 16
        NOISE_EMB_DIM = 16
        EPS = 1e-05

        def _cond_layer_norm(x, cond, sw, sb, bw, bb):
            mu = jnp.mean(x, axis=-1, keepdims=True)
            var = jnp.var(x, axis=-1, keepdims=True)
            xn = (x - mu) * jax.lax.rsqrt(var + EPS)
            scale = cond @ sw + sb
            bias = cond @ bw + bb
            return xn * (1.0 + scale) + bias

        def _sparse_attention(x, src, dst, wq, bq, wk, bk, wv, bv, wo, bo):
            N, D = x.shape
            H, Dh = (NUM_HEADS, D // NUM_HEADS)
            q = (x @ wq + bq).reshape(N, H, Dh) * Dh ** (-0.5)
            k = (x @ wk + bk).reshape(N, H, Dh)
            v = (x @ wv + bv).reshape(N, H, Dh)
            scores = jnp.einsum('ehd,ehd->eh', q[src], k[dst])
            smax = jax.ops.segment_max(scores, src, num_segments=N)
            ex = jnp.exp(scores - smax[src])
            denom = jax.ops.segment_sum(ex, src, num_segments=N)
            attn = ex / denom[src]
            out = jax.ops.segment_sum(attn[:, :, None] * v[dst], src, num_segments=N)
            return out.reshape(N, D) @ wo + bo

        def _forward(x, edge_index, noise_levels, f_w1, f_b1, f_w2, f_b2, s1_w, s1_b, b1_w, b1_b, wq, bq, wk, bk, wv, bv, wo, bo, s2_w, s2_b, b2_w, b2_b, m_w1, m_b1, m_w2, m_b2):
            src, dst = (edge_index[0], edge_index[1])
            freqs = jnp.arange(1, NUM_FREQ + 1, dtype=x.dtype) * (2.0 * np.pi / BASE_PERIOD)
            ph = noise_levels * freqs
            emb = jnp.concatenate([jnp.sin(ph), jnp.cos(ph)], axis=-1)
            cond = jax.nn.silu(emb @ f_w1 + f_b1) @ f_w2 + f_b2
            for i in range(NUM_BLOCKS):
                y = _cond_layer_norm(x, cond, s1_w[i], s1_b[i], b1_w[i], b1_b[i])
                y = _sparse_attention(y, src, dst, wq[i], bq[i], wk[i], bk[i], wv[i], bv[i], wo[i], bo[i])
                x = x + y
                y = _cond_layer_norm(x, cond, s2_w[i], s2_b[i], b2_w[i], b2_b[i])
                y = jax.nn.relu(y @ m_w1[i] + m_b1[i]) @ m_w2[i] + m_b2[i]
                x = x + y
            return x
        return _forward(latent_mesh_nodes, edge_index, noise_levels, f_w1, f_b1, f_w2, f_b2, s1_w, s1_b, b1_w, b1_b, wq, bq, wk, bk, wv, bv, wo, bo, s2_w, s2_b, b2_w, b2_b, m_w1, m_b1, m_w2, m_b2)

    def _L1_gnn_ref(x, bases, w_comp, h_bias, norm, src, dst, etype):
        import jax, jax.numpy as jnp
        import numpy as np
        N_NODES = 2500
        N_EDGES = 40000
        IN_FEAT = 512
        OUT_FEAT = 512
        NUM_RELS = 32
        NUM_BASES = 8
        n_nodes = x.shape[0]
        weight = jnp.einsum('rb,bio->rio', w_comp, bases)
        h_rel = jnp.einsum('ni,rio->rno', x, weight)
        msg = h_rel[etype, src] * norm
        out = jax.ops.segment_sum(msg, dst, num_segments=n_nodes)
        out = out + h_bias
        return out
    edge_index = jnp.stack([src, dst])
    x = _layernorm(x + _L0_gnn_ref(x, edge_index, node_vec1, L0_gnn_f_w1, L0_gnn_f_b1, L0_gnn_f_w2, L0_gnn_f_b2, L0_gnn_s1_w, L0_gnn_s1_b, L0_gnn_b1_w, L0_gnn_b1_b, L0_gnn_wq, L0_gnn_bq, L0_gnn_wk, L0_gnn_bk, L0_gnn_wv, L0_gnn_bv, L0_gnn_wo, L0_gnn_bo, L0_gnn_s2_w, L0_gnn_s2_b, L0_gnn_b2_w, L0_gnn_b2_b, L0_gnn_m_w1, L0_gnn_m_b1, L0_gnn_m_w2, L0_gnn_m_b2), axis=-1)
    x = _layernorm(x + _L1_gnn_ref(x, L1_gnn_bases, L1_gnn_w_comp, L1_gnn_h_bias, edge_weight1, src, dst, edge_type_32), axis=-1)
    return x

_drawn_inputs = setup_inputs


def setup_inputs(seed=0):
    import zlib

    import numpy as np

    out = dict(_drawn_inputs(seed))
    spreads = {'L0_gnn_f_b1': (0.0, 0.8),
     'L0_gnn_f_b2': (0.0, 0.8),
     'L0_gnn_s1_b': (0.0, 0.8),
     'L0_gnn_b1_b': (0.0, 0.324),
     'L0_gnn_bq': (0.0, 0.8),
     'L0_gnn_bk': (0.0, 0.8),
     'L0_gnn_bv': (0.0, 0.1),
     'L0_gnn_bo': (0.0, 0.1),
     'L0_gnn_s2_b': (0.0, 0.569),
     'L0_gnn_b2_b': (0.0, 0.51),
     'L0_gnn_m_b1': (0.0, 0.1),
     'L0_gnn_m_b2': (0.0, 0.1),
     'L1_gnn_h_bias': (0.0, 0.1)}
    factors = {'node_vec1': 8.0,
     'L0_gnn_f_w1': 8.0,
     'L0_gnn_f_w2': 8.0,
     'L0_gnn_s1_w': 8.0,
     'L0_gnn_b1_w': 8.0,
     'L0_gnn_wq': 5.727,
     'L0_gnn_wk': 5.566,
     'L0_gnn_s2_w': 8.0,
     'L0_gnn_b2_w': 8.0}
    for name, (base, spread) in spreads.items():
        noise = np.random.default_rng([zlib.crc32(name.encode()), seed]).standard_normal(out[name].shape)
        drawn = base * np.exp(spread * noise) if base else spread * noise
        out[name] = jnp.asarray(drawn.astype(out[name].dtype))
    for name, factor in factors.items():
        out[name] = (out[name] * factor).astype(out[name].dtype)
    return out
```

```python
from contextlib import ExitStack
import math

import concourse.bass as bass
from concourse import mybir

F32 = mybir.dt.float32
BF16 = mybir.dt.bfloat16
F16 = mybir.dt.float16
I32 = mybir.dt.int32
ALU = mybir.AluOpType
ACT = mybir.ActivationFunctionType
AX = mybir.AxisListType

P = 128
ds = bass.ds

COND_PART = [0, 0, 1, 0, 1, 2]
WEIGHT_PART = [0, 1, 0, 2, 1, 0]
NEG = -1.0e30
PAD_DST = 2047


class Chain:

    def __init__(self, eng, sem, base=0):
        self.eng, self.sem, self.base, self.n = eng, sem, base, 0

    def __call__(self, ins):
        ins.then_inc(self.sem, 1)
        self.n += 1
        self.eng.wait_ge(self.sem, self.base + self.n)


def graph_kernel(nc, A, out):
    N, D = A["x"].shape
    E = A["src"].shape[0]
    NB = A["L0_gnn_wq"].shape[0]
    NH = 4
    DH = D // NH
    KC = D // P
    NF = A["L0_gnn_f_w1"].shape[0] // 2
    CD = A["L0_gnn_f_w1"].shape[1]
    NT = 10
    TR = N // NT
    NP = NT // 2
    NR, BS = A["L1_gnn_w_comp"].shape
    assert TR * NT == N and TR <= P and DH == P
    SCALE = float(DH) ** -0.5
    KS = CD + 1
    KK = KS * len(COND_PART)
    HALF = -(-E // (2 * P))
    CH = 2 * HALF
    NPIECE = 8
    CH = -(-CH // NPIECE) * NPIECE
    HALF = CH // 2
    PCH = CH // NPIECE
    CHP = CH + 4
    CW, CU = NT, 2
    WD = P // BS
    JW = -(-TR // WD)
    RW, RU = NT * JW, 4
    CHUNKS = [(o, min(512, N - o)) for o in range(0, N, 512)]

    x_r = A["x"].rearrange("(t p) d -> p t d", p=TR)
    out_r = out.rearrange("(t p) d -> p t d", p=TR)

    with ExitStack() as ctx:
        ctx.enter_context(nc.allow_non_contiguous_dma(reason="short columns of biases and tables"))

        def sb(name, shape, dt=F32):
            return ctx.enter_context(nc.sbuf_tensor(name, shape, dt))

        def sem(name):
            return ctx.enter_context(nc.semaphore(name))

        x1_dram = nc.dram_tensor("x1_dram", (N, D), F32).ap()
        chunk_dram = nc.dram_tensor("chunk_dram", (2, CH), F32).ap()
        stack_dram = nc.dram_tensor("stack_dram", (KK, 6 * NB + 2, D), BF16).ap()
        tabc_dram = nc.dram_tensor("tabc_dram", (CW, 4), I32).ap()
        tabr_dram = nc.dram_tensor("tabr_dram", (RW, 4), I32).ap()

        arena = sb("arena", [P, NT * N + KC * N * 2])
        Lb = arena[0:TR, 0:NT * N].rearrange("p (t n) -> p t n", t=NT)
        yT = arena[:, NT * N:NT * N + KC * N].rearrange("p (k n) -> p k n", k=KC)
        OT = arena[:, NT * N + KC * N:NT * N + 2 * KC * N].rearrange("p (k n) -> p k n", k=KC)
        xs_full = sb("xs", [P, NT, D])
        xs = xs_full[0:TR]
        QT = sb("QT", [P, N])
        KT = sb("KT", [P, N])
        V = sb("V", [P, NT, P])
        work = sb("work", [P, 2 * N + 2 * NT * 2 * TR])
        S = work[:, 0:2 * N].rearrange("p (u n) -> p u n", u=2)
        VT = work[:, N:2 * N]
        PT = work[:, 2 * N:].rearrange("p (b k c) -> p b k c", b=2, k=NT)
        wqkv = sb("wqkv", [P, 3, KC, P])
        bqkv = sb("bqkv", [P, 3])
        w3 = sb("w3", [P, 3, KC, D])
        Wo, W1, W2 = (w3[:, j] for j in range(3))
        b1c = sb("b1c", [P, KC])
        stack = sb("stack", [P, 6, D], BF16)
        condS = sb("condS", [P, N], BF16)
        ident = sb("ident", [P, P])
        zeros = sb("zeros", [P, 512], BF16)
        iota16 = sb("iota16", [P, N + 32], F16)
        ed = sb("ed", [P, 4, CHP])
        srci = sb("srci", [P, CHP], I32)
        coef = sb("coef", [P, CHP, BS])
        rb = sb("rb", [P, 2, 2 * TR])
        small = sb("small", [P, 128])
        tabc = sb("tabc", [1, 4 * CW + 4], I32)
        tabr = sb("tabr", [1, 4 * RW + 4], I32)
        eps = small[:, 0:1]
        iop = small[:, 1:2]
        mx = small[0:TR, 8:18]
        nmx = small[0:TR, 18:28]
        den = small[0:TR, 28:38]
        rden = small[0:TR, 38:48]
        rrec = small[0:TR, 48:58]
        has = small[0:TR, 58:68]
        st6 = small[0:TR, 68:92].rearrange("p (r c) -> p r c", r=4)
        mv = small[0:TR, 92:100].rearrange("p (r c) -> p r c", r=4)
        sd = small[0:TR, 100:104]
        rstd = small[0:TR, 104:108]
        o = 0
        def take(n):
            nonlocal o
            o += n
            assert o <= work.shape[1]
            return work[:, o - n:o]
        ybuf = take(4 * D).rearrange("p (r d) -> p r d", r=4)
        xnb = take(2 * D).rearrange("p (r d) -> p r d", r=2)
        y2T = take(KC * 2 * TR).rearrange("p (k c) -> p k c", k=KC)
        hT = take(KC * 2 * TR).rearrange("p (k c) -> p k c", k=KC)

        ps = ctx.enter_context(nc.psum_tensor("ps", [P, 8 * 512], F32))
        def bank(b, n=1):
            return ps[:, 512 * b:512 * (b + n)]
        ps_s = bank(0, 3)
        ps_t = bank(3, 3)
        ps_t3 = ps_t[:, 0:NT * P].rearrange("p (k c) -> p k c", c=P)
        ps_o = bank(6).rearrange("p (b c) -> p b c", b=2)
        ps_r = bank(7).rearrange("p (b c) -> p b c", b=2)
        ps_a = [bank(0), bank(1)]
        ps_sc, ps_bi = bank(2), bank(3)
        ps_tt = [bank(4), bank(5)]
        ps_h = bank(6, 2).rearrange("p (f c) -> p f c", f=KC)

        erow_i = QT[0:HALF, 0:3 * 2 * P].bitcast(I32).rearrange("p (a h r) -> p a h r", a=3, h=2)
        erow = KT[0:HALF, 0:4 * 2 * P].rearrange("p (a h r) -> p a h r", a=4, h=2)
        cmm = sb("cmm", [P, 2, 2])
        cmB = V[:, 0:3, :].rearrange("p a b -> p (a b)")[:, 0:2 * CH].rearrange("p (a c) -> p a c", a=2)
        tA = V[:, 3:5, :].rearrange("p a b -> p (a b)")[:, 0:CH]
        tB = V[:, 5:7, :].rearrange("p a b -> p (a b)")[:, 0:CH]
        tI = V[:, 7:9, :].rearrange("p a b -> p (a b)")[:, 0:CH]
        w3f = w3[:, :, :, :].rearrange("p a k d -> p (a k d)")
        tri = w3f[:, 0:P]
        tc_ = sb("tc_", [P, 16])
        tci = sb("tci", [P, 12], I32)
        tri2 = w3f[:, P:2 * P]
        par = w3f[:, 2 * P:3 * P].bitcast(I32)
        oa = arena[:, NT * N + KC * N:]
        nlb = oa[0:2 * NF, 0:N]
        ph = oa[0:2 * NF, N:2 * N]
        nn = oa[0:2 * NF, 2 * N:3 * N]
        emb = oa[0:2 * NF, 3 * N:4 * N]
        ez = nn[0:CD]
        hh = ph[0:CD]
        ya = arena[:, NT * N:NT * N + KC * N]
        ct = ya[0:KS, 0:N]
        cr = ya[0:KS, N:2 * N]
        csp = ya[0:KS, 2 * N:2 * N + 3 * N // 2].bitcast(BF16).rearrange("p (a n) -> p a n", a=3)
        cw = w3f[:, 3 * P:3 * P + 64]
        fw1 = cw[0:2 * NF, 0:CD]
        fw2 = cw[0:CD, 16:16 + CD]
        fb1, nb1, fb2 = cw[0:CD, 32:33], cw[0:CD, 33:34], cw[0:CD, 34:35]
        fr = cw[0:2 * NF, 35:36]
        off1, off2 = cw[0:2 * NF, 36:37], cw[0:2 * NF, 37:38]
        fri = cw[0:2 * NF, 38:39].bitcast(I32)
        wc = cw[0:NR, 40:40 + BS]
        rel = cw[0:NR, 48:49]
        WN = 6 * D
        wf = arena[0:NB * KS, 0:WN]
        wr = arena[0:NB * KS, WN:2 * WN]
        wsp = arena[0:NB * KS, 2 * WN:2 * WN + 3 * WN // 2].bitcast(BF16).rearrange("p (a n) -> p a n", a=3)
        etb = work[0:NR, 0:PCH * P].bitcast(I32)
        oh32 = work[0:NR, PCH * P:2 * PCH * P]
        OS = work[:, 0:N].bitcast(BF16).rearrange("p (b n) -> p b n", b=2)
        OD = work[:, N:N + P].bitcast(BF16).rearrange("p (b n) -> p b n", b=2)
        lnt = work[0:TR, N + P:N + P + N].rearrange("p (t n) -> p t n", t=NT)

        bases = arena[:, 0:BS * KC * D].rearrange("p (b k d) -> p b k d", b=BS, k=KC)
        YT = arena[:, BS * KC * D:BS * KC * D + KC * BS * P].rearrange("p (k b n) -> p k b n", k=KC, b=BS)
        G = work[:, 0:2 * RU * D].rearrange("p (s j d) -> p s j d", s=2, j=RU)
        CO = w3f[:, 0:2 * RU * P].rearrange("p (s j c) -> p s j c", s=2, j=RU)
        Y = w3f[:, 1024:2048].rearrange("p (s d) -> p s d", s=2)
        OH = w3f[:, 2048:2048 + RU * WD].rearrange("p (j c) -> p j c", j=RU)
        hb = w3f[0:TR, 2560:2560 + D]
        fo = w3f[0:TR, 3072:3072 + 2 * D].rearrange("p (s d) -> p s d", s=2)
        idx = sb("idx", [P, 2, RU], I32)
        x0t = w3f[0:TR, 4096:5120].rearrange("p (s d) -> p s d", s=2)
        ln0 = w3f[0:TR, 5120:6144].rearrange("p (s d) -> p s d", s=2)

        names = """edge_in edge_rows edge_cols_ps edge_cols chunk_mm chunk_out chunk_in iotas tri_ready
        win_count win_prefix win_tab tab_out tab_in cond_in cond_emb cond_h1 cond_e cond_h cond_c ct_ready
        csp_ready condS_in wf_in wsp_ready wstack_out coef_in etype_in etype_oh coef_ps coef_done
        oh_ready oh_used cnt_done cnt_free cnt_max cnt_ln bias_done x_in memset_done
        w_in proj proj_ev vt_ps v_ready qk scored negmax exped probs_t pt_ready pv r_ps r_ready rden_ready
        ot_ready mlpw_in stats std y_ready cond_ps ln_t lnT_ready wo_ps x_added w1_ps h_ready
        in_even in_odd fin_x fin_std x1_ready x1_out base_in rg_idx rg_in0 rg_in1 rg_coef rg_used y_ps y_sb y_t yT_sb rel_ps rel_read
        rg_std out_ready out_done0 out_done1 dve_pro dve_piece dve_cnt dve_head dve_ln dve_fin dve_rg dve_rgt pool_pro head_loaded gate"""
        s = {n: sem(n) for n in names.split()}

        block = ctx.enter_context(nc.Block())

        def mlp_steps():
            steps = []
            for a in range(NT + 6):
                st = []
                if a < NT:
                    st.append(("A", a))
                if 0 <= a - 2 < NT:
                    st.append(("B", a - 2))
                    if (a - 2) % 2:
                        st.append(("C", (a - 2) // 2))
                if 0 <= a - 4 < NT:
                    st.append(("D", a - 4))
                if 0 <= a - 6 < NT:
                    st.append(("E", a - 6))
                steps.append(st)
            return steps
        STEPS = mlp_steps()
        LNQ = {}
        for st in STEPS:
            for kind, t in st:
                if kind in "AD":
                    LNQ[kind, t] = len(LNQ)
        NLN = len(LNQ)
        assert NLN % 4 == 0

        def ln_base(i):
            return NT + NLN * i

        def last_in_half(k, u0p, nup):
            return u0p + k + nup * ((k + 255) // 256) + 1

        @block.sync
        def _(sp):
            def load(dst, src, s_, n=None):
                sp.dma_start(dst, src).then_inc(s_, 16)

            sp.wait_ge(s["memset_done"], 1)
            for a, name in enumerate(("src", "dst", "edge_type_32")):
                for h in range(2):
                    lo, hi = h * HALF * P, min(E, (h + 1) * HALF * P)
                    rows = (hi - lo) // P
                    load(erow_i[0:rows, a, h, :], A[name][lo:lo + rows * P].rearrange("(c r) -> c r", r=P), s["edge_in"])
                    rest = hi - lo - rows * P
                    if rest:
                        load(erow_i[rows:rows + 1, a, h, 0:rest],
                             A[name][hi - rest:hi].rearrange("(c r) -> c r", c=1), s["edge_in"])
            for h in range(2):
                lo, hi = h * HALF * P, min(E, (h + 1) * HALF * P)
                rows = (hi - lo) // P
                ew = A["edge_weight1"].rearrange("e o -> (e o)")
                load(erow[0:rows, 3, h, :], ew[lo:lo + rows * P].rearrange("(c r) -> c r", r=P), s["edge_in"])
                rest = hi - lo - rows * P
                if rest:
                    load(erow[rows:rows + 1, 3, h, 0:rest],
                         ew[hi - rest:hi].rearrange("(c r) -> c r", c=1), s["edge_in"])
            load(nlb, A["node_vec1"].rearrange("n o -> o n").broadcast_to([2 * NF, N]), s["cond_in"])
            load(fw1, A["L0_gnn_f_w1"], s["cond_in"])
            load(fw2, A["L0_gnn_f_w2"], s["cond_in"])
            load(fb1, A["L0_gnn_f_b1"].rearrange("(c o) -> c o", o=1), s["cond_in"])
            load(fb2, A["L0_gnn_f_b2"].rearrange("(c o) -> c o", o=1), s["cond_in"])
            load(wc, A["L1_gnn_w_comp"], s["coef_in"])
            sp.wait_ge(s["memset_done"], 2)
            for i in range(NB):
                for j, (w, b) in enumerate((("s1_w", "s1_b"), ("b1_w", "b1_b"), (None, "bo"), (None, "m_b2"),
                                            ("s2_w", "s2_b"), ("b2_w", "b2_b"))):
                    c = slice(j * D, (j + 1) * D)
                    if w:
                        load(wf[i * KS:i * KS + CD, c], A["L0_gnn_" + w][i], s["wf_in"])
                    load(wf[i * KS + CD:i * KS + KS, c], A["L0_gnn_" + b][i:i + 1], s["wf_in"])
            sp.dma_start(xs, x_r).then_inc(s["x_in"], 16)
            sp.wait_ge(s["chunk_mm"], 1)
            for m in range(2):
                sp.dma_start(chunk_dram[m:m + 1, :].rearrange("o (h c) -> c (o h)", h=2),
                             cmm[0:HALF, m, :]).then_inc(s["chunk_out"], 16)
            sp.wait_ge(s["chunk_out"], 32)
            for m in range(2):
                sp.dma_start(cmB[:, m, :], chunk_dram[m:m + 1, :].broadcast_to([P, CH])).then_inc(s["chunk_in"], 16)
            for k, (dr, tb, W) in enumerate(((tabc_dram, tabc, CW), (tabr_dram, tabr, RW))):
                sp.wait_ge(s["win_tab"], k + 1)
                sp.dma_start(dr, tci[0:W, 4 * k:4 * k + 4]).then_inc(s["tab_out"], 16)
                sp.wait_ge(s["tab_out"], 16 * (k + 1))
                sp.dma_start(tb[0:1, 4:], dr.rearrange("(o w) c -> o (w c)", o=1)).then_inc(s["tab_in"], 16)
            sp.wait_ge(s["wsp_ready"], 1)
            for g, b in enumerate(WEIGHT_PART):
                for i in range(NB + 1):
                    k = 6 if i < NB else 2
                    ii = i % NB
                    sp.dma_start(stack_dram[g * KS:(g + 1) * KS, 6 * i:6 * i + k, :].rearrange("r k d -> r (k d)"),
                                 wsp[ii * KS:(ii + 1) * KS, b, 0:k * D]).then_inc(s["wstack_out"], 16)
            sp.wait_ge(s["wstack_out"], 16 * len(WEIGHT_PART) * (NB + 1))
            sp.dma_start(stack[0:KK, 4:6, :], stack_dram[:, 0:2, :]).then_inc(s["mlpw_in"], 16)
            sp.wait_ge(s["csp_ready"], 1)
            for g, a in enumerate(COND_PART):
                sp.dma_start(condS[g * KS:(g + 1) * KS, :], csp[:, a, :]).then_inc(s["condS_in"], 16)
            for p in range(NPIECE):
                lo, hi = p * PCH * P, min(E, (p + 1) * PCH * P)
                if p:
                    sp.wait_ge(s["etype_oh"], p)
                sp.dma_start(etb[:, 0:hi - lo],
                             A["edge_type_32"][lo:hi].rearrange("(o e) -> o e", o=1).broadcast_to([NR, hi - lo])
                             ).then_inc(s["etype_in"], 16)

            with sp.Fori(0, NB) as i:
                with sp.Fori(0, NH) as h:
                    g = i * NH + h
                    sp.wait_ge(s["proj_ev"], g * 3 + 1)
                    for m, w in enumerate("qkv"):
                        sp.dma_start(wqkv[:, m, :, :],
                                     A["L0_gnn_w" + w][ds(i, 1), :, ds(h * DH, DH)].rearrange("o (k p) d -> p (o k) d", p=P)
                                     ).then_inc(s["w_in"], 16)
                        sp.dma_start(bqkv[:, m:m + 1],
                                     A["L0_gnn_b" + w][ds(i, 1), ds(h * DH, DH)].rearrange("o d -> d o")
                                     ).then_inc(s["w_in"], 16)
                sp.wait_ge(s["lnT_ready"], ln_base(i))
                for j, w in enumerate(("wo", "m_w1", "m_w2")):
                    sp.dma_start(w3[:, j], A["L0_gnn_" + w][ds(i, 1)].rearrange("o (k p) d -> p (o k) d", p=P)
                                 ).then_inc(s["mlpw_in"], 16)
                sp.dma_start(stack[0:KK], stack_dram[:, ds(6 * i + 2, 6), :]).then_inc(s["mlpw_in"], 16)
                sp.dma_start(b1c[:, :], A["L0_gnn_m_b1"][ds(i, 1)].rearrange("o (k p) -> p (o k)", p=P)
                             ).then_inc(s["mlpw_in"], 16)

            sp.wait_ge(s["lnT_ready"], ln_base(NB))
            sp.dma_start(hb, A["L1_gnn_h_bias"].rearrange("(o d) -> o d", o=1).broadcast_to([TR, D])
                         ).then_inc(s["base_in"], 16)
            for b in range(BS):
                sp.dma_start(bases[:, b], A["L1_gnn_bases"][b].rearrange("(k p) d -> p k d", p=P)
                             ).then_inc(s["base_in"], 16)
            for t in range(NT):
                if t >= 2:
                    sp.wait_ge(s["fin_x"], t - 1)
                sp.dma_start(x0t[:, t % 2], x_r[:, t, :]).then_inc(s["in_odd" if t % 2 else "in_even"], 16)
            for t in range(NT):
                sp.wait_ge(s["x1_ready"], t + 1)
                sp.dma_start(x1_dram[t * TR:(t + 1) * TR, :], xs[:, t, :]).then_inc(s["x1_out"], 16)
            with sp.Fori(0, NP) as tp:
                for u in range(2):
                    sp.wait_ge(s["out_ready"], 2 * tp + u + 1)
                    sp.dma_start(out_r[:, ds(2 * tp + u, 1), :], fo[:, u:u + 1, :]).then_inc(s["out_done%d" % u], 16)
            for u in range(2):
                sp.wait_ge(s["out_done%d" % u], 16 * NP + 16)

        @block.gpsimd
        def _(pool):
            ch = Chain(pool, s["pool_pro"])
            ch(pool.memset(erow_i[:, 0], 0))
            ch(pool.memset(erow_i[:, 1], PAD_DST))
            ch(pool.memset(erow_i[:, 2], 0))
            ch(pool.memset(erow[:, 3], 0.0))
            pool.sem_inc(s["memset_done"], 1)
            ch(pool.memset(wf, 0.0))
            pool.sem_inc(s["memset_done"], 1)
            ch(pool.memset(ident[:, :], 0.0))
            ch(pool.memset(tri[:, :], 0.0))
            ch(pool.memset(zeros[:, :], 0.0))
            ch(pool.memset(eps, 1e-5))
            ch(pool.memset(ct, 1.0))
            ch(pool.memset(ed[:, 0], 0.0))
            ch(pool.memset(ed[:, 1], float(PAD_DST)))
            ch(pool.memset(ed[:, 2:4], 0.0))
            ch(pool.memset(off1[0:NF], 0.0))
            ch(pool.memset(off2[0:NF], 0.0))
            ch(pool.memset(off1[NF:2 * NF], 0.25))
            ch(pool.memset(off2[NF:2 * NF], math.pi / 2))
            ch(pool.memset(coef[:, CH:CHP, :], 0.0))
            ch(pool.affine_select(out=ident[:, :], in_=ident[:, :], compare_op=ALU.not_equal, fill=1.0, base=0,
                               pattern=[[-1, P]], channel_multiplier=1))
            ch(pool.affine_select(out=tri[:, :], in_=tri[:, :], compare_op=ALU.is_ge, fill=1.0, base=0,
                               pattern=[[-1, P]], channel_multiplier=1))
            ch(pool.iota(iota16[:, :], [[1, N + 32]], base=0, channel_multiplier=0, allow_small_or_imprecise_dtypes=True))
            ch(pool.iota(tI, [[1, CH]], base=0, channel_multiplier=0, allow_small_or_imprecise_dtypes=True))
            ch(pool.iota(tci[:, 11:12], [[1, 1]], base=0, channel_multiplier=1))
            ch(pool.iota(par[:, :], [[-1, P]], base=2 * P, channel_multiplier=1))
            ch(pool.memset(tabr[0:1, 0:4], 0))
            ch(pool.memset(tabc[0:1, 0:4], 0))
            ch(pool.iota(rel, [[1, 1]], base=0, channel_multiplier=1, allow_small_or_imprecise_dtypes=True))
            ch(pool.iota(fri[0:NF], [[1, 1]], base=1, channel_multiplier=1))
            ch(pool.iota(fri[NF:2 * NF], [[1, 1]], base=1, channel_multiplier=1))
            pool.sem_inc(s["iotas"], 1)

            pool.wait_ge(s["x1_out"], 16 * NT)
            pool.wait_ge(s["tab_in"], 32)
            with pool.Fori(0, RW // 2) as wp:
                for sd_ in range(2):
                    w = 2 * wp + sd_
                    first = pool.value_load(tabr[0:1, ds(4 * w + 4, 1)], min_val=0, max_val=CH)
                    u0 = pool.value_load(tabr[0:1, ds(4 * w + 5, 1)], min_val=0, max_val=RW * (CH // RU + 1))
                    nu = pool.value_load(tabr[0:1, ds(4 * w + 6, 1)], min_val=0, max_val=RW * (CH // RU + 1))
                    u0p = pool.value_load(tabr[0:1, ds(4 * w + 1, 1)], min_val=0, max_val=RW * (CH // RU + 1))
                    nup = pool.value_load(tabr[0:1, ds(4 * w + 2, 1)], min_val=0, max_val=CH // RU + 1)
                    with pool.Fori(0, nu) as k_:
                        c = nc.s_assert_within(first + RU * k_, 0, CH)
                        pool.wait_ge(s["rg_used"], last_in_half(k_, u0p, nup))
                        pool.tensor_copy(idx[:, sd_, :], srci[:, ds(c, RU)]).then_inc(s["rg_idx"], 1)
                        pool.wait_ge(s["rg_idx"], u0 + k_ + 1)
                        pool.sem_inc(s["gate"], 1)
                        for j in range(RU):
                            pool.indirect_dma_start(G[:, sd_, j, :], None, x1_dram,
                                                    bass.IndirectOffsetOnAxis(ap=idx[:, sd_, j:j + 1], axis=0)
                                                    ).then_inc(s["rg_in%d" % sd_], 16)

        def act_lnT(act, n, bk, dst):
            act.wait_ge(s["ln_t"], n + 1)
            act.activation(dst, ps_tt[bk][:, 0:KC * P].rearrange("p (k c) -> p k c", k=KC)[:, :, 0:TR],
                           ACT.Copy).then_inc(s["lnT_ready"], 1)

        @block.scalar
        def _(act):
            act.sem_inc(s["proj_ev"], 1)
            act.wait_ge(s["cond_emb"], 1)
            act.activation(emb, ph, ACT.Sin).then_inc(s["cond_emb"], 1)
            act.wait_ge(s["cond_h1"], 1)
            act.activation(ez, ps_s[0:CD, 0:N], ACT.Exp, bias=nb1, scale=-1.0).then_inc(s["cond_e"], 1)
            with act.Fori(0, CW) as w:
                act.wait_ge(s["cnt_max"], w + 1)
                act.activation(lnt, lnt, ACT.Ln).then_inc(s["cnt_ln"], 1)
            for n in range(NT):
                act.wait_ge(s["stats"], n + 1)
                act.activation(sd[:, n % 4:n % 4 + 1], mv[:, n % 4, 1:2], ACT.Sqrt, bias=eps[0:TR]).then_inc(s["std"], 1)
                act_lnT(act, n, n % 2, yT[:, :, n * TR:(n + 1) * TR])

            with act.Fori(0, NB) as i:
                with act.Fori(0, NH) as h:
                    g = i * NH + h
                    for m, (src, dst) in enumerate(((ps_s, QT), (ps_t, KT), (ps_s, VT))):
                        if m == 0:
                            act.wait_ge(s["w_in"], 96 * g + 96)
                        act.wait_ge(s["proj"], 3 * g + m + 1)
                        act.activation(dst[:, 0:N], src[:, 0:N], ACT.Identity, bias=bqkv[:, m:m + 1]
                                       ).then_inc(s["proj_ev"], 1)
                    for a in range(NT + 3):
                        if a < NT:
                            t = a
                            act.wait_ge(s["negmax"], NT * g + t + 1)
                            act.activation(S[0:TR, t % 2], S[0:TR, t % 2], ACT.Exp, bias=nmx[:, t:t + 1], scale=SCALE,
                                           accum_out=den[:, t:t + 1]).then_inc(s["exped"], 1)
                        if 0 <= a - 1 < NT:
                            t = a - 1
                            q, u = divmod(t, 2)
                            act.wait_ge(s["probs_t"], NT * g + t + 1)
                            if u == 0 and q >= 2:
                                act.wait_ge(s["pv"], NP * g + q - 1)
                            act.activation(PT[0:TR, q % 2, :, u * TR:(u + 1) * TR], ps_t3[0:TR, :, 0:TR], ACT.Copy
                                           ).then_inc(s["pt_ready"], 1)
                            if u == 1:
                                act.wait_ge(s["r_ps"], NT * g + t + 1)
                                if q >= 2:
                                    act.wait_ge(s["ot_ready"], NP * g + q - 1)
                                act.activation(rb[:, q % 2, :], ps_r[:, q % 2, 0:2 * TR], ACT.Copy
                                               ).then_inc(s["r_ready"], 1)
                nb = ln_base(i)

                def std(n):
                    act.wait_ge(s["stats"], nb + n + 1)
                    act.activation(sd[:, (n + NT) % 4:(n + NT) % 4 + 1], mv[:, (n + NT) % 4, 1:2], ACT.Sqrt,
                                   bias=eps[0:TR]).then_inc(s["std"], 1)
                act.wait_ge(s["mlpw_in"], 80 * i + 96)
                for st in STEPS:
                    st = dict(st)
                    if "B" in st:
                        t = st["B"]
                        n = LNQ["A", t]
                        if t % 2 == 0 and t >= 2:
                            act.wait_ge(s["w1_ps"], NP * i + t // 2)
                        act_lnT(act, nb + n, (n + NT) % 2, y2T[:, :, (t % 2) * TR:(t % 2 + 1) * TR])
                    if "C" in st:
                        q = st["C"]
                        act.wait_ge(s["w1_ps"], NP * i + q + 1)
                        if q >= 1:
                            act.wait_ge(s["wo_ps"], NLN * i + LNQ["D", 2 * q - 1] + 1)
                        for f in range(KC):
                            last = act.activation(hT[:, f, :], ps_h[:, f, 0:2 * TR], ACT.Relu, bias=b1c[:, f:f + 1])
                        last.then_inc(s["h_ready"], 1)
                    if "A" in st:
                        std(LNQ["A", st["A"]])
                    if "D" in st:
                        std(LNQ["D", st["D"]])
                    if "E" in st:
                        t = st["E"]
                        n = LNQ["D", t]
                        act_lnT(act, nb + n, (n + NT) % 2, yT[:, :, t * TR:(t + 1) * TR])

            for t in range(NT):
                act.wait_ge(s["fin_x"], t + 1)
                act.activation(sd[:, t % 4:t % 4 + 1], mv[:, t % 4, 1:2], ACT.Sqrt, bias=eps[0:TR]).then_inc(s["fin_std"], 1)
            with act.Fori(0, NT) as T:
                with act.Fori(0, JW // 2) as jp:
                    for sd_ in range(2):
                        w = T * JW + 2 * jp + sd_
                        act.wait_ge(s["y_ps"], w + 1)
                        act.activation(Y[:, sd_], bank(sd_), ACT.Copy).then_inc(s["y_sb"], 1)
                        act.wait_ge(s["y_t"], w + 1)
                        act.wait_ge(s["rel_ps"], T + 1)
                        src = bank(2 + sd_).rearrange("p (k n b) -> p k b n", k=KC, b=BS)
                        for k in range(KC):
                            last = act.activation(YT[:, k, :, ds((2 * jp + sd_) * WD, WD)], src[:, k], ACT.Copy)
                        last.then_inc(s["yT_sb"], 1)
                act.wait_ge(s["rg_std"], 2 * T + 1)
                act.activation(sd[:, 0:1], mv[:, 0, 1:2], ACT.Sqrt, bias=eps[0:TR]).then_inc(s["rg_std"], 1)

        @block.tensor
        def _(pe):
            def mm(o_, l_, r_, start=True, stop=True):
                return pe.matmul(o_, l_, r_, start=start, stop=stop)

            pe.sem_inc(s["oh_used"], 2)
            pe.sem_inc(s["rg_used"], 1)
            pe.sem_inc(s["rel_ps"], 1)
            pe.wait_ge(s["iotas"], 1)
            pe.wait_ge(s["edge_rows"], 1)
            for a in range(4):
                for h in range(2):
                    c = (2 * a + h) * P
                    last = pe.transpose(ps[:, c:c + HALF], erow[:, a, h, :], ident[0:HALF, 0:HALF])
            last.then_inc(s["edge_cols_ps"], 1)
            for k, W in enumerate((CW, RW)):
                pe.wait_ge(s["win_count"], k + 1)
                pe.wait_ge(s["tri_ready"], 1)
                mm(bank(7)[0:W, 4 + k:5 + k], tri2[0:W, 0:W], tc_[0:W, 8 + k:9 + k])
                mm(bank(7)[0:W, k:k + 1], tri[0:W, 0:W], tc_[0:W, 8 + k:9 + k]).then_inc(s["win_prefix"], 1)
            pe.wait_ge(s["cond_in"], 80)
            pe.wait_ge(s["cond_emb"], 2)
            pe.wait_ge(s["edge_cols"], 1)
            for c0, cn in CHUNKS:
                last = mm(ps_s[0:CD, c0:c0 + cn], fw1, emb[:, c0:c0 + cn])
            last.then_inc(s["cond_h1"], 1)
            pe.wait_ge(s["cond_h"], 1)
            for c0, cn in CHUNKS:
                last = mm(ps_t[0:CD, c0:c0 + cn], fw2, hh[:, c0:c0 + cn])
            last.then_inc(s["cond_c"], 1)
            pe.wait_ge(s["coef_in"], 16)
            for p in range(NPIECE):
                pe.wait_ge(s["etype_oh"], p + 1)
                if p:
                    pe.wait_ge(s["coef_done"], p)
                for c in range(PCH):
                    last = mm(bank(6)[:, c * BS:(c + 1) * BS], oh32[:, c * P:(c + 1) * P], wc)
                last.then_inc(s["coef_ps"], 1)
            pe.wait_ge(s["tab_in"], 32)
            pe.wait_ge(s["ct_ready"], 1)
            with pe.Fori(0, CW) as w:
                u0 = pe.value_load(tabc[0:1, ds(4 * w + 5, 1)], min_val=0, max_val=CW * CH)
                nu = pe.value_load(tabc[0:1, ds(4 * w + 6, 1)], min_val=0, max_val=CW * CH)
                pe.wait_ge(s["cnt_free"], w + 1)
                for b in range(3):
                    mm(bank(b)[0:TR], zeros[:, 0:TR], zeros[:, :], True, False)
                with pe.Fori(0, nu) as k_:
                    for j in range(CU):
                        pe.wait_ge(s["oh_ready"], 2 * u0 + 2 * k_ + j + 1)
                        for t in range(NT):
                            last = mm(ps_s[0:TR, t * P:t * P + TR], OS[:, j, t * TR:(t + 1) * TR], OD[:, j, 0:TR], False, False)
                        last.then_inc(s["oh_used"], 1)
                for b in range(3):
                    last = mm(bank(b)[0:TR], zeros[:, 0:TR], zeros[:, :], False, True)
                last.then_inc(s["cnt_done"], 1)

            pe.wait_ge(s["bias_done"], 1)

            def cond_mm(n, t, j):
                for b, dst in enumerate((ps_sc, ps_bi)):
                    last = mm(dst[0:TR, :], condS[0:KK, t * TR:(t + 1) * TR], stack[0:KK, j + b, :])
                last.then_inc(s["cond_ps"], 1)

            def y_transpose(n, slot, bk):
                pe.wait_ge(s["y_ready"], n + 1)
                for k in range(KC):
                    last = pe.transpose(ps_tt[bk][:, k * P:k * P + TR], ybuf[0:TR, slot, k * P:(k + 1) * P],
                                        ident[0:TR, 0:TR])
                last.then_inc(s["ln_t"], 1)

            pe.wait_ge(s["condS_in"], 16 * len(COND_PART))
            pe.wait_ge(s["mlpw_in"], 16)
            for n in range(NT):
                if n:
                    pe.wait_ge(s["y_ready"], n)
                cond_mm(n, n, 4)
                if n >= 2:
                    pe.wait_ge(s["lnT_ready"], n - 1)
                y_transpose(n, n % 4, n % 2)

            with pe.Fori(0, NB) as i:
                with pe.Fori(0, NH) as h:
                    g = i * NH + h
                    pe.wait_ge(s["w_in"], 96 * g + 96)
                    pe.wait_ge(s["lnT_ready"], ln_base(i))
                    for m, dst in enumerate((ps_s, ps_t, ps_s)):
                        if m == 2:
                            pe.wait_ge(s["proj_ev"], 3 * g + 2)
                        for c0, cn in CHUNKS:
                            for k in range(KC):
                                last = mm(dst[:, c0:c0 + cn], wqkv[:, m, k, :], yT[:, k, c0:c0 + cn], k == 0, k == KC - 1)
                        last.then_inc(s["proj"], 1)
                    pe.wait_ge(s["proj_ev"], 3 * g + 4)
                    for t in range(NT):
                        last = pe.transpose(ps_t3[0:TR, t, :], VT[:, t * TR:(t + 1) * TR], ident[:, :])
                    last.then_inc(s["vt_ps"], 1)
                    for a in range(NT + 3):
                        if a < NT:
                            t = a
                            if t:
                                pe.wait_ge(s["scored"], NT * g + t)
                            for c0, cn in CHUNKS:
                                last = mm(ps_s[0:TR, c0:c0 + cn], QT[:, t * TR:(t + 1) * TR], KT[:, c0:c0 + cn])
                            last.then_inc(s["qk"], 1)
                        if 0 <= a - 3 < NT:
                            q, half = divmod(a - 3, 2)
                            if half == 0:
                                pe.wait_ge(s["pt_ready"], NT * g + 2 * q + 2)
                                pe.wait_ge(s["v_ready"], g + 1)
                                if q >= 1:
                                    pe.wait_ge(s["ot_ready"], NP * g + q)
                            for k in range(half * NP, (half + 1) * NP):
                                last = mm(ps_o[:, q % 2, 0:2 * TR], V[0:TR, k, :], PT[0:TR, q % 2, k, :],
                                          k == 0, k == NT - 1)
                            if half:
                                last.then_inc(s["pv"], 1)
                        if 0 <= a - 1 < NT:
                            t = a - 1
                            q, u = divmod(t, 2)
                            pe.wait_ge(s["exped"], NT * g + t + 1)
                            if t == 0:
                                pe.wait_ge(s["v_ready"], g + 1)
                            else:
                                pe.wait_ge(s["pt_ready"], NT * g + t)
                            for k in range(NT):
                                last = pe.transpose(ps_t3[0:TR, k, 0:TR], S[0:TR, t % 2, k * TR:(k + 1) * TR],
                                                    ident[0:TR, 0:TR])
                            last.then_inc(s["probs_t"], 1)
                            pe.wait_ge(s["rden_ready"], NT * g + t + 1)
                            if u == 0 and q >= 1:
                                pe.wait_ge(s["r_ready"], NP * g + q)
                            mm(ps_r[:, q % 2, u * TR:(u + 1) * TR], rden[:, t:t + 1].broadcast_to([TR, P]),
                               ident[0:TR, 0:TR]).then_inc(s["r_ps"], 1)
                nb = ln_base(i)
                pe.wait_ge(s["mlpw_in"], 80 * i + 96)
                pe.wait_ge(s["ot_ready"], NP * NH * i + NP * NH)

                def out_mm(n, t, lhs, w, j):
                    if n >= 2:
                        pe.wait_ge(s["x_added"], NLN * i + n - 1)
                    dst = ps_a[n % 2][0:TR, :]
                    mm(dst, condS[0:KK, t * TR:(t + 1) * TR], stack[0:KK, j, :], True, False)
                    for k in range(KC):
                        last = mm(dst, lhs(k), w[:, k, :], False, k == KC - 1)
                    last.then_inc(s["wo_ps"], 1)

                for st in STEPS:
                    for kind, t in st:
                        if kind == "A":
                            n = LNQ[kind, t]
                            out_mm(n, t, lambda k: OT[:, k, t * TR:(t + 1) * TR], Wo, 0)
                            pe.wait_ge(s["y_ready"], nb + n)
                            cond_mm(nb + n, t, 2)
                        if kind == "D":
                            n = LNQ[kind, t]
                            if t % 2 == 0:
                                pe.wait_ge(s["h_ready"], NP * i + t // 2 + 1)
                            out_mm(n, t, lambda k: hT[:, k, (t % 2) * TR:(t % 2 + 1) * TR], W2, 1)
                            pe.wait_ge(s["y_ready"], nb + n)
                            cond_mm(nb + n, t, 4)
                        if kind in "BE":
                            n = LNQ["A" if kind == "B" else "D", t]
                            pe.wait_ge(s["lnT_ready"], nb + n - 1)
                            y_transpose(nb + n, (n + NT) % 4, (n + NT) % 2)
                        if kind == "C":
                            q = t
                            pe.wait_ge(s["lnT_ready"], nb + LNQ["A", 2 * q + 1] + 1)
                            if q:
                                pe.wait_ge(s["h_ready"], NP * i + q)
                            for f in range(KC):
                                for k in range(KC):
                                    last = mm(ps_h[:, f, 0:2 * TR], W1[:, k, f * P:(f + 1) * P], y2T[:, k, :], k == 0, k == KC - 1)
                            last.then_inc(s["w1_ps"], 1)

            pe.wait_ge(s["base_in"], 16 * (BS + 1))
            with pe.Fori(0, NT) as T:
                with pe.Fori(0, JW // 2) as jp:
                    for sd_ in range(2):
                        w = T * JW + 2 * jp + sd_
                        u0 = pe.value_load(tabr[0:1, ds(4 * w + 5, 1)], min_val=0, max_val=RW * (CH // RU + 1))
                        nu = pe.value_load(tabr[0:1, ds(4 * w + 6, 1)], min_val=0, max_val=RW * (CH // RU + 1))
                        p0 = pe.value_load(tabr[0:1, ds(4 * w + 7, 1)], min_val=0, max_val=RW * (CH // RU + 1))
                        pe.wait_ge(s["y_sb"], w + 1)
                        mm(bank(sd_), zeros[:, 0:P], zeros[:, :], True, False)
                        with pe.Fori(0, nu) as k_:
                            pe.wait_ge(s["rg_coef"], u0 + k_ + 2)
                            pe.wait_ge(s["rg_in%d" % sd_], 16 * RU * (p0 + k_ + 1))
                            for j in range(RU):
                                last = mm(bank(sd_), CO[:, sd_, j, :], G[:, sd_, j, :], False, False)
                            last.then_inc(s["rg_used"], 1)
                        mm(bank(sd_), zeros[:, 0:P], zeros[:, :], False, True).then_inc(s["y_ps"], 1)
                        pe.wait_ge(s["y_sb"], w + 3)
                        pe.wait_ge(s["yT_sb"], w + 1)
                        for k in range(KC):
                            last = pe.transpose(bank(2 + sd_)[:, k * P:(k + 1) * P], Y[:, sd_, k * P:(k + 1) * P], ident[:, :])
                        last.then_inc(s["y_t"], 1)
                pe.wait_ge(s["yT_sb"], JW * T + JW + 2)
                pe.wait_ge(s["rel_read"], T + 1)
                for b in range(BS):
                    for k in range(KC):
                        last = mm(bank(4)[0:TR, :], YT[:, k, b, 0:TR], bases[:, b, k, :], b + k == 0,
                                  b == BS - 1 and k == KC - 1)
                last.then_inc(s["rel_ps"], 1)

        @block.vector
        def _(dve):
            ch = Chain(dve, s["dve_pro"])
            dve.sem_inc(s["cnt_free"], 1)
            dve.sem_inc(s["y_sb"], 2)
            dve.sem_inc(s["yT_sb"], 2)
            dve.sem_inc(s["rel_read"], 1)
            dve.sem_inc(s["rg_coef"], 1)
            dve.sem_inc(s["out_done0"], 16)
            dve.sem_inc(s["out_done1"], 16)
            nload = sum(1 + ((min(E, (h + 1) * HALF * P) - h * HALF * P) % P != 0) for h in range(2)) * 4
            dve.wait_ge(s["edge_in"], 16 * nload)
            dve.tensor_copy(erow[:, 0:3], erow_i[:, :]).then_inc(s["edge_rows"], 1)
            dve.wait_ge(s["edge_rows"], 1)
            dve.tensor_reduce(cmm[0:HALF, 0, :], erow[:, 1], AX.X, ALU.min)
            dve.tensor_reduce(cmm[0:HALF, 1, :], erow[:, 1], AX.X, ALU.max).then_inc(s["chunk_mm"], 1)
            dve.wait_ge(s["edge_cols_ps"], 1)
            dve.wait_ge(s["iotas"], 1)
            for a in range(4):
                ch(dve.tensor_copy(ed[:, a, 0:CH].rearrange("p (h c) -> p h c", h=2),
                                   ps[:, 2 * a * P:2 * (a + 1) * P].rearrange("p (h c) -> p h c", c=P)[:, :, 0:HALF]))
            ch(dve.tensor_copy(srci[:, :], ed[:, 0, :]))
            dve.sem_inc(s["edge_cols"], 1)
            ch(dve.tensor_scalar(par[:, :], par[:, :], 1, None, ALU.bitwise_and))
            ch(dve.tensor_copy(tri2[:, :], par[:, :]))
            ch(dve.tensor_scalar(tri2[:, :], tri2[:, :], 0.5, None, ALU.is_lt))
            dve.tensor_tensor(tri2[:, :], tri2[:, :], tri[:, :], ALU.mult).then_inc(s["tri_ready"], 1)
            dve.wait_ge(s["chunk_in"], 32)
            for k, (W, width, unit) in enumerate(((CW, TR, CU), (RW, WD, RU))):
                lo, hi = tc_[0:W, 0:1], tc_[0:W, 1:2]
                wi = tci[0:W, 11:12]
                first, last1, cnt = tc_[0:W, 2:3], tc_[0:W, 3:4], tc_[0:W, 8 + k:9 + k]
                ch(dve.tensor_copy(tc_[0:W, 4:5], wi))
                if k == 0:
                    ch(dve.tensor_scalar(lo, tc_[0:W, 4:5], float(TR), None, ALU.mult))
                else:
                    sh = JW.bit_length() - 1
                    assert 1 << sh == JW
                    ch(dve.tensor_scalar(tci[0:W, 8:9], wi, sh, None, ALU.logical_shift_right))
                    ch(dve.tensor_copy(tc_[0:W, 5:6], tci[0:W, 8:9]))
                    ch(dve.tensor_scalar(tc_[0:W, 5:6], tc_[0:W, 5:6], float(TR - WD * JW), None, ALU.mult))
                    ch(dve.scalar_tensor_tensor(lo, tc_[0:W, 4:5], float(WD), tc_[0:W, 5:6], ALU.mult, ALU.add))
                ch(dve.tensor_scalar(hi, lo, float(width - 1), None, ALU.add))
                ch(dve.tensor_scalar(tA[0:W], cmB[0:W, 1, :], lo, None, ALU.is_ge))
                ch(dve.scalar_tensor_tensor(tA[0:W], cmB[0:W, 0, :], hi, tA[0:W], ALU.is_le, ALU.mult))
                ch(dve.scalar_tensor_tensor(tB[0:W], tA[0:W], -1000.0, tI[0:W], ALU.mult, ALU.add))
                ch(dve.tensor_reduce(first, tB[0:W], AX.X, ALU.min))
                ch(dve.tensor_scalar(first, first, 1000.0, float(CH), ALU.add, ALU.min))
                ch(dve.tensor_scalar(tB[0:W], tI[0:W], 1.0, None, ALU.add))
                ch(dve.tensor_tensor(tB[0:W], tB[0:W], tA[0:W], ALU.mult))
                ch(dve.tensor_reduce(last1, tB[0:W], AX.X, ALU.max))
                ch(dve.tensor_tensor(last1, last1, first, ALU.subtract))
                ch(dve.tensor_scalar(last1, last1, 1.0, float(unit - 1), ALU.max, ALU.add))
                ch(dve.tensor_copy(tci[0:W, 8:9], last1))
                ch(dve.tensor_scalar(tci[0:W, 8:9], tci[0:W, 8:9], unit.bit_length() - 1, None, ALU.logical_shift_right))
                ch(dve.tensor_copy(cnt, tci[0:W, 8:9]))
                dve.sem_inc(s["win_count"], 1)
                dve.wait_ge(s["win_prefix"], k + 1)
                ch(dve.tensor_copy(tc_[0:W, 5:6], bank(7)[0:W, k:k + 1]))
                ch(dve.tensor_copy(tc_[0:W, 6:7], cnt))
                if k == 1:
                    dve.wait_ge(s["tab_out"], 16)
                dve.tensor_copy(tci[0:W, 4 * k:4 * k + 1], first)
                dve.tensor_copy(tci[0:W, 4 * k + 3:4 * k + 4], bank(7)[0:W, 4 + k:5 + k])
                ch(dve.tensor_copy(tci[0:W, 4 * k + 1:4 * k + 3], tc_[0:W, 5:7]))
                dve.sem_inc(s["win_tab"], 1)
            dve.wait_ge(s["wf_in"], 16 * NB * 10)
            ch(dve.tensor_copy(wsp[:, 0], wf))
            ch(dve.tensor_tensor(wr, wf, wsp[:, 0], ALU.subtract))
            ch(dve.tensor_copy(wsp[:, 1], wr))
            ch(dve.tensor_tensor(wr, wr, wsp[:, 1], ALU.subtract))
            dve.tensor_copy(wsp[:, 2], wr).then_inc(s["wsp_ready"], 1)
            dve.wait_ge(s["cond_in"], 80)
            ch(dve.tensor_copy(fr, fri))
            ch(dve.tensor_scalar(fr, fr, 2.0 * math.pi / 16.0, None, ALU.mult))
            ch(dve.tensor_scalar(ph, nlb, fr, None, ALU.mult))
            ch(dve.tensor_scalar(nn, ph, 1.0 / (2.0 * math.pi), off1, ALU.mult, ALU.add))
            magic = 12582912.0
            ch(dve.tensor_scalar(nn, nn, magic, None, ALU.add))
            ch(dve.tensor_scalar(nn, nn, magic, None, ALU.subtract))
            c1 = 6.28125
            c2 = float(int((2 * math.pi - c1) * 2 ** 21)) / 2 ** 21
            c3 = 2 * math.pi - c1 - c2
            for c in (c1, c2, c3):
                ch(dve.scalar_tensor_tensor(ph, nn, -c, ph, ALU.mult, ALU.add))
            ch(dve.tensor_scalar(ph, ph, off2, None, ALU.add))
            ch(dve.tensor_scalar(ph, ph, -3.1415925, 3.1415925, ALU.max, ALU.min))
            ch(dve.tensor_scalar(nb1, fb1, -1.0, None, ALU.mult))
            dve.sem_inc(s["cond_emb"], 1)
            dve.wait_ge(s["cond_e"], 1)
            ch(dve.tensor_scalar(ez, ez, 1.0, None, ALU.add))
            ch(dve.reciprocal(ez, ez))
            dve.scalar_tensor_tensor(hh, ps_s[0:CD, 0:N], fb1, ez, ALU.add, ALU.mult).then_inc(s["cond_h"], 1)
            dve.wait_ge(s["cond_c"], 1)
            dve.tensor_scalar(ct[0:CD], ps_t[0:CD, 0:N], fb2, None, ALU.add).then_inc(s["ct_ready"], 1)
            dve.wait_ge(s["ct_ready"], 1)
            ch(dve.tensor_copy(csp[:, 0], ct))
            ch(dve.tensor_tensor(cr, ct, csp[:, 0], ALU.subtract))
            ch(dve.tensor_copy(csp[:, 1], cr))
            ch(dve.tensor_tensor(cr, cr, csp[:, 1], ALU.subtract))
            dve.tensor_copy(csp[:, 2], cr).then_inc(s["csp_ready"], 1)
            for p in range(NPIECE):
                dve.wait_ge(s["etype_in"], 16 * (p + 1))
                if p:
                    dve.wait_ge(s["coef_ps"], p)
                n = min(E, (p + 1) * PCH * P) - p * PCH * P
                if n < PCH * P:
                    ch(dve.memset(oh32[:, n:PCH * P], 0.0))
                dve.tensor_scalar(oh32[:, 0:n], etb[:, 0:n], rel, None, ALU.is_equal).then_inc(s["etype_oh"], 1)
                dve.wait_ge(s["coef_ps"], p + 1)
                w_ = ed[:, 3, p * PCH:(p + 1) * PCH].unsqueeze(2).broadcast_to([P, PCH, BS])
                dve.tensor_tensor(coef[:, p * PCH:(p + 1) * PCH, :],
                                  bank(6)[:, 0:PCH * BS].rearrange("p (c b) -> p c b", b=BS), w_, ALU.mult
                                  ).then_inc(s["coef_done"], 1)
            dve.wait_ge(s["tab_in"], 32)
            dve.wait_ge(s["wstack_out"], 16 * len(WEIGHT_PART) * (NB + 1))
            with dve.Fori(0, CW) as w:
                first = dve.value_load(tabc[0:1, ds(4 * w + 4, 1)], min_val=0, max_val=CH)
                u0 = dve.value_load(tabc[0:1, ds(4 * w + 5, 1)], min_val=0, max_val=CW * CH)
                nu = dve.value_load(tabc[0:1, ds(4 * w + 6, 1)], min_val=0, max_val=CW * CH)
                with dve.Fori(0, nu) as k_:
                    for j in range(CU):
                        c = nc.s_assert_within(first + CU * k_ + j, 0, CHP - 1)
                        dve.wait_ge(s["oh_used"], 2 * u0 + 2 * k_ + j + 1)
                        dve.tensor_scalar(OS[:, j, :], iota16[:, 0:N], ed[:, 0, ds(c, 1)], None, ALU.is_equal)
                        dve.tensor_scalar(OD[:, j, 0:TR], iota16[:, ds(w * TR, TR)], ed[:, 1, ds(c, 1)], None,
                                          ALU.is_equal).then_inc(s["oh_ready"], 1)
                dve.wait_ge(s["cnt_done"], w + 1)
                cs = ps_s[0:TR, 0:NT * P].rearrange("p (t c) -> p t c", c=P)[:, :, 0:TR]
                Lw = Lb[:, :, ds(w * TR, TR)]
                dve.tensor_scalar(lnt, cs, 1.0, None, ALU.max).then_inc(s["cnt_max"], 1)
                dve.tensor_scalar(Lw, cs, 0.5, NEG, ALU.is_lt, ALU.mult).then_inc(s["cnt_free"], 1)
                dve.wait_ge(s["cnt_ln"], w + 1)
                dve.wait_ge(s["cnt_free"], w + 2)
                dve.scalar_tensor_tensor(Lw, lnt, 1.0 / SCALE, Lw, ALU.mult, ALU.add).then_inc(s["dve_cnt"], 1)
                dve.wait_ge(s["dve_cnt"], w + 1)
            ch(dve.tensor_reduce(has, Lb, AX.X, ALU.max))
            ch(dve.tensor_scalar(has, has, NEG / 2, None, ALU.is_gt))
            dve.sem_inc(s["bias_done"], 1)

            def layer_norm(n, r, t, c, add=None):
                x_ = xs[:, t, :]
                if add is not None:
                    dve.tensor_tensor(x_, x_, add, ALU.add).then_inc(s["x_added"], 1)
                    dve.wait_ge(s["x_added"], c)
                r4, r2 = r % 4, r % 2
                ins = dve.bn_stats(st6[:, r4, :], x_)
                ins.then_inc(s["dve_ln"], 1)
                dve.wait_ge(s["dve_ln"], 5 * n + 1)
                dve.sem_inc(s["gate"], 1)
                dve.bn_aggr(mv[:, r4, :], st6[:, r4, :]).then_inc(s["stats"], 1)
                dve.wait_ge(s["std"], n + 1)
                dve.reciprocal(rstd[:, r4:r4 + 1], sd[:, r4:r4 + 1]).then_inc(s["dve_ln"], 1)
                dve.wait_ge(s["dve_ln"], 5 * n + 2)
                dve.tensor_scalar(xnb[0:TR, r2], x_, mv[:, r4, 0:1], rstd[:, r4:r4 + 1], ALU.subtract, ALU.mult
                                  ).then_inc(s["dve_ln"], 1)
                dve.wait_ge(s["dve_ln"], 5 * n + 3)
                dve.wait_ge(s["cond_ps"], n + 1)
                dve.scalar_tensor_tensor(xnb[0:TR, r2], ps_sc[0:TR, :], 1.0, xnb[0:TR, r2], ALU.add, ALU.mult
                                         ).then_inc(s["dve_ln"], 1)
                dve.wait_ge(s["dve_ln"], 5 * n + 4)
                dve.tensor_tensor(ybuf[0:TR, r4], ps_bi[0:TR, :], xnb[0:TR, r2], ALU.add).then_inc(s["y_ready"], 1)
                dve.sem_inc(s["dve_ln"], 1)

            dve.wait_ge(s["x_in"], 16)
            for n in range(NT):
                if n >= 4:
                    dve.wait_ge(s["ln_t"], n - 3)
                layer_norm(n, n, n, None)

            with dve.Fori(0, NB) as i:
                with dve.Fori(0, NH) as h:
                    g = i * NH + h
                    dve.wait_ge(s["vt_ps"], g + 1)
                    dve.tensor_copy(V[0:TR], ps_t3[0:TR]).then_inc(s["v_ready"], 1)
                    for a in range(NT + 3):
                        if a < NT:
                            t = a
                            dve.wait_ge(s["qk"], NT * g + t + 1)
                            if t >= 2:
                                dve.wait_ge(s["probs_t"], NT * g + t - 1)
                            dve.sem_inc(s["gate"], 1)
                            dve.tensor_tensor_reduce(out=S[0:TR, t % 2], in0=ps_s[0:TR, 0:N], in1=Lb[:, t, :],
                                                     scale=1.0, scalar=-3.0e38, op0=ALU.add, op1=ALU.max,
                                                     accum_out=mx[:, t:t + 1]).then_inc(s["scored"], 1)
                            dve.wait_ge(s["scored"], NT * g + t + 1)
                            dve.tensor_scalar(nmx[:, t:t + 1], mx[:, t:t + 1], -SCALE, None, ALU.mult
                                              ).then_inc(s["negmax"], 1)
                        if 0 <= a - 1 < NT:
                            t = a - 1
                            dve.wait_ge(s["exped"], NT * g + t + 1)
                            dve.reciprocal(rrec[:, t:t + 1], den[:, t:t + 1]).then_inc(s["dve_head"], 1)
                            dve.wait_ge(s["dve_head"], NT * g + t + 1)
                            dve.tensor_tensor(rden[:, t:t + 1], rrec[:, t:t + 1], has[:, t:t + 1], ALU.mult
                                              ).then_inc(s["rden_ready"], 1)
                        if a >= 4 and a % 2 == 0:
                            q = (a - 4) // 2
                            dve.wait_ge(s["pv"], NP * g + q + 1)
                            dve.wait_ge(s["r_ready"], NP * g + q + 1)
                            dve.tensor_tensor(OT[:, ds(h, 1), q * 2 * TR:(q + 1) * 2 * TR].rearrange("p o c -> p (o c)"),
                                              ps_o[:, q % 2, 0:2 * TR], rb[:, q % 2, :], ALU.mult
                                              ).then_inc(s["ot_ready"], 1)
                nb = ln_base(i)
                for st in STEPS:
                    for kind, t in st:
                        if kind in "AD":
                            n = LNQ[kind, t]
                            dve.wait_ge(s["wo_ps"], NLN * i + n + 1)
                            dve.wait_ge(s["ln_t"], nb + n - 3)
                            layer_norm(nb + n, n + NT, t, NLN * i + n + 1, add=ps_a[n % 2][0:TR, :])

            for t in range(NT):
                ch2 = Chain(dve, s["dve_fin"], 4 * t)
                dve.wait_ge(s["in_odd" if t % 2 else "in_even"], 16 * (t // 2 + 1))
                ch2(dve.tensor_tensor(ln0[:, t % 2], xs[:, t, :], x0t[:, t % 2], ALU.add))
                ch2(dve.bn_stats(st6[:, t % 4, :], ln0[:, t % 2]))
                dve.bn_aggr(mv[:, t % 4, :], st6[:, t % 4, :]).then_inc(s["fin_x"], 1)
                dve.wait_ge(s["fin_std"], t + 1)
                ch2(dve.reciprocal(rstd[:, t % 4:t % 4 + 1], sd[:, t % 4:t % 4 + 1]))
                dve.tensor_scalar(xs[:, t, :], ln0[:, t % 2], mv[:, t % 4, 0:1], rstd[:, t % 4:t % 4 + 1],
                                  ALU.subtract, ALU.mult).then_inc(s["x1_ready"], 1)
                dve.sem_inc(s["dve_fin"], 1)

            dve.wait_ge(s["base_in"], 16 * (BS + 1))
            dve.wait_ge(s["x1_ready"], NT)
            with dve.Fori(0, NT // 2) as tp:
                for tu in range(2):
                    T = 2 * tp + tu
                    with dve.Fori(0, JW // 2) as jp:
                        for sd_ in range(2):
                            w = T * JW + 2 * jp + sd_
                            lo = T * TR + (2 * jp + sd_) * WD
                            first = dve.value_load(tabr[0:1, ds(4 * w + 4, 1)], min_val=0, max_val=CH)
                            u0 = dve.value_load(tabr[0:1, ds(4 * w + 5, 1)], min_val=0, max_val=RW * (CH // RU + 1))
                            nu = dve.value_load(tabr[0:1, ds(4 * w + 6, 1)], min_val=0, max_val=RW * (CH // RU + 1))
                            u0p = dve.value_load(tabr[0:1, ds(4 * w + 1, 1)], min_val=0, max_val=RW * (CH // RU + 1))
                            nup = dve.value_load(tabr[0:1, ds(4 * w + 2, 1)], min_val=0, max_val=CH // RU + 1)
                            with dve.Fori(0, nu) as k_:
                                c = nc.s_assert_within(first + RU * k_, 0, CH)
                                dve.wait_ge(s["rg_used"], last_in_half(k_, u0p, nup))
                                dve.wait_ge(s["rg_coef"], u0 + k_ + 1)
                                dve.tensor_tensor(OH, iota16[:, ds(lo, WD)].unsqueeze(1).broadcast_to([P, RU, WD]),
                                                  ed[:, 1, ds(c, RU)].unsqueeze(2).broadcast_to([P, RU, WD]),
                                                  ALU.is_equal).then_inc(s["dve_rg"], 1)
                                dve.wait_ge(s["dve_rg"], u0 + k_ + 1)
                                dve.tensor_tensor(CO[:, sd_].rearrange("p j (n b) -> p j n b", b=BS),
                                                  OH.unsqueeze(3).broadcast_to([P, RU, WD, BS]),
                                                  coef[:, ds(c, RU), :].unsqueeze(2).broadcast_to([P, RU, WD, BS]),
                                                  ALU.mult).then_inc(s["rg_coef"], 1)
                    ch3 = Chain(dve, s["dve_rgt"], 5 * T)
                    dve.wait_ge(s["rel_ps"], T + 2)
                    dve.tensor_tensor(ln0[:, 0], xs[:, ds(T, 1), :].rearrange("p o d -> p (o d)"), bank(4)[0:TR, :],
                                      ALU.add).then_inc(s["rel_read"], 1)
                    dve.wait_ge(s["rel_read"], T + 2)
                    ch3(dve.tensor_tensor(ln0[:, 0], ln0[:, 0], hb, ALU.add))
                    ch3(dve.bn_stats(st6[:, 0, :], ln0[:, 0]))
                    dve.sem_inc(s["gate"], 1)
                    ch3(dve.bn_aggr(mv[:, 0, :], st6[:, 0, :]))
                    dve.sem_inc(s["rg_std"], 1)
                    dve.wait_ge(s["rg_std"], 2 * T + 2)
                    ch3(dve.reciprocal(rstd[:, 0:1], sd[:, 0:1]))
                    dve.wait_ge(s["out_done%d" % tu], 16 * tp + 16)
                    dve.tensor_scalar(fo[:, tu], ln0[:, 0], mv[:, 0, 0:1], rstd[:, 0:1],
                                      ALU.subtract, ALU.mult).then_inc(s["out_ready"], 1)
                    dve.sem_inc(s["dve_rgt"], 1)


_INS = ["x", "src", "dst", "edge_type_32", "edge_weight1", "node_vec1",
        "L0_gnn_f_w1", "L0_gnn_f_b1", "L0_gnn_f_w2", "L0_gnn_f_b2", "L0_gnn_s1_w", "L0_gnn_s1_b", "L0_gnn_b1_w",
        "L0_gnn_b1_b", "L0_gnn_wq", "L0_gnn_bq", "L0_gnn_wk", "L0_gnn_bk", "L0_gnn_wv", "L0_gnn_bv", "L0_gnn_wo",
        "L0_gnn_bo", "L0_gnn_s2_w", "L0_gnn_s2_b", "L0_gnn_b2_w", "L0_gnn_b2_b", "L0_gnn_m_w1", "L0_gnn_m_b1",
        "L0_gnn_m_w2", "L0_gnn_m_b2", "L1_gnn_bases", "L1_gnn_w_comp", "L1_gnn_h_bias"]


def kernel(**inputs):
    import numpy as np
    import concourse.bacc as bacc
    from concourse.bass_utils import run_bass_kernel_spmd

    nc = bacc.Bacc("TRN2", target_bir_lowering=False, num_devices=1)
    arrays, aps = {}, {}
    for name in _INS:
        a = np.ascontiguousarray(inputs[name])
        arrays["in_" + name] = a
        aps[name] = nc.dram_tensor("in_" + name, a.shape, mybir.dt.from_np(a.dtype), kind="ExternalInput").ap()
    out = nc.dram_tensor("out", inputs["x"].shape, F32, kind="ExternalOutput").ap()
    graph_kernel(nc, aps, out)
    r = run_bass_kernel_spmd(nc, [arrays], core_ids=[0])
    return r.results[0]["out"]
```

```python
from contextlib import ExitStack
import math

import concourse.bass as bass
from concourse import mybir

F32 = mybir.dt.float32
BF16 = mybir.dt.bfloat16
F16 = mybir.dt.float16
I32 = mybir.dt.int32
ALU = mybir.AluOpType
ACT = mybir.ActivationFunctionType
AX = mybir.AxisListType

P = 128
ds = bass.ds

COND_PART = [0, 0, 1, 0, 1, 2]
WEIGHT_PART = [0, 1, 0, 2, 1, 0]
NEG = -1.0e30
PAD_DST = 2047


class Chain:

    def __init__(self, eng, sem, base=0):
        self.eng, self.sem, self.base, self.n = eng, sem, base, 0

    def __call__(self, ins):
        ins.then_inc(self.sem, 1)
        self.n += 1
        self.eng.wait_ge(self.sem, self.base + self.n)


def graph_kernel(nc, A, out):
    N, D = A["x"].shape
    E = A["src"].shape[0]
    NB = A["L0_gnn_wq"].shape[0]
    NH = 4
    DH = D // NH
    KC = D // P
    NF = A["L0_gnn_f_w1"].shape[0] // 2
    CD = A["L0_gnn_f_w1"].shape[1]
    NT = 10
    TR = N // NT
    NP = NT // 2
    NR, BS = A["L1_gnn_w_comp"].shape
    assert TR * NT == N and TR <= P and DH == P
    SCALE = float(DH) ** -0.5
    KS = CD + 1
    KK = KS * len(COND_PART)
    HALF = -(-E // (2 * P))
    CH = 2 * HALF
    CG = 8
    CH = -(-CH // CG) * CG
    HALF = CH // 2
    CHP = CH + 4
    CW, CU = NT, 4
    WD = P // BS
    JW = -(-TR // WD)
    RW, RU = NT * JW, 4
    NS = 4
    assert JW % NS == 0 and JW > NS
    TW = 6
    CHUNKS = [(o, min(512, N - o)) for o in range(0, N, 512)]
    Q1, Q2 = slice(0, 512), slice(512, N)

    x_r = A["x"].rearrange("(t p) d -> p t d", p=TR)
    out_r = out.rearrange("(t p) d -> p t d", p=TR)

    with ExitStack() as ctx:
        ctx.enter_context(nc.allow_non_contiguous_dma(reason="short columns of biases and tables"))

        def sb(name, shape, dt=F32):
            return ctx.enter_context(nc.sbuf_tensor(name, shape, dt))

        def sem(name):
            return ctx.enter_context(nc.semaphore(name))

        x1_dram = nc.dram_tensor("x1_dram", (N, D), F32).ap()
        chunk_dram = nc.dram_tensor("chunk_dram", (2, CH), F32).ap()
        stack_dram = nc.dram_tensor("stack_dram", (KK, 6 * NB + 2, D), BF16).ap()
        tabc_dram = nc.dram_tensor("tabc_dram", (CW, TW), I32).ap()
        tabr_dram = nc.dram_tensor("tabr_dram", (RW, TW), I32).ap()

        arena = sb("arena", [P, NT * N + KC * N * 2])
        Lb = arena[0:TR, 0:NT * N].rearrange("p (t n) -> p t n", t=NT)
        yT = arena[:, NT * N:NT * N + KC * N].rearrange("p (k n) -> p k n", k=KC)
        OT = arena[:, NT * N + KC * N:NT * N + 2 * KC * N].rearrange("p (k n) -> p k n", k=KC)
        xs_full = sb("xs", [P, NT, D])
        xs = xs_full[0:TR]
        hbuf = sb("hbuf", [P, 2 * N + NT * P + 3 * KC * P + P + 2 * N + 2 * NT * 2 * TR])
        o = 0

        def take(n):
            nonlocal o
            o += n
            assert o <= hbuf.shape[1]
            return hbuf[:, o - n:o]
        QT, KT = take(N), take(N)
        V = take(NT * P).rearrange("p (k d) -> p k d", k=NT)
        wqkv = take(3 * KC * P).rearrange("p (m k d) -> p m k d", m=3, k=KC)
        bvB = take(P)
        work = take(2 * N + 2 * NT * 2 * TR)
        S = work[:, 0:2 * N].rearrange("p (u n) -> p u n", u=2)
        PT = work[:, 2 * N:].rearrange("p (b k c) -> p b k c", b=2, k=NT)
        bqk = sb("bqk", [P, 2])
        w3 = sb("w3", [P, 3, KC, D])
        Wo, W1, W2 = (w3[:, j] for j in range(3))
        b1c = sb("b1c", [P, KC])
        stack = sb("stack", [P, 6, D], BF16)
        condS = sb("condS", [P, N], BF16)
        ident = sb("ident", [P, P])
        zeros = sb("zeros", [P, 512], BF16)
        iota16 = sb("iota16", [P, N + 32], F16)
        ed = sb("ed", [P, 4, CHP])
        cfi = sb("cfi", [P, CG], I32)
        cfg = sb("cfg", [P, CG, BS])
        coef = sb("coef", [P, CHP, BS])
        rb = sb("rb", [P, 2 * TR])
        small = sb("small", [P, 128])
        tabc = sb("tabc", [1, TW * CW], I32)
        tabr = sb("tabr", [1, TW * RW], I32)
        eps = small[:, 0:1]
        one, mone = small[:, 1:2], small[:, 2:3]
        mx = small[0:TR, 8:18]
        nmx = small[0:TR, 18:28]
        den = small[0:TR, 28:38]
        rden = small[0:TR, 38:48]
        rrec = small[0:TR, 48:58]
        noedge = small[0:TR, 58:68]
        st6 = small[0:TR, 68:92].rearrange("p (r c) -> p r c", r=4)
        mv = small[0:TR, 92:100].rearrange("p (r c) -> p r c", r=4)
        sd = small[0:TR, 100:104]
        rstd = small[0:TR, 104:108]
        o -= work.shape[1]
        ybuf = take(4 * D).rearrange("p (r d) -> p r d", r=4)
        xnb = take(2 * D).rearrange("p (r d) -> p r d", r=2)
        y2T = take(KC * 2 * TR).rearrange("p (k c) -> p k c", k=KC)
        hT = take(KC * 2 * TR).rearrange("p (k c) -> p k c", k=KC)

        ps = ctx.enter_context(nc.psum_tensor("ps", [P, 8 * 512], F32))
        def bank(b, n=1):
            return ps[:, 512 * b:512 * (b + n)]
        ps_s = bank(0, 3)
        ps_t = bank(3, 3)
        ps_t3 = ps_t[:, 0:NT * P].rearrange("p (k c) -> p k c", c=P)
        ps_o = bank(6).rearrange("p (b c) -> p b c", b=2)
        ps_r = bank(7).rearrange("p (b c) -> p b c", b=2)
        ps_a = [bank(0), bank(1)]
        ps_sc, ps_bi = bank(2), bank(3)
        ps_tt = [bank(4), bank(5)]
        ps_h = bank(6, 2).rearrange("p (f c) -> p f c", f=KC)

        erow_i = QT[0:HALF, 0:3 * 2 * P].bitcast(I32).rearrange("p (a h r) -> p a h r", a=3, h=2)
        erow = KT[0:HALF, 0:4 * 2 * P].rearrange("p (a h r) -> p a h r", a=4, h=2)
        cmm = sb("cmm", [P, 2, 2])
        cmB = V[:, 0:3, :].rearrange("p a b -> p (a b)")[:, 0:2 * CH].rearrange("p (a c) -> p a c", a=2)
        tA = V[:, 3:5, :].rearrange("p a b -> p (a b)")[:, 0:CH]
        tB = V[:, 5:7, :].rearrange("p a b -> p (a b)")[:, 0:CH]
        tI = V[:, 7:9, :].rearrange("p a b -> p (a b)")[:, 0:CH]
        w3f = w3[:, :, :, :].rearrange("p a k d -> p (a k d)")
        tri = w3f[:, 0:P]
        tc_ = sb("tc_", [P, 16])
        tci = sb("tci", [P, 16], I32)
        tri2 = w3f[:, P:2 * P]
        par = w3f[:, 2 * P:3 * P].bitcast(I32)
        oa = arena[:, NT * N + KC * N:]
        nlb = oa[0:2 * NF, 0:N]
        ph = oa[0:2 * NF, N:2 * N]
        nn = oa[0:2 * NF, 2 * N:3 * N]
        emb = oa[0:2 * NF, 3 * N:4 * N]
        ez = nn[0:CD]
        hh = ph[0:CD]
        ya = arena[:, NT * N:NT * N + KC * N]
        ct = ya[0:KS, 0:N]
        cr = ya[0:KS, N:2 * N]
        csp = ya[0:KS, 2 * N:2 * N + 3 * N // 2].bitcast(BF16).rearrange("p (a n) -> p a n", a=3)
        cw = w3f[:, 3 * P:3 * P + 64]
        fw1 = cw[0:2 * NF, 0:CD]
        fw2 = cw[0:CD, 16:16 + CD]
        fb1, nb1, fb2 = cw[0:CD, 32:33], cw[0:CD, 33:34], cw[0:CD, 34:35]
        fr = cw[0:2 * NF, 35:36]
        off1, off2 = cw[0:2 * NF, 36:37], cw[0:2 * NF, 37:38]
        fri = cw[0:2 * NF, 38:39].bitcast(I32)
        WN = 6 * D
        wf = xs_full[0:NB * KS, :, :].rearrange("p t d -> p (t d)")[:, 0:WN]
        wsp = w3f[0:NB * KS, 4 * P:4 * P + 3 * WN // 2].bitcast(BF16).rearrange("p (a n) -> p a n", a=3)
        OS = work[:, 0:CU * N // 2].bitcast(BF16).rearrange("p (b n) -> p b n", b=CU)
        OD = work[:, CU * N // 2:CU * N // 2 + CU * P // 2].bitcast(BF16).rearrange("p (b n) -> p b n", b=CU)
        lnt = work[0:TR, CU * (N + P) // 2:CU * (N + P) // 2 + 2 * N].rearrange("p (b t n) -> p b t n", b=2, t=NT)

        bases = arena[:, 0:BS * KC * D].rearrange("p (b k d) -> p b k d", b=BS, k=KC)
        YT = arena[:, BS * KC * D:BS * KC * D + KC * BS * P].rearrange("p (k b n) -> p k b n", k=KC, b=BS)
        G = hbuf[:, 0:NS * RU * D].rearrange("p (s j d) -> p s j d", s=NS, j=RU)
        o = NS * RU * D
        CO = take(NS * RU * P).rearrange("p (s j c) -> p s j c", s=NS, j=RU)
        Y = take(2 * D).rearrange("p (s d) -> p s d", s=2)
        OH = take(2 * RU * WD).rearrange("p (u j c) -> p u j c", u=2, j=RU)
        hb = w3f[0:TR, 2560:2560 + D]
        fo = w3f[0:TR, 3072:3072 + 2 * D].rearrange("p (s d) -> p s d", s=2)
        idx = sb("idx", [P, NS, RU], I32)
        x0t = w3f[0:TR, 4096:5120].rearrange("p (s d) -> p s d", s=2)
        ln0 = w3f[0:TR, 5120:6144].rearrange("p (s d) -> p s d", s=2)

        names = """edge_in edge_rows edge_cols_ps edge_cols chunk_mm chunk_out chunk_in iotas tri_ready
        win_count win_prefix win_tab tab_out tab_in cond_in cond_emb cond_h1 cond_e cond_h cond_c ct_ready
        csp_ready condS_in wf_in wsp_ready wstack_out cf_idx cf_in coef_done
        oh_ready oh_used cnt_done cnt_relu cnt_neg cnt_ln bias_done x_in memset_done
        wqk_in wv_in proj proj_ev vproj v_ready qk scored negmax exped probs_t pt_ready pv r_ps r_ready rden_ready
        ot_ready mlpw_in stats std y_ready cond_ps ln_t lnT_ready wo_ps x_added w1_ps h_ready
        in_even in_odd fin_x fin_std x1_ready x1_out base_in rg_idx rg_in0 rg_in1 rg_in2 rg_in3 rg_coef rg_4th0 rg_4th1 rg_4th2 rg_4th3 rg_xin0 rg_xin1 rg_xin2 rg_xin3 rg_xidx rg_xcoef rg_used y_ps y_sb y_t yT_sb rel_ps rel_read
        rg_stats rg_std out_ready out_done dve_pro dve_piece dve_cnt dve_head dve_ln dve_fin dve_rg dve_rgx dve_rgt pool_pro head_loaded gate"""
        s = {n: sem(n) for n in names.split()}

        block = ctx.enter_context(nc.Block())

        def mlp_steps():
            steps = []
            for a in range(NT + 6):
                st = []
                if a < NT:
                    st.append(("A", a))
                if 0 <= a - 2 < NT:
                    st.append(("B", a - 2))
                    if (a - 2) % 2:
                        st.append(("C", (a - 2) // 2))
                if 0 <= a - 4 < NT:
                    st.append(("D", a - 4))
                if 0 <= a - 6 < NT:
                    st.append(("E", a - 6))
                steps.append(st)
            return steps
        STEPS = mlp_steps()
        LNQ = {}
        for st in STEPS:
            for kind, t in st:
                if kind in "AD":
                    LNQ[kind, t] = len(LNQ)
        NLN = len(LNQ)
        assert NLN % 4 == 0

        def ln_base(i):
            return NT + NLN * i

        def entry(eng, w, c, hi=RW * (CH // RU + 1)):
            return eng.value_load(tabr[0:1, ds(TW * w + c, 1)], min_val=0, max_val=hi)
        FIRST, BEFORE, UNITS, SET_BEFORE, FOURTH, FOURTHS_BEFORE = range(TW)

        @block.sync
        def _(sp):
            def load(dst, src, s_, n=None):
                sp.dma_start(dst, src).then_inc(s_, 16)

            sp.wait_ge(s["memset_done"], 1)
            for a, name in enumerate(("src", "dst", "edge_type_32")):
                for h in range(2):
                    lo, hi = h * HALF * P, min(E, (h + 1) * HALF * P)
                    rows = (hi - lo) // P
                    load(erow_i[0:rows, a, h, :], A[name][lo:lo + rows * P].rearrange("(c r) -> c r", r=P), s["edge_in"])
                    rest = hi - lo - rows * P
                    if rest:
                        load(erow_i[rows:rows + 1, a, h, 0:rest],
                             A[name][hi - rest:hi].rearrange("(c r) -> c r", c=1), s["edge_in"])
            for h in range(2):
                lo, hi = h * HALF * P, min(E, (h + 1) * HALF * P)
                rows = (hi - lo) // P
                ew = A["edge_weight1"].rearrange("e o -> (e o)")
                load(erow[0:rows, 3, h, :], ew[lo:lo + rows * P].rearrange("(c r) -> c r", r=P), s["edge_in"])
                rest = hi - lo - rows * P
                if rest:
                    load(erow[rows:rows + 1, 3, h, 0:rest],
                         ew[hi - rest:hi].rearrange("(c r) -> c r", c=1), s["edge_in"])
            load(nlb, A["node_vec1"].rearrange("n o -> o n").broadcast_to([2 * NF, N]), s["cond_in"])
            load(fw1, A["L0_gnn_f_w1"], s["cond_in"])
            load(fw2, A["L0_gnn_f_w2"], s["cond_in"])
            load(fb1, A["L0_gnn_f_b1"].rearrange("(c o) -> c o", o=1), s["cond_in"])
            load(fb2, A["L0_gnn_f_b2"].rearrange("(c o) -> c o", o=1), s["cond_in"])
            sp.wait_ge(s["memset_done"], 2)
            for i in range(NB):
                for j, (w, b) in enumerate((("s1_w", "s1_b"), ("b1_w", "b1_b"), (None, "bo"), (None, "m_b2"),
                                            ("s2_w", "s2_b"), ("b2_w", "b2_b"))):
                    c = slice(j * D, (j + 1) * D)
                    if w:
                        load(wf[i * KS:i * KS + CD, c], A["L0_gnn_" + w][i], s["wf_in"])
                    load(wf[i * KS + CD:i * KS + KS, c], A["L0_gnn_" + b][i:i + 1], s["wf_in"])
            sp.wait_ge(s["chunk_mm"], 1)
            for m in range(2):
                sp.dma_start(chunk_dram[m:m + 1, :].rearrange("o (h c) -> c (o h)", h=2),
                             cmm[0:HALF, m, :]).then_inc(s["chunk_out"], 16)
            sp.wait_ge(s["chunk_out"], 32)
            for m in range(2):
                sp.dma_start(cmB[:, m, :], chunk_dram[m:m + 1, :].broadcast_to([P, CH])).then_inc(s["chunk_in"], 16)
            for k, (dr, tb, W) in enumerate(((tabc_dram, tabc, CW), (tabr_dram, tabr, RW))):
                sp.wait_ge(s["win_tab"], k + 1)
                sp.dma_start(dr, tci[0:W, TW * k:TW * k + TW]).then_inc(s["tab_out"], 16)
                sp.wait_ge(s["tab_out"], 16 * (k + 1))
                sp.dma_start(tb[0:1, :], dr.rearrange("(o w) c -> o (w c)", o=1)).then_inc(s["tab_in"], 16)
            sp.wait_ge(s["csp_ready"], 1)
            for g, a in enumerate(COND_PART):
                sp.dma_start(condS[g * KS:(g + 1) * KS, :], csp[:, a, :]).then_inc(s["condS_in"], 16)
            sp.wait_ge(s["wsp_ready"], 1)
            sp.dma_start(xs, x_r).then_inc(s["x_in"], 16)
            for g, b in enumerate(WEIGHT_PART):
                for i in range(NB + 1):
                    k = 6 if i < NB else 2
                    ii = i % NB
                    sp.dma_start(stack_dram[g * KS:(g + 1) * KS, 6 * i:6 * i + k, :].rearrange("r k d -> r (k d)"),
                                 wsp[ii * KS:(ii + 1) * KS, b, 0:k * D]).then_inc(s["wstack_out"], 16)
            sp.wait_ge(s["wstack_out"], 16 * len(WEIGHT_PART) * (NB + 1))
            sp.dma_start(stack[0:KK, 4:6, :], stack_dram[:, 0:2, :]).then_inc(s["mlpw_in"], 16)

            with sp.Fori(0, NB) as i:
                with sp.Fori(0, NH) as h:
                    g = i * NH + h
                    sp.wait_ge(s["proj_ev"], 3 * g + 1)
                    for m, w in enumerate("qk"):
                        sp.dma_start(wqkv[:, m, :, :],
                                     A["L0_gnn_w" + w][ds(i, 1), :, ds(h * DH, DH)].rearrange("o (k p) d -> p (o k) d", p=P)
                                     ).then_inc(s["wqk_in"], 16)
                        sp.dma_start(bqk[:, m:m + 1],
                                     A["L0_gnn_b" + w][ds(i, 1), ds(h * DH, DH)].rearrange("o d -> d o")
                                     ).then_inc(s["wqk_in"], 16)
                    sp.wait_ge(s["v_ready"], g + 1)
                    sp.dma_start(wqkv[:, 2, :, :],
                                 A["L0_gnn_wv"][ds(i, 1), :, ds(h * DH, DH)].rearrange("o (k p) d -> p (o k) d", p=P)
                                 ).then_inc(s["wv_in"], 16)
                    sp.dma_start(bvB[0:TR, :], A["L0_gnn_bv"][ds(i, 1), ds(h * DH, DH)].broadcast_to([TR, DH])
                                 ).then_inc(s["wv_in"], 16)
                sp.wait_ge(s["lnT_ready"], ln_base(i))
                for j, w in enumerate(("wo", "m_w1", "m_w2")):
                    sp.dma_start(w3[:, j], A["L0_gnn_" + w][ds(i, 1)].rearrange("o (k p) d -> p (o k) d", p=P)
                                 ).then_inc(s["mlpw_in"], 16)
                sp.dma_start(stack[0:KK], stack_dram[:, ds(6 * i + 2, 6), :]).then_inc(s["mlpw_in"], 16)
                sp.dma_start(b1c[:, :], A["L0_gnn_m_b1"][ds(i, 1)].rearrange("o (k p) -> p (o k)", p=P)
                             ).then_inc(s["mlpw_in"], 16)

            sp.wait_ge(s["ot_ready"], NP * NH * NB)
            early = NT * N // (KC * D)
            for b in range(early):
                sp.dma_start(bases[:, b], A["L1_gnn_bases"][b].rearrange("(k p) d -> p k d", p=P)
                             ).then_inc(s["base_in"], 16)
            sp.wait_ge(s["lnT_ready"], ln_base(NB))
            sp.dma_start(hb, A["L1_gnn_h_bias"].rearrange("(o d) -> o d", o=1).broadcast_to([TR, D])
                         ).then_inc(s["base_in"], 16)
            for t in range(NT):
                if t >= 2:
                    sp.wait_ge(s["fin_x"], t - 1)
                sp.dma_start(x0t[:, t % 2], x_r[:, t, :]).then_inc(s["in_odd" if t % 2 else "in_even"], 16)
            for b in range(early, BS):
                sp.dma_start(bases[:, b], A["L1_gnn_bases"][b].rearrange("(k p) d -> p k d", p=P)
                             ).then_inc(s["base_in"], 16)
            for t in range(NT):
                sp.wait_ge(s["x1_ready"], t + 1)
                sp.dma_start(x1_dram[t * TR:(t + 1) * TR, :], xs[:, t, :]).then_inc(s["x1_out"], 16)
            with sp.Fori(0, NT) as t:
                sp.wait_ge(s["out_ready"], t + 1)
                sp.dma_start(out_r[:, ds(t, 1), :], fo[:, 0:1, :]).then_inc(s["out_done"], 16)
            sp.wait_ge(s["out_done"], 16 * NT + 16)

        @block.gpsimd
        def _(pool):
            ch = Chain(pool, s["pool_pro"])
            ch(pool.memset(erow_i[:, 0], 0))
            ch(pool.memset(erow_i[:, 1], PAD_DST))
            ch(pool.memset(erow_i[:, 2], 0))
            ch(pool.memset(erow[:, 3], 0.0))
            pool.sem_inc(s["memset_done"], 1)
            ch(pool.memset(wf, 0.0))
            pool.sem_inc(s["memset_done"], 1)
            ch(pool.memset(ident[:, :], 0.0))
            ch(pool.memset(tri[:, :], 0.0))
            ch(pool.memset(zeros[:, :], 0.0))
            ch(pool.memset(eps, 1e-5))
            ch(pool.memset(one, 1.0))
            ch(pool.memset(mone, -1.0))
            ch(pool.memset(ct, 1.0))
            ch(pool.memset(ed[:, 0], 0.0))
            ch(pool.memset(ed[:, 1], float(PAD_DST)))
            ch(pool.memset(ed[:, 2:4], 0.0))
            ch(pool.memset(off1[0:NF], 0.0))
            ch(pool.memset(off2[0:NF], 0.0))
            ch(pool.memset(off1[NF:2 * NF], 0.25))
            ch(pool.memset(off2[NF:2 * NF], math.pi / 2))
            ch(pool.memset(coef[:, CH:CHP, :], 0.0))
            ch(pool.affine_select(out=ident[:, :], in_=ident[:, :], compare_op=ALU.not_equal, fill=1.0, base=0,
                               pattern=[[-1, P]], channel_multiplier=1))
            ch(pool.affine_select(out=tri[:, :], in_=tri[:, :], compare_op=ALU.is_ge, fill=1.0, base=0,
                               pattern=[[-1, P]], channel_multiplier=1))
            ch(pool.iota(iota16[:, :], [[1, N + 32]], base=0, channel_multiplier=0, allow_small_or_imprecise_dtypes=True))
            ch(pool.iota(tI, [[1, CH]], base=0, channel_multiplier=0, allow_small_or_imprecise_dtypes=True))
            ch(pool.iota(tci[:, 15:16], [[1, 1]], base=0, channel_multiplier=1))
            ch(pool.iota(par[:, :], [[-1, P]], base=2 * P, channel_multiplier=1))
            ch(pool.iota(fri[0:NF], [[1, 1]], base=1, channel_multiplier=1))
            ch(pool.iota(fri[NF:2 * NF], [[1, 1]], base=1, channel_multiplier=1))
            pool.sem_inc(s["iotas"], 1)

            pool.wait_ge(s["wf_in"], 16 * NB * 10)
            for a in range(3):
                ch(pool.tensor_copy(wsp[:, a], wf))
                if a < 2:
                    ch(pool.tensor_tensor(wf, wf, wsp[:, a], ALU.subtract))
            pool.sem_inc(s["wsp_ready"], 1)
            pool.wait_ge(s["edge_cols"], 1)
            with pool.Fori(0, CH // CG) as m:
                pool.tensor_copy(cfi[:, :], ed[:, 2, ds(CG * m, CG)]).then_inc(s["cf_idx"], 1)
                pool.wait_ge(s["cf_idx"], m + 1)
                pool.sem_inc(s["gate"], 1)
                for j in range(CG):
                    pool.indirect_dma_start(cfg[:, j, :], None, A["L1_gnn_w_comp"],
                                            bass.IndirectOffsetOnAxis(ap=cfi[:, j:j + 1], axis=0)
                                            ).then_inc(s["cf_in"], 16)
                pool.wait_ge(s["cf_in"], 16 * CG * (m + 1))
                pool.tensor_tensor(coef[:, ds(CG * m, CG), :], cfg[:, :, :],
                                   ed[:, 3, ds(CG * m, CG)].unsqueeze(2).broadcast_to([P, CG, BS]), ALU.mult
                                   ).then_inc(s["coef_done"], 1)
                pool.wait_ge(s["coef_done"], m + 1)

            pool.wait_ge(s["x1_out"], 16 * NT)
            pool.wait_ge(s["tab_in"], 32)

            def gather(st, c, k):
                pool.indirect_dma_start(G[:, st, k, :], None, x1_dram,
                                        bass.IndirectOffsetOnAxis(ap=idx[:, st, k:k + 1], axis=0)
                                        ).then_inc(s[c + str(st)], 16)

            def window(w, st, used):
                first = entry(pool, w, FIRST, CH)
                nu = entry(pool, w, UNITS)
                fourth = entry(pool, w, FOURTH, 1)
                if used is not None:
                    pool.wait_ge(s["y_ps"], used)
                pool.tensor_copy(idx[:, st, :], ed[:, 0, ds(first, RU)]).then_inc(s["rg_idx"], 1)
                pool.wait_ge(s["rg_idx"], w + 1)
                pool.sem_inc(s["gate"], 1)
                for j in range(RU - 1):
                    gather(st, "rg_in", j)
                with pool.If(fourth):
                    gather(st, "rg_4th", RU - 1)
                with pool.If(nu > 1), pool.Fori(1, nu) as k_:
                    c = nc.s_assert_within(first + RU * k_, 0, CH)
                    before = entry(pool, w, BEFORE)
                    pool.wait_ge(s["rg_used"], before + w + k_)
                    pool.tensor_copy(idx[:, st, :], ed[:, 0, ds(c, RU)]).then_inc(s["rg_xidx"], 1)
                    pool.wait_ge(s["rg_xidx"], before + k_)
                    pool.sem_inc(s["gate"], 1)
                    for j in range(RU):
                        gather(st, "rg_xin", j)

            for st in range(NS):
                window(st, st, None)
            with pool.Fori(0, RW // NS - 1) as wq:
                for st in range(NS):
                    window(NS * wq + NS + st, st, NS * wq + st + 1)

        def counts(b):
            return bank(3 * b, 3)[0:TR, 0:NT * P].rearrange("p (t c) -> p t c", c=P)[:, :, 0:TR]

        def act_lnT(act, n, bk, dst):
            act.wait_ge(s["ln_t"], n + 1)
            act.activation(dst, ps_tt[bk][:, 0:KC * P].rearrange("p (k c) -> p k c", k=KC)[:, :, 0:TR],
                           ACT.Copy).then_inc(s["lnT_ready"], 1)

        @block.scalar
        def _(act):
            act.sem_inc(s["proj_ev"], 1)
            act.wait_ge(s["cond_emb"], 1)
            act.activation(emb, ph, ACT.Sin).then_inc(s["cond_emb"], 1)
            act.wait_ge(s["cond_h1"], 1)
            act.activation(ez, ps_s[0:CD, 0:N], ACT.Exp, bias=nb1, scale=-1.0).then_inc(s["cond_e"], 1)
            act.sem_inc(s["cnt_relu"], 2)
            with act.Fori(0, CW // 2) as wp:
                for b in range(2):
                    w = 2 * wp + b
                    act.wait_ge(s["cnt_done"], w + 1)
                    act.wait_ge(s["dve_cnt"], w + 1)
                    act.activation(lnt[:, b], counts(b), ACT.Relu, bias=mone[0:TR]).then_inc(s["cnt_relu"], 1)
                    act.wait_ge(s["cnt_relu"], w + 3)
                    act.activation(lnt[:, b], lnt[:, b], ACT.Ln, bias=one[0:TR]).then_inc(s["cnt_ln"], 1)
            for n in range(NT):
                act.wait_ge(s["stats"], n + 1)
                act.activation(sd[:, n % 4:n % 4 + 1], mv[:, n % 4, 1:2], ACT.Sqrt, bias=eps[0:TR]).then_inc(s["std"], 1)
                act_lnT(act, n, n % 2, yT[:, :, n * TR:(n + 1) * TR])

            with act.Fori(0, NB) as i:
                def kq_evac(g):
                    act.wait_ge(s["wqk_in"], 64 * g + 64)
                    for n, (m, src, dst, c) in enumerate(((1, ps_s, KT, slice(0, N)), (0, ps_t, QT, Q1), (0, ps_t, QT, Q2))):
                        act.wait_ge(s["proj"], 3 * g + n + 1)
                        act.activation(dst[:, c], src[:, c], ACT.Identity, bias=bqk[:, m:m + 1]
                                       ).then_inc(s["proj_ev"], 1)

                def head(g, last):
                    for a in range(NT + 1):
                        if a < NT:
                            t = a
                            act.wait_ge(s["negmax"], NT * g + t + 1)
                            act.activation(S[0:TR, t % 2], S[0:TR, t % 2], ACT.Exp, bias=nmx[:, t:t + 1], scale=SCALE,
                                           accum_out=den[:, t:t + 1]).then_inc(s["exped"], 1)
                        if a:
                            t = a - 1
                            q, u = divmod(t, 2)
                            act.wait_ge(s["probs_t"], NT * g + t + 1)
                            if u == 0 and q >= 2:
                                act.wait_ge(s["pv"], NP * g + q - 1)
                            act.activation(PT[0:TR, q % 2, :, u * TR:(u + 1) * TR], ps_t3[0:TR, :, 0:TR], ACT.Copy
                                           ).then_inc(s["pt_ready"], 1)
                            if u == 1:
                                act.wait_ge(s["r_ps"], NT * g + t + 1)
                                if q >= 1:
                                    act.wait_ge(s["ot_ready"], NP * g + q)
                                act.activation(rb[:, :], ps_r[:, 0, 0:2 * TR], ACT.Copy).then_inc(s["r_ready"], 1)
                    if not last:
                        kq_evac(g + 1)
                kq_evac(i * NH)
                with act.Fori(0, NH - 1) as h:
                    head(i * NH + h, False)
                head(i * NH + NH - 1, True)
                nb = ln_base(i)

                def std(n):
                    act.wait_ge(s["stats"], nb + n + 1)
                    act.activation(sd[:, (n + NT) % 4:(n + NT) % 4 + 1], mv[:, (n + NT) % 4, 1:2], ACT.Sqrt,
                                   bias=eps[0:TR]).then_inc(s["std"], 1)
                act.wait_ge(s["mlpw_in"], 80 * i + 96)
                for st in STEPS:
                    st = dict(st)
                    if "B" in st:
                        t = st["B"]
                        n = LNQ["A", t]
                        if t % 2 == 0 and t >= 2:
                            act.wait_ge(s["w1_ps"], NP * i + t // 2)
                        act_lnT(act, nb + n, (n + NT) % 2, y2T[:, :, (t % 2) * TR:(t % 2 + 1) * TR])
                    if "A" in st:
                        std(LNQ["A", st["A"]])
                    if "C" in st:
                        q = st["C"]
                        act.wait_ge(s["w1_ps"], NP * i + q + 1)
                        if q >= 1:
                            act.wait_ge(s["wo_ps"], NLN * i + LNQ["D", 2 * q - 1] + 1)
                        for f in range(KC):
                            last = act.activation(hT[:, f, :], ps_h[:, f, 0:2 * TR], ACT.Relu, bias=b1c[:, f:f + 1])
                        last.then_inc(s["h_ready"], 1)
                    if "D" in st:
                        std(LNQ["D", st["D"]])
                    if "E" in st:
                        t = st["E"]
                        n = LNQ["D", t]
                        act_lnT(act, nb + n, (n + NT) % 2, yT[:, :, t * TR:(t + 1) * TR])

            for t in range(NT):
                act.wait_ge(s["fin_x"], t + 1)
                act.activation(sd[:, t % 4:t % 4 + 1], mv[:, t % 4, 1:2], ACT.Sqrt, bias=eps[0:TR]).then_inc(s["fin_std"], 1)
            def y_evac(T, j):
                act.wait_ge(s["y_ps"], T * JW + j + 1)
                act.activation(Y[:, j % 2], bank(j % 2), ACT.Copy).then_inc(s["y_sb"], 1)

            def yT_copy(T, j):
                act.wait_ge(s["y_t"], T * JW + j + 1)
                src = bank(2 + j % 2).rearrange("p (k n b) -> p k b n", k=KC, b=BS)
                for k in range(KC):
                    last = act.activation(YT[:, k, :, j * WD:(j + 1) * WD], src[:, k], ACT.Copy)
                last.then_inc(s["yT_sb"], 1)

            def rel_std(T):
                act.wait_ge(s["rg_stats"], T + 1)
                act.activation(sd[:, 0:1], mv[:, 0, 1:2], ACT.Sqrt, bias=eps[0:TR]).then_inc(s["rg_std"], 1)

            def tile(T, before):
                y_evac(T, 0)
                if before is not None:
                    yT_copy(before, JW - 1)
                for j in range(1, JW):
                    y_evac(T, j)
                    if j == 1 and before is not None:
                        act.wait_ge(s["rel_ps"], before + 1)
                    yT_copy(T, j - 1)
                    if j == 2 and before is not None:
                        rel_std(before)

            tile(0, None)
            with act.Fori(0, NT - 1) as T:
                tile(T + 1, T)
            yT_copy(NT - 1, JW - 1)
            rel_std(NT - 1)

        @block.tensor
        def _(pe):
            def mm(o_, l_, r_, start=True, stop=True):
                return pe.matmul(o_, l_, r_, start=start, stop=stop)

            pe.sem_inc(s["oh_used"], CU)
            pe.wait_ge(s["iotas"], 1)
            pe.wait_ge(s["edge_rows"], 1)
            for a in range(4):
                for h in range(2):
                    c = (2 * a + h) * P
                    last = pe.transpose(ps[:, c:c + HALF], erow[:, a, h, :], ident[0:HALF, 0:HALF])
            last.then_inc(s["edge_cols_ps"], 1)
            for k, W in enumerate((CW, RW)):
                pe.wait_ge(s["win_count"], k + 1)
                pe.wait_ge(s["tri_ready"], 1)
                mm(bank(7)[0:W, 4 + k:5 + k], tri2[0:W, 0:W], tc_[0:W, 8 + k:9 + k])
                mm(bank(7)[0:W, 6 + k:7 + k], tri2[0:W, 0:W], tc_[0:W, 11:12])
                mm(bank(7)[0:W, k:k + 1], tri[0:W, 0:W], tc_[0:W, 8 + k:9 + k]).then_inc(s["win_prefix"], 1)
            pe.wait_ge(s["cond_in"], 80)
            pe.wait_ge(s["cond_emb"], 2)
            pe.wait_ge(s["edge_cols"], 1)
            for c0, cn in CHUNKS:
                last = mm(ps_s[0:CD, c0:c0 + cn], fw1, emb[:, c0:c0 + cn])
            last.then_inc(s["cond_h1"], 1)
            pe.wait_ge(s["cond_h"], 1)
            for c0, cn in CHUNKS:
                last = mm(ps_t[0:CD, c0:c0 + cn], fw2, hh[:, c0:c0 + cn])
            last.then_inc(s["cond_c"], 1)
            pe.wait_ge(s["tab_in"], 32)
            pe.wait_ge(s["ct_ready"], 1)
            with pe.Fori(0, CW // 2) as wp:
                for b2 in range(2):
                    w = 2 * wp + b2
                    u0 = pe.value_load(tabc[0:1, ds(TW * w + 1, 1)], min_val=0, max_val=CW * CH)
                    nu = pe.value_load(tabc[0:1, ds(TW * w + 2, 1)], min_val=0, max_val=CW * CH)
                    pe.wait_ge(s["cnt_relu"], w + 1)
                    pe.wait_ge(s["cnt_neg"], w + 1)
                    for b in range(3):
                        mm(bank(3 * b2 + b)[0:TR], zeros[:, 0:TR], zeros[:, :], True, False)
                    with pe.Fori(0, nu) as k_:
                        for j in range(CU):
                            pe.wait_ge(s["oh_ready"], CU * u0 + CU * k_ + j + 1)
                            for t in range(NT):
                                last = mm(bank(3 * b2, 3)[0:TR, t * P:t * P + TR], OS[:, j, t * TR:(t + 1) * TR],
                                          OD[:, j, 0:TR], False, False)
                            last.then_inc(s["oh_used"], 1)
                    for b in range(3):
                        last = mm(bank(3 * b2 + b)[0:TR], zeros[:, 0:TR], zeros[:, :], False, True)
                    last.then_inc(s["cnt_done"], 1)

            pe.wait_ge(s["bias_done"], 1)

            def cond_mm(n, t, j):
                for b, dst in enumerate((ps_sc, ps_bi)):
                    last = mm(dst[0:TR, :], condS[0:KK, t * TR:(t + 1) * TR], stack[0:KK, j + b, :])
                last.then_inc(s["cond_ps"], 1)

            def y_transpose(n, slot, bk):
                pe.wait_ge(s["y_ready"], n + 1)
                for k in range(KC):
                    last = pe.transpose(ps_tt[bk][:, k * P:k * P + TR], ybuf[0:TR, slot, k * P:(k + 1) * P],
                                        ident[0:TR, 0:TR])
                last.then_inc(s["ln_t"], 1)

            pe.wait_ge(s["condS_in"], 16 * len(COND_PART))
            pe.wait_ge(s["mlpw_in"], 16)
            for n in range(NT):
                if n:
                    pe.wait_ge(s["y_ready"], n)
                cond_mm(n, n, 4)
                if n >= 2:
                    pe.wait_ge(s["lnT_ready"], n - 1)
                y_transpose(n, n % 4, n % 2)

            with pe.Fori(0, NB) as i:
                def kq_proj(g, n):
                    m, dst = ((1, ps_s), (0, ps_t))[n]
                    if n == 0:
                        pe.wait_ge(s["wqk_in"], 64 * g + 64)
                    for c0, cn in CHUNKS:
                        for k in range(KC):
                            last = mm(dst[:, c0:c0 + cn], wqkv[:, m, k, :], yT[:, k, c0:c0 + cn], k == 0, k == KC - 1)
                        if n == 1 and c0 == 0:
                            last.then_inc(s["proj"], 1)
                    last.then_inc(s["proj"], 1)

                def head(g, last_head):
                    pe.wait_ge(s["proj_ev"], 3 * g + 3)
                    for a in range(NT + 3):
                        if a < NT:
                            t = a
                            if t:
                                pe.wait_ge(s["scored"], NT * g + t)
                            for c0, cn in CHUNKS:
                                last = mm(ps_s[0:TR, c0:c0 + cn], QT[:, t * TR:(t + 1) * TR], KT[:, c0:c0 + cn])
                            last.then_inc(s["qk"], 1)
                        if 0 <= a - 2 < NT:
                            t = a - 2
                            q, u = divmod(t, 2)
                            pe.wait_ge(s["rden_ready"], NT * g + t + 1)
                            if u == 0 and q >= 1:
                                pe.wait_ge(s["r_ready"], NP * g + q)
                            mm(ps_r[:, 0, u * TR:(u + 1) * TR], rden[:, t:t + 1].broadcast_to([TR, P]),
                               ident[0:TR, 0:TR]).then_inc(s["r_ps"], 1)
                        if a == 0:
                            pe.wait_ge(s["wv_in"], 32 * g + 32)
                            pe.wait_ge(s["proj_ev"], 3 * g + 4)
                            for t in range(NT):
                                for k in range(KC):
                                    last = mm(ps_t3[0:TR, t, :], yT[:, k, t * TR:(t + 1) * TR], wqkv[:, 2, k, :],
                                              k == 0, k == KC - 1)
                            last.then_inc(s["vproj"], 1)
                        if 0 <= a - 3 < NT:
                            q, half = divmod(a - 3, 2)
                            if half == 0:
                                pe.wait_ge(s["pt_ready"], NT * g + 2 * q + 2)
                                if q >= 1:
                                    pe.wait_ge(s["ot_ready"], NP * g + q)
                            for k in range(half * NP, (half + 1) * NP):
                                last = mm(ps_o[:, 0, 0:2 * TR], V[0:TR, k, :], PT[0:TR, q % 2, k, :],
                                          k == 0, k == NT - 1)
                            if half:
                                last.then_inc(s["pv"], 1)
                        if 0 <= a - 1 < NT:
                            t = a - 1
                            q, u = divmod(t, 2)
                            pe.wait_ge(s["exped"], NT * g + t + 1)
                            if t == 0:
                                pe.wait_ge(s["v_ready"], g + 2)
                            else:
                                pe.wait_ge(s["pt_ready"], NT * g + t)
                            for k in range(NT):
                                last = pe.transpose(ps_t3[0:TR, k, 0:TR], S[0:TR, t % 2, k * TR:(k + 1) * TR],
                                                    ident[0:TR, 0:TR])
                            last.then_inc(s["probs_t"], 1)
                        if not last_head and a == NT:
                            kq_proj(g + 1, 0)
                        if not last_head and a == NT + 1:
                            pe.wait_ge(s["pt_ready"], NT * g + NT)
                            kq_proj(g + 1, 1)
                pe.wait_ge(s["lnT_ready"], ln_base(i))
                for n in range(2):
                    kq_proj(i * NH, n)
                with pe.Fori(0, NH - 1) as h:
                    head(i * NH + h, False)
                head(i * NH + NH - 1, True)
                nb = ln_base(i)
                pe.wait_ge(s["mlpw_in"], 80 * i + 96)
                pe.wait_ge(s["ot_ready"], NP * NH * i + NP * NH)

                def out_mm(n, t, lhs, w, j):
                    if n >= 2:
                        pe.wait_ge(s["x_added"], NLN * i + n - 1)
                    dst = ps_a[n % 2][0:TR, :]
                    mm(dst, condS[0:KK, t * TR:(t + 1) * TR], stack[0:KK, j, :], True, False)
                    for k in range(KC):
                        last = mm(dst, lhs(k), w[:, k, :], False, k == KC - 1)
                    last.then_inc(s["wo_ps"], 1)

                def scale_bias(kind, t, j):
                    n = LNQ[kind, t]
                    pe.wait_ge(s["y_ready"], nb + n)
                    cond_mm(nb + n, t, j)

                def transposed(kind, t):
                    n = LNQ[kind, t]
                    pe.wait_ge(s["lnT_ready"], nb + n - 1)
                    y_transpose(nb + n, (n + NT) % 4, (n + NT) % 2)

                for st in STEPS:
                    st = dict(st)
                    if "A" in st:
                        t = st["A"]
                        out_mm(LNQ["A", t], t, lambda k: OT[:, k, t * TR:(t + 1) * TR], Wo, 0)
                    if "B" in st:
                        transposed("A", st["B"])
                    if "A" in st:
                        scale_bias("A", st["A"], 2)
                    if "C" in st:
                        q = st["C"]
                        pe.wait_ge(s["lnT_ready"], nb + LNQ["A", 2 * q + 1] + 1)
                        if q:
                            pe.wait_ge(s["h_ready"], NP * i + q)
                        for f in range(KC):
                            for k in range(KC):
                                last = mm(ps_h[:, f, 0:2 * TR], W1[:, k, f * P:(f + 1) * P], y2T[:, k, :], k == 0, k == KC - 1)
                        last.then_inc(s["w1_ps"], 1)
                    if "D" in st:
                        t = st["D"]
                        if t % 2 == 0:
                            pe.wait_ge(s["h_ready"], NP * i + t // 2 + 1)
                        out_mm(LNQ["D", t], t, lambda k: hT[:, k, (t % 2) * TR:(t % 2 + 1) * TR], W2, 1)
                    if "E" in st:
                        transposed("D", st["E"])
                    if "D" in st:
                        scale_bias("D", st["D"], 4)

            pe.wait_ge(s["base_in"], 16 * (BS + 1))

            def transposes(T, j, wait_bank):
                w = T * JW + j
                pe.wait_ge(s["y_sb"], w + 1)
                if wait_bank is not None:
                    pe.wait_ge(s["yT_sb"], wait_bank)
                for k in range(KC):
                    last = pe.transpose(bank(2 + j % 2)[:, k * P:(k + 1) * P], Y[:, j % 2, k * P:(k + 1) * P],
                                        ident[:, :])
                last.then_inc(s["y_t"], 1)

            def entries(T, j):
                return entry(pe, T * JW + j, UNITS), entry(pe, T * JW + j, FOURTH, 1)

            def window(T, j, nu, fourth, wait_bank):
                w = T * JW + j
                st = j % NS
                bk = bank(j % 2)
                if wait_bank is not None:
                    pe.wait_ge(s["y_sb"], wait_bank)
                pe.wait_ge(s["rg_coef"], w + 1)
                pe.wait_ge(s["rg_in%d" % st], 16 * (RU - 1) * (T * (JW // NS) + j // NS + 1))
                mm(bk, CO[:, st, 0, :], G[:, st, 0, :], True, False)
                with pe.If(fourth):
                    fourths = entry(pe, w, FOURTHS_BEFORE)
                    pe.wait_ge(s["rg_4th%d" % st], 16 * fourths + 16)
                    mm(bk, CO[:, st, RU - 1, :], G[:, st, RU - 1, :], False, False)
                for c in range(1, RU - 1):
                    last = mm(bk, CO[:, st, c, :], G[:, st, c, :], False, False)
                last.then_inc(s["rg_used"], 1)
                with pe.If(nu > 1), pe.Fori(1, nu) as k_:
                    before = entry(pe, w, BEFORE)
                    set_before = entry(pe, w, SET_BEFORE)
                    pe.wait_ge(s["rg_xcoef"], before + k_ + 1)
                    pe.wait_ge(s["rg_xin%d" % st], 16 * RU * (set_before + k_))
                    for c in range(RU):
                        last = mm(bk, CO[:, st, c, :], G[:, st, c, :], False, False)
                    last.then_inc(s["rg_used"], 1)
                mm(bk, zeros[:, 0:P], zeros[:, :], False, True).then_inc(s["y_ps"], 1)

            def times_bases(T):
                pe.wait_ge(s["yT_sb"], JW * T + JW)
                pe.wait_ge(s["rel_read"], T + 1)
                for b in range(BS):
                    for k in range(KC):
                        last = mm(bank(4)[0:TR, :], YT[:, k, b, 0:TR], bases[:, b, k, :], b + k == 0,
                                  b == BS - 1 and k == KC - 1)
                last.then_inc(s["rel_ps"], 1)

            def tile(T, before):
                later = before is not None
                regs = entries(T, 0)
                if later:
                    transposes(before, JW - 2, before * JW + JW - 3)
                window(T, 0, *regs, before * JW + JW - 1 if later else None)
                regs = entries(T, 1)
                if later:
                    transposes(before, JW - 1, before * JW + JW - 2)
                    times_bases(before)
                for j in range(1, JW):
                    window(T, j, *regs, T * JW + j - 1 if later or j >= 2 else None)
                    if j < JW - 1:
                        regs = entries(T, j + 1)
                        transposes(T, j - 1, T * JW + j - 2 if later or j >= 3 else None)

            tile(0, None)
            with pe.Fori(0, NT - 1) as T:
                tile(T + 1, T)
            transposes(NT - 1, JW - 2, NT * JW - 3)
            transposes(NT - 1, JW - 1, NT * JW - 2)
            times_bases(NT - 1)

        @block.vector
        def _(dve):
            ch = Chain(dve, s["dve_pro"])
            dve.sem_inc(s["cnt_neg"], 2)
            dve.sem_inc(s["dve_cnt"], 2)
            dve.sem_inc(s["v_ready"], 1)
            dve.sem_inc(s["rel_read"], 1)
            dve.sem_inc(s["rg_xcoef"], 1)
            dve.sem_inc(s["out_done"], 16)
            nload = sum(1 + ((min(E, (h + 1) * HALF * P) - h * HALF * P) % P != 0) for h in range(2)) * 4
            dve.wait_ge(s["edge_in"], 16 * nload)
            dve.tensor_copy(erow[:, 0:3], erow_i[:, :]).then_inc(s["edge_rows"], 1)
            dve.wait_ge(s["edge_rows"], 1)
            dve.tensor_reduce(cmm[0:HALF, 0, :], erow[:, 1], AX.X, ALU.min)
            dve.tensor_reduce(cmm[0:HALF, 1, :], erow[:, 1], AX.X, ALU.max).then_inc(s["chunk_mm"], 1)
            dve.wait_ge(s["edge_cols_ps"], 1)
            dve.wait_ge(s["iotas"], 1)
            for a in range(4):
                ch(dve.tensor_copy(ed[:, a, 0:CH].rearrange("p (h c) -> p h c", h=2),
                                   ps[:, 2 * a * P:2 * (a + 1) * P].rearrange("p (h c) -> p h c", c=P)[:, :, 0:HALF]))
            dve.sem_inc(s["edge_cols"], 1)
            ch(dve.tensor_scalar(par[:, :], par[:, :], NS - 1, None, ALU.bitwise_and))
            ch(dve.tensor_copy(tri2[:, :], par[:, :]))
            ch(dve.tensor_scalar(tri2[:, :], tri2[:, :], 0.5, None, ALU.is_lt))
            dve.tensor_tensor(tri2[:, :], tri2[:, :], tri[:, :], ALU.mult).then_inc(s["tri_ready"], 1)
            dve.wait_ge(s["chunk_in"], 32)
            for k, (W, width, unit) in enumerate(((CW, TR, CU), (RW, WD, RU))):
                lo, hi = tc_[0:W, 0:1], tc_[0:W, 1:2]
                wi = tci[0:W, 15:16]
                first, last1, cnt = tc_[0:W, 2:3], tc_[0:W, 3:4], tc_[0:W, 8 + 2 * k:9 + 2 * k]
                ch(dve.tensor_copy(tc_[0:W, 4:5], wi))
                if k == 0:
                    ch(dve.tensor_scalar(lo, tc_[0:W, 4:5], float(TR), None, ALU.mult))
                else:
                    sh = JW.bit_length() - 1
                    assert 1 << sh == JW
                    ch(dve.tensor_scalar(tci[0:W, 14:15], wi, sh, None, ALU.logical_shift_right))
                    ch(dve.tensor_copy(tc_[0:W, 5:6], tci[0:W, 14:15]))
                    ch(dve.tensor_scalar(tc_[0:W, 5:6], tc_[0:W, 5:6], float(TR - WD * JW), None, ALU.mult))
                    ch(dve.scalar_tensor_tensor(lo, tc_[0:W, 4:5], float(WD), tc_[0:W, 5:6], ALU.mult, ALU.add))
                ch(dve.tensor_scalar(hi, lo, float(width - 1), None, ALU.add))
                ch(dve.tensor_scalar(tA[0:W], cmB[0:W, 1, :], lo, None, ALU.is_ge))
                ch(dve.scalar_tensor_tensor(tA[0:W], cmB[0:W, 0, :], hi, tA[0:W], ALU.is_le, ALU.mult))
                ch(dve.scalar_tensor_tensor(tB[0:W], tA[0:W], -1000.0, tI[0:W], ALU.mult, ALU.add))
                ch(dve.tensor_reduce(first, tB[0:W], AX.X, ALU.min))
                ch(dve.tensor_scalar(first, first, 1000.0, float(CH), ALU.add, ALU.min))
                ch(dve.tensor_scalar(tB[0:W], tI[0:W], 1.0, None, ALU.add))
                ch(dve.tensor_tensor(tB[0:W], tB[0:W], tA[0:W], ALU.mult))
                ch(dve.tensor_reduce(last1, tB[0:W], AX.X, ALU.max))
                ch(dve.tensor_tensor(last1, last1, first, ALU.subtract))
                ch(dve.tensor_scalar(last1, last1, 1.0, float(unit - 1), ALU.max, ALU.add))
                ch(dve.tensor_copy(tci[0:W, 14:15], last1))
                ch(dve.tensor_scalar(tci[0:W, 14:15], tci[0:W, 14:15], unit.bit_length() - 1, None, ALU.logical_shift_right))
                ch(dve.tensor_copy(cnt, tci[0:W, 14:15]))
                ch(dve.tensor_scalar(tc_[0:W, 11:12], last1, 2 * unit - 1.5, None, ALU.is_ge))
                if k == 1:
                    ch(dve.tensor_scalar(tc_[0:W, 9:10], cnt, 1.0, None, ALU.subtract))
                dve.sem_inc(s["win_count"], 1)
                dve.wait_ge(s["win_prefix"], k + 1)
                ch(dve.tensor_copy(tc_[0:W, 5:6], bank(7)[0:W, k:k + 1]))
                ch(dve.tensor_copy(tc_[0:W, 6:7], cnt))
                if k == 1:
                    dve.wait_ge(s["tab_out"], 16)
                o5 = TW * k
                dve.tensor_copy(tci[0:W, o5:o5 + 1], first)
                dve.tensor_copy(tci[0:W, o5 + 3:o5 + 4], bank(7)[0:W, 4 + k:5 + k])
                dve.tensor_copy(tci[0:W, o5 + 4:o5 + 5], tc_[0:W, 11:12])
                dve.tensor_copy(tci[0:W, o5 + 5:o5 + 6], bank(7)[0:W, 6 + k:7 + k])
                ch(dve.tensor_copy(tci[0:W, o5 + 1:o5 + 3], tc_[0:W, 5:7]))
                dve.sem_inc(s["win_tab"], 1)
            dve.wait_ge(s["cond_in"], 80)
            ch(dve.tensor_copy(fr, fri))
            ch(dve.tensor_scalar(fr, fr, 2.0 * math.pi / 16.0, None, ALU.mult))
            ch(dve.tensor_scalar(ph, nlb, fr, None, ALU.mult))
            ch(dve.tensor_scalar(nn, ph, 1.0 / (2.0 * math.pi), off1, ALU.mult, ALU.add))
            magic = 12582912.0
            ch(dve.tensor_scalar(nn, nn, magic, None, ALU.add))
            ch(dve.tensor_scalar(nn, nn, magic, None, ALU.subtract))
            c1 = 6.28125
            c2 = float(int((2 * math.pi - c1) * 2 ** 21)) / 2 ** 21
            c3 = 2 * math.pi - c1 - c2
            for c in (c1, c2, c3):
                ch(dve.scalar_tensor_tensor(ph, nn, -c, ph, ALU.mult, ALU.add))
            ch(dve.tensor_scalar(ph, ph, off2, None, ALU.add))
            ch(dve.tensor_scalar(ph, ph, -3.1415925, 3.1415925, ALU.max, ALU.min))
            ch(dve.tensor_scalar(nb1, fb1, -1.0, None, ALU.mult))
            dve.sem_inc(s["cond_emb"], 1)
            dve.wait_ge(s["cond_e"], 1)
            ch(dve.tensor_scalar(ez, ez, 1.0, None, ALU.add))
            ch(dve.reciprocal(ez, ez))
            dve.scalar_tensor_tensor(hh, ps_s[0:CD, 0:N], fb1, ez, ALU.add, ALU.mult).then_inc(s["cond_h"], 1)
            dve.wait_ge(s["cond_c"], 1)
            dve.tensor_scalar(ct[0:CD], ps_t[0:CD, 0:N], fb2, None, ALU.add).then_inc(s["ct_ready"], 1)
            dve.wait_ge(s["ct_ready"], 1)
            ch(dve.tensor_copy(csp[:, 0], ct))
            ch(dve.tensor_tensor(cr, ct, csp[:, 0], ALU.subtract))
            ch(dve.tensor_copy(csp[:, 1], cr))
            ch(dve.tensor_tensor(cr, cr, csp[:, 1], ALU.subtract))
            dve.tensor_copy(csp[:, 2], cr).then_inc(s["csp_ready"], 1)
            dve.wait_ge(s["tab_in"], 32)
            def onehots(w):
                first = dve.value_load(tabc[0:1, ds(TW * w, 1)], min_val=0, max_val=CH)
                u0 = dve.value_load(tabc[0:1, ds(TW * w + 1, 1)], min_val=0, max_val=CW * CH)
                nu = dve.value_load(tabc[0:1, ds(TW * w + 2, 1)], min_val=0, max_val=CW * CH)
                with dve.Fori(0, nu) as k_:
                    for j in range(CU):
                        c = nc.s_assert_within(first + CU * k_ + j, 0, CHP - 1)
                        dve.wait_ge(s["oh_used"], CU * u0 + CU * k_ + j + 1)
                        dve.tensor_scalar(OS[:, j, :], iota16[:, 0:N], ed[:, 0, ds(c, 1)], None, ALU.is_equal)
                        dve.tensor_scalar(OD[:, j, 0:TR], iota16[:, ds(w * TR, TR)], ed[:, 1, ds(c, 1)], None,
                                          ALU.is_equal).then_inc(s["oh_ready"], 1)

            with dve.Fori(0, CW // 2) as wp:
                for b in range(2):
                    onehots(2 * wp + b)
                for b in range(2):
                    w = 2 * wp + b
                    Lw = Lb[:, :, ds(w * TR, TR)]
                    dve.wait_ge(s["cnt_relu"], w + 3)
                    dve.tensor_scalar(Lw, counts(b), 0.5, NEG, ALU.is_lt, ALU.mult).then_inc(s["cnt_neg"], 1)
                    dve.wait_ge(s["cnt_ln"], w + 1)
                    dve.wait_ge(s["cnt_neg"], w + 3)
                    dve.scalar_tensor_tensor(Lw, lnt[:, b], 1.0 / SCALE, Lw, ALU.mult, ALU.add
                                             ).then_inc(s["dve_cnt"], 1)
                    dve.wait_ge(s["dve_cnt"], w + 3)
            ch(dve.tensor_reduce(noedge, Lb, AX.X, ALU.max))
            ch(dve.tensor_scalar(noedge, noedge, NEG / 2, None, ALU.is_lt))
            dve.sem_inc(s["bias_done"], 1)

            def layer_norm(n, r, t, c, add=None):
                x_ = xs[:, t, :]
                if add is not None:
                    dve.tensor_tensor(x_, x_, add, ALU.add).then_inc(s["x_added"], 1)
                    dve.wait_ge(s["x_added"], c)
                r4, r2 = r % 4, r % 2
                ins = dve.bn_stats(st6[:, r4, :], x_)
                ins.then_inc(s["dve_ln"], 1)
                dve.wait_ge(s["dve_ln"], 5 * n + 1)
                dve.sem_inc(s["gate"], 1)
                dve.bn_aggr(mv[:, r4, :], st6[:, r4, :]).then_inc(s["stats"], 1)
                dve.wait_ge(s["std"], n + 1)
                dve.reciprocal(rstd[:, r4:r4 + 1], sd[:, r4:r4 + 1]).then_inc(s["dve_ln"], 1)
                dve.wait_ge(s["dve_ln"], 5 * n + 2)
                dve.tensor_scalar(xnb[0:TR, r2], x_, mv[:, r4, 0:1], rstd[:, r4:r4 + 1], ALU.subtract, ALU.mult
                                  ).then_inc(s["dve_ln"], 1)
                dve.wait_ge(s["dve_ln"], 5 * n + 3)
                dve.wait_ge(s["cond_ps"], n + 1)
                dve.scalar_tensor_tensor(xnb[0:TR, r2], ps_sc[0:TR, :], 1.0, xnb[0:TR, r2], ALU.add, ALU.mult
                                         ).then_inc(s["dve_ln"], 1)
                dve.wait_ge(s["dve_ln"], 5 * n + 4)
                dve.tensor_tensor(ybuf[0:TR, r4], ps_bi[0:TR, :], xnb[0:TR, r2], ALU.add).then_inc(s["y_ready"], 1)
                dve.sem_inc(s["dve_ln"], 1)

            dve.wait_ge(s["x_in"], 16)
            for n in range(NT):
                if n >= 4:
                    dve.wait_ge(s["ln_t"], n - 3)
                layer_norm(n, n, n, None)

            with dve.Fori(0, NB) as i:
                with dve.Fori(0, NH) as h:
                    g = i * NH + h
                    for a in range(NT + 3):
                        if a < NT:
                            t = a
                            dve.wait_ge(s["qk"], NT * g + t + 1)
                            if t >= 2:
                                dve.wait_ge(s["probs_t"], NT * g + t - 1)
                            dve.sem_inc(s["gate"], 1)
                            dve.tensor_tensor_reduce(out=S[0:TR, t % 2], in0=ps_s[0:TR, 0:N], in1=Lb[:, t, :],
                                                     scale=1.0, scalar=-3.0e38, op0=ALU.add, op1=ALU.max,
                                                     accum_out=mx[:, t:t + 1]).then_inc(s["scored"], 1)
                            dve.wait_ge(s["scored"], NT * g + t + 1)
                            dve.tensor_scalar(nmx[:, t:t + 1], mx[:, t:t + 1], -SCALE, 1.0e20, ALU.mult, ALU.min
                                              ).then_inc(s["negmax"], 1)
                        if a == 0:
                            dve.wait_ge(s["vproj"], g + 1)
                            dve.tensor_tensor(V[0:TR], ps_t3[0:TR], bvB[0:TR].unsqueeze(1).broadcast_to([TR, NT, P]),
                                              ALU.add).then_inc(s["v_ready"], 1)
                        if 0 <= a - 1 < NT:
                            t = a - 1
                            dve.wait_ge(s["exped"], NT * g + t + 1)
                            dve.tensor_tensor(rrec[:, t:t + 1], den[:, t:t + 1], noedge[:, t:t + 1], ALU.add
                                              ).then_inc(s["dve_head"], 1)
                            dve.wait_ge(s["dve_head"], NT * g + t + 1)
                            dve.reciprocal(rden[:, t:t + 1], rrec[:, t:t + 1]).then_inc(s["rden_ready"], 1)
                        if a >= 4 and a % 2 == 0:
                            q = (a - 4) // 2
                            dve.wait_ge(s["pv"], NP * g + q + 1)
                            dve.wait_ge(s["r_ready"], NP * g + q + 1)
                            dve.tensor_tensor(OT[:, ds(h, 1), q * 2 * TR:(q + 1) * 2 * TR].rearrange("p o c -> p (o c)"),
                                              ps_o[:, 0, 0:2 * TR], rb[:, :], ALU.mult
                                              ).then_inc(s["ot_ready"], 1)
                nb = ln_base(i)
                for st in STEPS:
                    for kind, t in st:
                        if kind in "AD":
                            n = LNQ[kind, t]
                            dve.wait_ge(s["wo_ps"], NLN * i + n + 1)
                            dve.wait_ge(s["ln_t"], nb + n - 3)
                            layer_norm(nb + n, n + NT, t, NLN * i + n + 1, add=ps_a[n % 2][0:TR, :])

            ch2 = Chain(dve, s["dve_fin"])
            for a in range(NT + 1):
                if a < NT:
                    t = a
                    dve.wait_ge(s["in_odd" if t % 2 else "in_even"], 16 * (t // 2 + 1))
                    if t >= 2:
                        dve.wait_ge(s["x1_ready"], t - 1)
                    ch2(dve.tensor_tensor(ln0[:, t % 2], xs[:, t, :], x0t[:, t % 2], ALU.add))
                    ch2(dve.bn_stats(st6[:, t % 4, :], ln0[:, t % 2]))
                    dve.bn_aggr(mv[:, t % 4, :], st6[:, t % 4, :]).then_inc(s["fin_x"], 1)
                if a:
                    t = a - 1
                    dve.wait_ge(s["fin_std"], t + 1)
                    ch2(dve.reciprocal(rstd[:, t % 4:t % 4 + 1], sd[:, t % 4:t % 4 + 1]))
                    dve.tensor_scalar(xs[:, t, :], ln0[:, t % 2], mv[:, t % 4, 0:1], rstd[:, t % 4:t % 4 + 1],
                                      ALU.subtract, ALU.mult).then_inc(s["x1_ready"], 1)

            dve.wait_ge(s["base_in"], 16 * (BS + 1))
            dve.wait_ge(s["x1_ready"], NT)
            dve.wait_ge(s["coef_done"], CH // CG)

            def coefficients(w, lo, st, c, oh):
                ohx, cox = ("dve_rg", "rg_coef") if oh == 0 else ("dve_rgx", "rg_xcoef")
                return (dve.tensor_tensor(OH[:, oh], iota16[:, ds(lo, WD)].unsqueeze(1).broadcast_to([P, RU, WD]),
                                          ed[:, 1, ds(c, RU)].unsqueeze(2).broadcast_to([P, RU, WD]),
                                          ALU.is_equal).then_inc(s[ohx], 1),
                        lambda: dve.tensor_tensor(CO[:, st].rearrange("p j (n b) -> p j n b", b=BS),
                                                  OH[:, oh].unsqueeze(3).broadcast_to([P, RU, WD, BS]),
                                                  coef[:, ds(c, RU), :].unsqueeze(2).broadcast_to([P, RU, WD, BS]),
                                                  ALU.mult).then_inc(s[cox], 1))[1]

            def window(T, j, used):
                w = T * JW + j
                st = j % NS
                lo = T * TR + j * WD
                first = entry(dve, w, FIRST, CH)
                nu = entry(dve, w, UNITS)
                if used is not None:
                    dve.wait_ge(s["y_ps"], used)
                if not (isinstance(w, int) and w == 0):
                    dve.wait_ge(s["rg_coef"], w)
                multiply = coefficients(w, lo, st, first, 0)
                dve.wait_ge(s["dve_rg"], w + 1)
                multiply()
                with dve.If(nu > 1), dve.Fori(1, nu) as k_:
                    c = nc.s_assert_within(first + RU * k_, 0, CH)
                    before = entry(dve, w, BEFORE)
                    dve.wait_ge(s["rg_used"], before + w + k_)
                    dve.wait_ge(s["rg_xcoef"], before + k_)
                    multiply = coefficients(w, lo, st, c, 1)
                    dve.wait_ge(s["dve_rgx"], before + k_)
                    multiply()

            def finish(T):
                ch3 = Chain(dve, s["dve_rgt"], 5 * T)
                dve.wait_ge(s["rel_ps"], T + 1)
                dve.tensor_tensor(ln0[:, 0], xs[:, ds(T, 1), :].rearrange("p o d -> p (o d)"), bank(4)[0:TR, :],
                                  ALU.add).then_inc(s["rel_read"], 1)
                dve.wait_ge(s["rel_read"], T + 2)
                ch3(dve.tensor_tensor(ln0[:, 0], ln0[:, 0], hb, ALU.add))
                ch3(dve.bn_stats(st6[:, 0, :], ln0[:, 0]))
                dve.sem_inc(s["gate"], 1)
                ch3(dve.bn_aggr(mv[:, 0, :], st6[:, 0, :]))
                dve.sem_inc(s["rg_stats"], 1)
                dve.wait_ge(s["rg_std"], T + 1)
                ch3(dve.reciprocal(rstd[:, 0:1], sd[:, 0:1]))
                dve.wait_ge(s["out_done"], 16 * T + 16)
                dve.tensor_scalar(fo[:, 0], ln0[:, 0], mv[:, 0, 0:1], rstd[:, 0:1],
                                  ALU.subtract, ALU.mult).then_inc(s["out_ready"], 1)
                dve.sem_inc(s["dve_rgt"], 1)
                dve.wait_ge(s["out_ready"], T + 1)

            for j in range(JW):
                window(0, j, j - NS + 1 if j >= NS else None)
            with dve.Fori(0, NT - 1) as T:
                for j in range(JW):
                    window(T + 1, j, T * JW + JW + j - NS + 1)
                    if j == NS - 1:
                        finish(T)
            finish(NT - 1)


_INS = ["x", "src", "dst", "edge_type_32", "edge_weight1", "node_vec1",
        "L0_gnn_f_w1", "L0_gnn_f_b1", "L0_gnn_f_w2", "L0_gnn_f_b2", "L0_gnn_s1_w", "L0_gnn_s1_b", "L0_gnn_b1_w",
        "L0_gnn_b1_b", "L0_gnn_wq", "L0_gnn_bq", "L0_gnn_wk", "L0_gnn_bk", "L0_gnn_wv", "L0_gnn_bv", "L0_gnn_wo",
        "L0_gnn_bo", "L0_gnn_s2_w", "L0_gnn_s2_b", "L0_gnn_b2_w", "L0_gnn_b2_b", "L0_gnn_m_w1", "L0_gnn_m_b1",
        "L0_gnn_m_w2", "L0_gnn_m_b2", "L1_gnn_bases", "L1_gnn_w_comp", "L1_gnn_h_bias"]


def kernel(**inputs):
    import numpy as np
    import concourse.bacc as bacc
    from concourse.bass_utils import run_bass_kernel_spmd

    nc = bacc.Bacc("TRN2", target_bir_lowering=False, num_devices=1)
    arrays, aps = {}, {}
    for name in _INS:
        a = np.ascontiguousarray(inputs[name])
        arrays["in_" + name] = a
        aps[name] = nc.dram_tensor("in_" + name, a.shape, mybir.dt.from_np(a.dtype), kind="ExternalInput").ap()
    out = nc.dram_tensor("out", inputs["x"].shape, F32, kind="ExternalOutput").ap()
    graph_kernel(nc, aps, out)
    r = run_bass_kernel_spmd(nc, [arrays], core_ids=[0])
    return r.results[0]["out"]
```

```python
from contextlib import ExitStack
import math

import concourse.bass as bass
from concourse import mybir

F32 = mybir.dt.float32
BF16 = mybir.dt.bfloat16
F16 = mybir.dt.float16
I32 = mybir.dt.int32
F32R = mybir.dt.float32r
ALU = mybir.AluOpType
ACT = mybir.ActivationFunctionType
AX = mybir.AxisListType

P = 128
ds = bass.ds

COND_PART = [0, 0, 1, 0, 1, 2]
WEIGHT_PART = [0, 1, 0, 2, 1, 0]
NEG = -1.0e30
PAD_DST = 2047


class Chain:

    def __init__(self, eng, sem, base=0):
        self.eng, self.sem, self.base, self.n = eng, sem, base, 0

    def __call__(self, ins):
        ins.then_inc(self.sem, 1)
        self.n += 1
        self.eng.wait_ge(self.sem, self.base + self.n)


def graph_kernel(nc, A, out):
    N, D = A["x"].shape
    E = A["src"].shape[0]
    NB = A["L0_gnn_wq"].shape[0]
    NH = 4
    DH = D // NH
    KC = D // P
    NF = A["L0_gnn_f_w1"].shape[0] // 2
    CD = A["L0_gnn_f_w1"].shape[1]
    NT = 10
    TR = N // NT
    NP = NT // 2
    BS = A["L1_gnn_w_comp"].shape[1]
    assert TR * NT == N and TR <= P and DH == P
    SCALE = float(DH) ** -0.5
    KS = CD + 1
    KK = KS * len(COND_PART)
    HALF = -(-E // (2 * P))
    CH = 2 * HALF
    CG = 8
    CH = -(-CH // CG) * CG
    HALF = CH // 2
    CHP = CH + 4
    CW, CU = NT, 4
    WD = P // BS
    JW = -(-TR // WD)
    RW, RU = NT * JW, 4
    NS = 4
    assert JW % NS == 0 and JW > NS
    TW = 6
    CHUNKS = [(o, min(512, N - o)) for o in range(0, N, 512)]
    TB = 512 // TR
    assert TB % 2 == 0 and NT % 2 == 0
    YCHUNKS = [(b * TB, min(TB, NT - b * TB)) for b in range(-(-NT // TB))]

    x_r = A["x"].rearrange("(t p) d -> p t d", p=TR)
    out_r = out.rearrange("(t p) d -> p t d", p=TR)

    with ExitStack() as ctx:
        ctx.enter_context(nc.allow_non_contiguous_dma(reason="short columns of biases and tables"))

        def sb(name, shape, dt=F32):
            return ctx.enter_context(nc.sbuf_tensor(name, shape, dt))

        def next_place():
            return -(-nc.sbuf_base // 32) * 32

        def sem(name):
            return ctx.enter_context(nc.semaphore(name))

        x_dram = nc.dram_tensor("x_dram", (N, D), F32).ap()
        x1_dram = nc.dram_tensor("x1_dram", (N, D), F32).ap()
        chunk_dram = nc.dram_tensor("chunk_dram", (2, CH), F32).ap()
        stack_dram = nc.dram_tensor("stack_dram", (KK, 6 * NB + 2, D), BF16).ap()
        tabc_dram = nc.dram_tensor("tabc_dram", (CW, TW), I32).ap()
        tabr_dram = nc.dram_tensor("tabr_dram", (RW, TW), I32).ap()

        arena_at = next_place()
        arena = sb("arena", [P, NT * N + KC * N * 2])
        Lb = arena[0:TR, 0:NT * N].rearrange("p (t n) -> p t n", t=NT)
        OT = arena[:, NT * N + KC * N:NT * N + 2 * KC * N].rearrange("p (k n) -> p k n", k=KC)
        xs_at = next_place()
        xs_full = sb("xs", [P, NT, D])
        xs = xs_full[0:TR]
        hbuf_at = next_place()
        hbuf = sb("hbuf", [P, 2 * N + NT * P + 3 * KC * P + P + 2 * N + 2 * NT * 2 * TR])
        o = 0

        def take(n):
            nonlocal o
            o += n
            assert o <= hbuf.shape[1]
            return hbuf[:, o - n:o]
        QT, KT = take(N), take(N)
        V = take(NT * P).rearrange("p (k d) -> p k d", k=NT)
        wqkv = take(3 * KC * P).rearrange("p (m k d) -> p m k d", m=3, k=KC)
        bv = take(P)[:, 0:1]
        work = take(2 * N + 2 * NT * 2 * TR)
        S = work[:, 0:2 * N].rearrange("p (u n) -> p u n", u=2)
        PT = work[:, 2 * N:].rearrange("p (b k c) -> p b k c", b=2, k=NT)
        x0t = hbuf[0:TR, 0:4 * D].rearrange("p (s d) -> p s d", s=4)
        xsum = wqkv[0:TR].rearrange("p m k d -> p (m k d)")[:, 0:2 * D].rearrange("p (s d) -> p s d", s=2)
        w3_at = next_place()
        w3 = sb("w3", [P, 3, KC, D])
        Wo, W1, W2 = (w3[:, j] for j in range(3))
        qk_hi = nc.alloc_sbuf_tensor_at("qk_hi", [P, 2, N], F32R, offset=hbuf_at)
        qk_lo = nc.alloc_sbuf_tensor_at("qk_lo", [P, 2, N], F32R, offset=w3_at + 4 * KC * D)
        yT_hi = nc.alloc_sbuf_tensor_at("y_hi", [P, NT * N + KC * N], F32R, offset=arena_at)[:, NT * N:].rearrange(
            "p (k n) -> p k n", k=KC)
        yT_lo = nc.alloc_sbuf_tensor_at("y_lo", [P, NT, D], F32R, offset=xs_at).rearrange(
            "p (q u) d -> p q (u d)", u=2)[:, :, 0:KC * 2 * TR].rearrange("p q (k c) -> p q k c", k=KC)

        def y_lo(t):
            return yT_lo[:, t // 2, :, (t % 2) * TR:(t % 2 + 1) * TR]
        w_hi = nc.alloc_sbuf_tensor_at("w_hi", [P, 3, KC, P], F32R,
                                       offset=w3_at + 4 * (KC * D + -(-2 * N // 8) * 8))
        assert KC * D + -(-2 * N // 8) * 8 + 3 * KC * P <= 3 * KC * D
        w_lo = nc.alloc_sbuf_tensor_at("w_lo", [P, 2 * N + NT * P + 3 * KC * P], F32R, offset=hbuf_at
                                       )[:, 2 * N + NT * P:].rearrange("p (m k d) -> p m k d", m=3, k=KC)
        vT = PT[:, 1].rearrange("p k c -> p (k c)")[:, 0:N]
        bqk = sb("bqk", [P, 2])
        b1c = sb("b1c", [P, KC])
        stack = sb("stack", [P, 6, D], BF16)
        condS = sb("condS", [P, N], BF16)
        ident = sb("ident", [P, P])
        zeros = sb("zeros", [P, 512], BF16)
        iota16 = sb("iota16", [P, N + 32], F16)
        ed = sb("ed", [P, 4, CHP])
        cfi = sb("cfi", [P, CG], I32)
        cfg = sb("cfg", [P, CG, BS])
        coef = sb("coef", [P, CHP, BS])
        rb = sb("rb", [P, 2 * TR])
        small = sb("small", [P, 128])
        tabc = sb("tabc", [1, TW * CW], I32)
        tabr = sb("tabr", [1, TW * RW], I32)
        eps = small[:, 0:1]
        one, mone = small[:, 1:2], small[:, 2:3]
        mx = small[0:TR, 8:18]
        nmx = small[0:TR, 18:28]
        den = small[0:TR, 28:38]
        rden = small[0:TR, 38:48]
        rrec = small[0:TR, 48:58]
        st6 = small[0:TR, 68:92].rearrange("p (r c) -> p r c", r=4)
        mv = small[0:TR, 92:100].rearrange("p (r c) -> p r c", r=4)
        sd = small[0:TR, 100:104]
        fst6 = small[0:TR, 110:122].rearrange("p (r c) -> p r c", r=2)
        fmv = small[0:TR, 122:126].rearrange("p (r c) -> p r c", r=2)
        fsd, frstd = small[0:TR, 126:128], small[0:TR, 58:60]
        rstd = small[0:TR, 104:108]
        o -= work.shape[1]
        ybuf = take(4 * D).rearrange("p (r d) -> p r d", r=4)
        xnb = take(2 * D).rearrange("p (r d) -> p r d", r=2)
        y2T = take(KC * 2 * TR).rearrange("p (k c) -> p k c", k=KC)
        hT = take(KC * 2 * TR).rearrange("p (k c) -> p k c", k=KC)

        ps = ctx.enter_context(nc.psum_tensor("ps", [P, 8 * 512], F32))
        def bank(b, n=1):
            return ps[:, 512 * b:512 * (b + n)]
        ps_s = bank(0, 3)
        ps_t = bank(3, 3)
        ps_t3 = ps_t[:, 0:NT * P].rearrange("p (k c) -> p k c", c=P)
        ps_o = bank(6).rearrange("p (b c) -> p b c", b=2)
        ps_r = bank(7).rearrange("p (b c) -> p b c", b=2)
        assert len(YCHUNKS) == 3 and YCHUNKS[2][1] * P <= 256
        ps_vT = [bank(b)[:, 0:tn * TR] for b, (_, tn) in zip((3, 4, 6), YCHUNKS)]
        ps_v = [b[:, 0:tn * P].rearrange("p (k d) -> p k d", d=P)
                for b, (_, tn) in zip((bank(6), bank(7), bank(6)[:, 256:]), YCHUNKS)]
        ps_a = [bank(0), bank(1)]
        ps_sc, ps_bi = bank(2), bank(3)
        ps_tt = [bank(4), bank(5)]
        FIRST_LN = [(ps_sc, ps_bi), ps_a]
        ps_h = bank(6, 2).rearrange("p (f c) -> p f c", f=KC)

        erow_i = QT[0:HALF, 0:3 * 2 * P].bitcast(I32).rearrange("p (a h r) -> p a h r", a=3, h=2)
        erow = KT[0:HALF, 0:4 * 2 * P].rearrange("p (a h r) -> p a h r", a=4, h=2)
        cmm = sb("cmm", [P, 2, 2])
        cmB = V[:, 0:3, :].rearrange("p a b -> p (a b)")[:, 0:2 * CH].rearrange("p (a c) -> p a c", a=2)
        tA = V[:, 3:5, :].rearrange("p a b -> p (a b)")[:, 0:CH]
        tB = V[:, 5:7, :].rearrange("p a b -> p (a b)")[:, 0:CH]
        tI = V[:, 7:9, :].rearrange("p a b -> p (a b)")[:, 0:CH]
        w3f = w3[:, :, :, :].rearrange("p a k d -> p (a k d)")
        tri = w3f[:, 0:P]
        tc_ = sb("tc_", [P, 16])
        tci = sb("tci", [P, 16], I32)
        tri2 = w3f[:, P:2 * P]
        par = w3f[:, 2 * P:3 * P].bitcast(I32)
        oa = arena[:, NT * N + KC * N:]
        nlb = oa[0:2 * NF, 0:N]
        ph = oa[0:2 * NF, N:2 * N]
        nn = oa[0:2 * NF, 2 * N:3 * N]
        emb = oa[0:2 * NF, 3 * N:4 * N]
        ez = nn[0:CD]
        hh = ph[0:CD]
        ya = arena[:, NT * N:NT * N + KC * N]
        ct = ya[0:KS, 0:N]
        cr = ya[0:KS, N:2 * N]
        csp = ya[0:KS, 2 * N:2 * N + 3 * N // 2].bitcast(BF16).rearrange("p (a n) -> p a n", a=3)
        cw = w3f[:, 3 * P:3 * P + 64]
        fw1 = cw[0:2 * NF, 0:CD]
        fw2 = cw[0:CD, 16:16 + CD]
        fb1, nb1, fb2 = cw[0:CD, 32:33], cw[0:CD, 33:34], cw[0:CD, 34:35]
        fr = cw[0:2 * NF, 35:36]
        off1, off2 = cw[0:2 * NF, 36:37], cw[0:2 * NF, 37:38]
        fri = cw[0:2 * NF, 38:39].bitcast(I32)
        WN = 6 * D
        wf = xs_full[0:NB * KS, :, :].rearrange("p t d -> p (t d)")[:, 0:WN]
        wsp = w3f[0:NB * KS, 4 * P:4 * P + 3 * WN // 2].bitcast(BF16).rearrange("p (a n) -> p a n", a=3)
        OS = work[:, 0:CU * N // 2].bitcast(BF16).rearrange("p (b n) -> p b n", b=CU)
        OD = work[:, CU * N // 2:CU * N // 2 + CU * P // 2].bitcast(BF16).rearrange("p (b n) -> p b n", b=CU)
        lnt = work[0:TR, CU * (N + P) // 2:CU * (N + P) // 2 + 2 * N].rearrange("p (b t n) -> p b t n", b=2, t=NT)

        bases = arena[:, 0:BS * KC * D].rearrange("p (b k d) -> p b k d", b=BS, k=KC)
        YT = arena[:, BS * KC * D:BS * KC * D + KC * BS * P].rearrange("p (k b n) -> p k b n", k=KC, b=BS)
        G = hbuf[:, 0:NS * RU * D].rearrange("p (s j d) -> p s j d", s=NS, j=RU)
        o = NS * RU * D
        CO = take(NS * RU * P).rearrange("p (s j c) -> p s j c", s=NS, j=RU)
        Y = take(2 * D).rearrange("p (s d) -> p s d", s=2)
        OH = take(2 * RU * WD).rearrange("p (u j c) -> p u j c", u=2, j=RU)
        hb = w3f[0:TR, 2560:2560 + D]
        fo = w3f[0:TR, 3072:3072 + 2 * D].rearrange("p (s d) -> p s d", s=2)
        idx = sb("idx", [P, NS, RU], I32)
        ln0 = w3f[0:TR, 5120:5632]

        names = """edge_in edge_rows edge_cols_ps edge_cols chunk_mm chunk_out chunk_in iotas tri_ready
        win_count win_prefix win_tab tab_out tab_in cond_in cond_emb cond_h1 cond_e cond_h cond_c ct_ready
        csp_ready condS_in wf_in wsp_ready wstack_out cf_idx cf_in coef_done
        oh_ready oh_used cnt_done cnt_relu cnt_neg cnt_ln bias_done x_in memset_done
        wqk_in wv_in x_out0 x_out1 x_out2 x_out3 y_low w_hi w_split proj proj_ev proj_lo vproj vT_ready v_t v_ready qk scored negmax exped probs_t pt_ready pv r_ps r_ready rden_ready
        ot_ready mlpw_in stats std y_ready cond_ps ln_t lnT_ready wo_ps x_added w1_ps h_ready
        x0_in0 x0_in1 x0_in2 x0_in3 fin_x fin_std x1_ready x1_out base_in rg_idx rg_in0 rg_in1 rg_in2 rg_in3 rg_coef rg_4th0 rg_4th1 rg_4th2 rg_4th3 rg_xin0 rg_xin1 rg_xin2 rg_xin3 rg_xidx rg_xcoef rg_used y_ps y_sb y_t yT_sb rel_ps rel_read
        rg_stats rg_std out_ready out_done dve_pro dve_cnt dve_head dve_ln dve_fin dve_rg dve_rgx dve_rgt pool_pro gate"""
        s = {n: sem(n) for n in names.split()}

        block = ctx.enter_context(nc.Block())

        def mlp_steps():
            steps = []
            for a in range(NT + 6):
                st = []
                if a < NT:
                    st.append(("A", a))
                if 0 <= a - 2 < NT:
                    st.append(("B", a - 2))
                    if (a - 2) % 2:
                        st.append(("C", (a - 2) // 2))
                if 0 <= a - 4 < NT:
                    st.append(("D", a - 4))
                if 0 <= a - 6 < NT:
                    st.append(("E", a - 6))
                steps.append(st)
            return steps
        STEPS = mlp_steps()
        LNQ = {}
        for st in STEPS:
            for kind, t in st:
                if kind in "AD":
                    LNQ[kind, t] = len(LNQ)
        NLN = len(LNQ)
        KIND = {n: t if kind == "D" else "A" for (kind, t), n in LNQ.items()}
        assert NLN % 4 == 0

        def ln_base(i):
            return NT + NLN * i

        def entry(eng, w, c, hi=RW * (CH // RU + 1)):
            return eng.value_load(tabr[0:1, ds(TW * w + c, 1)], min_val=0, max_val=hi)
        FIRST, BEFORE, UNITS, SET_BEFORE, FOURTH, FOURTHS_BEFORE = range(TW)

        @block.sync
        def _(sp):
            def load(dst, src, s_, n=None):
                sp.dma_start(dst, src).then_inc(s_, 16)

            sp.wait_ge(s["memset_done"], 1)
            for a, name in enumerate(("src", "dst", "edge_type_32")):
                for h in range(2):
                    lo, hi = h * HALF * P, min(E, (h + 1) * HALF * P)
                    rows = (hi - lo) // P
                    load(erow_i[0:rows, a, h, :], A[name][lo:lo + rows * P].rearrange("(c r) -> c r", r=P), s["edge_in"])
                    rest = hi - lo - rows * P
                    if rest:
                        load(erow_i[rows:rows + 1, a, h, 0:rest],
                             A[name][hi - rest:hi].rearrange("(c r) -> c r", c=1), s["edge_in"])
            for h in range(2):
                lo, hi = h * HALF * P, min(E, (h + 1) * HALF * P)
                rows = (hi - lo) // P
                ew = A["edge_weight1"].rearrange("e o -> (e o)")
                load(erow[0:rows, 3, h, :], ew[lo:lo + rows * P].rearrange("(c r) -> c r", r=P), s["edge_in"])
                rest = hi - lo - rows * P
                if rest:
                    load(erow[rows:rows + 1, 3, h, 0:rest],
                         ew[hi - rest:hi].rearrange("(c r) -> c r", c=1), s["edge_in"])
            load(nlb, A["node_vec1"].rearrange("n o -> o n").broadcast_to([2 * NF, N]), s["cond_in"])
            load(fw1, A["L0_gnn_f_w1"], s["cond_in"])
            load(fw2, A["L0_gnn_f_w2"], s["cond_in"])
            load(fb1, A["L0_gnn_f_b1"].rearrange("(c o) -> c o", o=1), s["cond_in"])
            load(fb2, A["L0_gnn_f_b2"].rearrange("(c o) -> c o", o=1), s["cond_in"])
            sp.wait_ge(s["memset_done"], 2)
            for i in range(NB):
                for j, (w, b) in enumerate((("s1_w", "s1_b"), ("b1_w", "b1_b"), (None, "bo"), (None, "m_b2"),
                                            ("s2_w", "s2_b"), ("b2_w", "b2_b"))):
                    c = slice(j * D, (j + 1) * D)
                    if w:
                        load(wf[i * KS:i * KS + CD, c], A["L0_gnn_" + w][i], s["wf_in"])
                    load(wf[i * KS + CD:i * KS + KS, c], A["L0_gnn_" + b][i:i + 1], s["wf_in"])
            sp.wait_ge(s["chunk_mm"], 1)
            for m in range(2):
                sp.dma_start(chunk_dram[m:m + 1, :].rearrange("o (h c) -> c (o h)", h=2),
                             cmm[0:HALF, m, :]).then_inc(s["chunk_out"], 16)
            sp.wait_ge(s["chunk_out"], 32)
            for m in range(2):
                sp.dma_start(cmB[:, m, :], chunk_dram[m:m + 1, :].broadcast_to([P, CH])).then_inc(s["chunk_in"], 16)
            for k, (dr, tb, W) in enumerate(((tabc_dram, tabc, CW), (tabr_dram, tabr, RW))):
                sp.wait_ge(s["win_tab"], k + 1)
                sp.dma_start(dr, tci[0:W, TW * k:TW * k + TW]).then_inc(s["tab_out"], 16)
                sp.wait_ge(s["tab_out"], 16 * (k + 1))
                sp.dma_start(tb[0:1, :], dr.rearrange("(o w) c -> o (w c)", o=1)).then_inc(s["tab_in"], 16)
            sp.wait_ge(s["csp_ready"], 1)
            for g, a in enumerate(COND_PART):
                sp.dma_start(condS[g * KS:(g + 1) * KS, :], csp[:, a, :]).then_inc(s["condS_in"], 16)
            sp.wait_ge(s["wsp_ready"], 1)
            sp.dma_start(xs, x_r).then_inc(s["x_in"], 16)
            for t in range(NT):
                sp.dma_start(x_dram[t * TR:(t + 1) * TR, :], A["x"][t * TR:(t + 1) * TR, :]
                             ).then_inc(s["x_out%d" % (t % 4)], 16)
            for g, b in enumerate(WEIGHT_PART):
                for i in range(NB + 1):
                    k = 6 if i < NB else 2
                    ii = i % NB
                    sp.dma_start(stack_dram[g * KS:(g + 1) * KS, 6 * i:6 * i + k, :].rearrange("r k d -> r (k d)"),
                                 wsp[ii * KS:(ii + 1) * KS, b, 0:k * D]).then_inc(s["wstack_out"], 16)
            sp.wait_ge(s["wstack_out"], 16 * len(WEIGHT_PART) * (NB + 1))
            sp.dma_start(stack[0:KK, 4:6, :], stack_dram[:, 0:2, :]).then_inc(s["mlpw_in"], 16)

            def head_weights(g, i, h):
                sp.wait_ge(s["proj_lo"], 3 * g + 1)
                for m, w in enumerate("qk"):
                    sp.dma_start(wqkv[:, m, :, :],
                                 A["L0_gnn_w" + w][ds(i, 1), :, ds(h * DH, DH)].rearrange("o (k p) d -> p (o k) d", p=P)
                                 ).then_inc(s["wqk_in"], 16)
                    sp.dma_start(bqk[:, m:m + 1],
                                 A["L0_gnn_b" + w][ds(i, 1), ds(h * DH, DH)].rearrange("o d -> d o")
                                 ).then_inc(s["wqk_in"], 16)
                sp.wait_ge(s["v_ready"], 3 * g + 1)
                sp.dma_start(wqkv[:, 2, :, :],
                             A["L0_gnn_wv"][ds(i, 1), :, ds(h * DH, DH)].rearrange("o (k p) d -> p (o k) d", p=P)
                             ).then_inc(s["wv_in"], 16)
                sp.dma_start(bv, A["L0_gnn_bv"][ds(i, 1), ds(h * DH, DH)].rearrange("o d -> d o")
                             ).then_inc(s["wv_in"], 16)

            head_weights(0, 0, 0)
            with sp.Fori(0, NB) as i:
                with sp.Fori(0, NH - 1) as h:
                    head_weights(i * NH + h + 1, i, h + 1)
                sp.wait_ge(s["v_ready"], 3 * NH * (i + 1) + 1)
                sp.sem_inc(s["gate"], 1)
                for j in range(4):
                    sp.wait_ge(s["x_out%d" % j], 16 * len(range(j, NT, 4)) * (i + 1))
                    sp.sem_inc(s["gate"], 1)
                sp.dma_start(xs, x_dram.rearrange("(t p) d -> p t d", p=TR)).then_inc(s["x_in"], 16)
                sp.wait_ge(s["lnT_ready"], ln_base(i))
                for j, w in enumerate(("wo", "m_w1", "m_w2")):
                    if j == 1:
                        sp.wait_ge(s["qk"], NT * NH * i + NT * NH)
                    sp.dma_start(w3[:, j], A["L0_gnn_" + w][ds(i, 1)].rearrange("o (k p) d -> p (o k) d", p=P)
                                 ).then_inc(s["mlpw_in"], 16)
                sp.dma_start(stack[0:KK], stack_dram[:, ds(6 * i + 2, 6), :]).then_inc(s["mlpw_in"], 16)
                sp.dma_start(b1c[:, :], A["L0_gnn_m_b1"][ds(i, 1)].rearrange("o (k p) -> p (o k)", p=P)
                             ).then_inc(s["mlpw_in"], 16)
                with sp.If(i < NB - 1):
                    head_weights(i * NH + NH, nc.s_assert_within(i + 1, 0, NB - 1), 0)
                    for t in range(NT):
                        sp.wait_ge(s["x_added"], NLN * i + LNQ["D", t] + 1)
                        sp.dma_start(x_dram[t * TR:(t + 1) * TR, :], xs[:, t, :]).then_inc(s["x_out%d" % (t % 4)], 16)

            sp.wait_ge(s["ot_ready"], NP * NH * NB)
            def x0_in(t):
                sp.dma_start(x0t[:, t % 4], x_r[:, t, :]).then_inc(s["x0_in%d" % (t % 4)], 16)
            for t in range(4):
                x0_in(t)
            early = NT * N // (KC * D)
            for b in range(early):
                sp.dma_start(bases[:, b], A["L1_gnn_bases"][b].rearrange("(k p) d -> p k d", p=P)
                             ).then_inc(s["base_in"], 16)
            for t in range(NT):
                sp.wait_ge(s["x1_ready"], t + 1)
                sp.dma_start(x1_dram[t * TR:(t + 1) * TR, :], xs[:, t, :]).then_inc(s["x1_out"], 16)
                if t + 4 < NT:
                    x0_in(t + 4)
            sp.wait_ge(s["lnT_ready"], ln_base(NB))
            sp.dma_start(hb, A["L1_gnn_h_bias"].rearrange("(o d) -> o d", o=1).broadcast_to([TR, D])
                         ).then_inc(s["base_in"], 16)
            for b in range(early, BS):
                sp.dma_start(bases[:, b], A["L1_gnn_bases"][b].rearrange("(k p) d -> p k d", p=P)
                             ).then_inc(s["base_in"], 16)
            with sp.Fori(0, NT) as t:
                sp.wait_ge(s["out_ready"], t + 1)
                sp.dma_start(out_r[:, ds(t, 1), :], fo[:, 0:1, :]).then_inc(s["out_done"], 16)
            sp.wait_ge(s["out_done"], 16 * NT + 16)

        @block.gpsimd
        def _(pool):
            ch = Chain(pool, s["pool_pro"])
            ch(pool.memset(erow_i[:, 0], 0))
            ch(pool.memset(erow_i[:, 1], PAD_DST))
            ch(pool.memset(erow_i[:, 2], 0))
            ch(pool.memset(erow[:, 3], 0.0))
            pool.sem_inc(s["memset_done"], 1)
            ch(pool.memset(wf, 0.0))
            pool.sem_inc(s["memset_done"], 1)
            ch(pool.memset(ident[:, :], 0.0))
            ch(pool.memset(tri[:, :], 0.0))
            ch(pool.memset(zeros[:, :], 0.0))
            ch(pool.memset(eps, 1e-5))
            ch(pool.memset(one, 1.0))
            ch(pool.memset(mone, -1.0))
            ch(pool.memset(ct, 1.0))
            ch(pool.memset(ed[:, 0], 0.0))
            ch(pool.memset(ed[:, 1], float(PAD_DST)))
            ch(pool.memset(ed[:, 2:4], 0.0))
            ch(pool.memset(off1[0:NF], 0.0))
            ch(pool.memset(off2[0:NF], 0.0))
            ch(pool.memset(off1[NF:2 * NF], 0.25))
            ch(pool.memset(off2[NF:2 * NF], math.pi / 2))
            ch(pool.memset(coef[:, CH:CHP, :], 0.0))
            ch(pool.affine_select(out=ident[:, :], in_=ident[:, :], compare_op=ALU.not_equal, fill=1.0, base=0,
                               pattern=[[-1, P]], channel_multiplier=1))
            ch(pool.affine_select(out=tri[:, :], in_=tri[:, :], compare_op=ALU.is_ge, fill=1.0, base=0,
                               pattern=[[-1, P]], channel_multiplier=1))
            ch(pool.iota(iota16[:, :], [[1, N + 32]], base=0, channel_multiplier=0, allow_small_or_imprecise_dtypes=True))
            ch(pool.iota(tI, [[1, CH]], base=0, channel_multiplier=0, allow_small_or_imprecise_dtypes=True))
            ch(pool.iota(tci[:, 15:16], [[1, 1]], base=0, channel_multiplier=1))
            ch(pool.iota(par[:, :], [[-1, P]], base=2 * P, channel_multiplier=1))
            ch(pool.iota(fri[0:NF], [[1, 1]], base=1, channel_multiplier=1))
            ch(pool.iota(fri[NF:2 * NF], [[1, 1]], base=1, channel_multiplier=1))
            pool.sem_inc(s["iotas"], 1)

            pool.wait_ge(s["wf_in"], 16 * NB * 10)
            for a in range(3):
                ch(pool.tensor_copy(wsp[:, a], wf))
                if a < 2:
                    ch(pool.tensor_tensor(wf, wf, wsp[:, a], ALU.subtract))
            pool.sem_inc(s["wsp_ready"], 1)
            pool.wait_ge(s["ct_ready"], 1)
            for a in range(3):
                ch(pool.tensor_copy(csp[:, a], ct if a == 0 else cr))
                if a < 2:
                    ch(pool.tensor_tensor(cr, ct if a == 0 else cr, csp[:, a], ALU.subtract))
            pool.sem_inc(s["csp_ready"], 1)
            pool.wait_ge(s["edge_cols"], 1)
            with pool.Fori(0, CH // CG) as m:
                pool.tensor_copy(cfi[:, :], ed[:, 2, ds(CG * m, CG)]).then_inc(s["cf_idx"], 1)
                pool.wait_ge(s["cf_idx"], m + 1)
                pool.sem_inc(s["gate"], 1)
                for j in range(CG):
                    pool.indirect_dma_start(cfg[:, j, :], None, A["L1_gnn_w_comp"],
                                            bass.IndirectOffsetOnAxis(ap=cfi[:, j:j + 1], axis=0)
                                            ).then_inc(s["cf_in"], 16)
                pool.wait_ge(s["cf_in"], 16 * CG * (m + 1))
                pool.tensor_tensor(coef[:, ds(CG * m, CG), :], cfg[:, :, :],
                                   ed[:, 3, ds(CG * m, CG)].unsqueeze(2).broadcast_to([P, CG, BS]), ALU.mult
                                   ).then_inc(s["coef_done"], 1)
                pool.wait_ge(s["coef_done"], m + 1)

            pool.wait_ge(s["x1_out"], 16 * NT)
            pool.wait_ge(s["lnT_ready"], ln_base(NB))
            pool.wait_ge(s["tab_in"], 32)

            def gather(st, c, k):
                pool.indirect_dma_start(G[:, st, k, :], None, x1_dram,
                                        bass.IndirectOffsetOnAxis(ap=idx[:, st, k:k + 1], axis=0)
                                        ).then_inc(s[c + str(st)], 16)

            def window(w, st, used):
                first = entry(pool, w, FIRST, CH)
                nu = entry(pool, w, UNITS)
                fourth = entry(pool, w, FOURTH, 1)
                if used is not None:
                    pool.wait_ge(s["y_ps"], used)
                pool.tensor_copy(idx[:, st, :], ed[:, 0, ds(first, RU)]).then_inc(s["rg_idx"], 1)
                pool.wait_ge(s["rg_idx"], w + 1)
                pool.sem_inc(s["gate"], 1)
                for j in range(RU - 1):
                    gather(st, "rg_in", j)
                with pool.If(fourth):
                    gather(st, "rg_4th", RU - 1)
                with pool.If(nu > 1), pool.Fori(1, nu) as k_:
                    c = nc.s_assert_within(first + RU * k_, 0, CH)
                    before = entry(pool, w, BEFORE)
                    pool.wait_ge(s["rg_used"], before + w + k_)
                    pool.tensor_copy(idx[:, st, :], ed[:, 0, ds(c, RU)]).then_inc(s["rg_xidx"], 1)
                    pool.wait_ge(s["rg_xidx"], before + k_)
                    pool.sem_inc(s["gate"], 1)
                    for j in range(RU):
                        gather(st, "rg_xin", j)

            for st in range(NS):
                window(st, st, None)
            with pool.Fori(0, RW // NS - 1) as wq:
                for st in range(NS):
                    window(NS * wq + NS + st, st, NS * wq + st + 1)

        def counts(b):
            return bank(3 * b, 3)[0:TR, 0:NT * P].rearrange("p (t c) -> p t c", c=P)[:, :, 0:TR]

        def kq_pieces(n):
            m, src, banks = ((1, ps_s, range(len(YCHUNKS))), (0, ps_t, range(1)), (0, ps_t, range(1, len(YCHUNKS))))[n]
            for b in banks:
                t0, tn = YCHUNKS[b]
                yield m, src[:, 512 * b:512 * b + tn * TR], slice(t0 * TR, (t0 + tn) * TR)

        def act_lnT(act, n, bk, dst):
            act.wait_ge(s["ln_t"], n + 1)
            act.activation(dst, ps_tt[bk][:, 0:KC * P].rearrange("p (k c) -> p k c", k=KC)[:, :, 0:TR],
                           ACT.Copy).then_inc(s["lnT_ready"], 1)

        @block.scalar
        def _(act):
            act.sem_inc(s["proj_ev"], 1)
            act.wait_ge(s["cond_emb"], 1)
            act.activation(emb, ph, ACT.Sin).then_inc(s["cond_emb"], 1)
            act.wait_ge(s["cond_h1"], 1)
            act.activation(ez, ps_s[0:CD, 0:N], ACT.Exp, bias=nb1, scale=-1.0).then_inc(s["cond_e"], 1)
            act.sem_inc(s["cnt_relu"], 2)
            with act.Fori(0, CW // 2) as wp:
                for b in range(2):
                    w = 2 * wp + b
                    act.wait_ge(s["cnt_done"], w + 1)
                    act.wait_ge(s["dve_cnt"], w + 1)
                    act.activation(lnt[:, b], counts(b), ACT.Relu, bias=mone[0:TR]).then_inc(s["cnt_relu"], 1)
                    act.wait_ge(s["cnt_relu"], w + 3)
                    act.activation(lnt[:, b], lnt[:, b], ACT.Ln, bias=one[0:TR]).then_inc(s["cnt_ln"], 1)
            for n in range(NT):
                act.wait_ge(s["stats"], n + 1)
                act.activation(sd[:, n % 4:n % 4 + 1], mv[:, n % 4, 1:2], ACT.Sqrt, bias=eps[0:TR]).then_inc(s["std"], 1)
                act_lnT(act, n, n % 2, yT_hi[:, :, n * TR:(n + 1) * TR])

            with act.Fori(0, NB) as i:
                def kq_evac(g):
                    act.wait_ge(s["wqk_in"], 64 * g + 64)
                    for n in range(3):
                        act.wait_ge(s["proj"], 3 * g + n + 1)
                        for m, src, c in kq_pieces(n):
                            last = act.activation(qk_hi[:, m, c], src, ACT.Identity, bias=bqk[:, m:m + 1])
                        last.then_inc(s["proj_ev"], 1)

                def vT_evac(g, b):
                    t0, tn = YCHUNKS[b]
                    act.wait_ge(s["vproj"], 3 * g + b + 1)
                    act.activation(vT[:, t0 * TR:(t0 + tn) * TR], ps_vT[b], ACT.Identity, bias=bv
                                   ).then_inc(s["vT_ready"], 1)

                def head(g, last):
                    for a in range(NT + 1):
                        if a < NT:
                            t = a
                            act.wait_ge(s["negmax"], NT * g + t + 1)
                            act.activation(S[0:TR, t % 2], S[0:TR, t % 2], ACT.Exp, bias=nmx[:, t:t + 1], scale=SCALE,
                                           accum_out=den[:, t:t + 1]).then_inc(s["exped"], 1)
                        if a == 0:
                            act.wait_ge(s["wv_in"], 32 * g + 32)
                            vT_evac(g, 0)
                            vT_evac(g, 1)
                        if a:
                            t = a - 1
                            q, u = divmod(t, 2)
                            act.wait_ge(s["probs_t"], NT * g + t + 1)
                            if u == 0 and q >= 2:
                                act.wait_ge(s["pv"], NP * g + q - 1)
                            act.activation(PT[0:TR, q % 2, :, u * TR:(u + 1) * TR], ps_t3[0:TR, :, 0:TR], ACT.Copy
                                           ).then_inc(s["pt_ready"], 1)
                            if a == 1:
                                vT_evac(g, 2)
                            if u == 1:
                                act.wait_ge(s["r_ps"], NT * g + t + 1)
                                if q >= 1:
                                    act.wait_ge(s["ot_ready"], NP * g + q)
                                act.activation(rb[:, :], ps_r[:, 0, 0:2 * TR], ACT.Copy).then_inc(s["r_ready"], 1)
                    if not last:
                        kq_evac(g + 1)
                kq_evac(i * NH)
                with act.Fori(0, NH - 1) as h:
                    head(i * NH + h, False)
                head(i * NH + NH - 1, True)
                nb = ln_base(i)

                def std(n):
                    act.wait_ge(s["stats"], nb + n + 1)
                    act.activation(sd[:, (n + NT) % 4:(n + NT) % 4 + 1], mv[:, (n + NT) % 4, 1:2], ACT.Sqrt,
                                   bias=eps[0:TR]).then_inc(s["std"], 1)
                act.wait_ge(s["mlpw_in"], 80 * i + 96)
                for st in STEPS:
                    st = dict(st)
                    if "B" in st:
                        t = st["B"]
                        n = LNQ["A", t]
                        if t % 2 == 0 and t >= 2:
                            act.wait_ge(s["w1_ps"], NP * i + t // 2)
                        act_lnT(act, nb + n, (n + NT) % 2, y2T[:, :, (t % 2) * TR:(t % 2 + 1) * TR])
                    if "A" in st:
                        std(LNQ["A", st["A"]])
                    if "C" in st:
                        q = st["C"]
                        act.wait_ge(s["w1_ps"], NP * i + q + 1)
                        if q >= 1:
                            act.wait_ge(s["wo_ps"], NLN * i + LNQ["D", 2 * q - 1] + 1)
                        for f in range(KC):
                            last = act.activation(hT[:, f, :], ps_h[:, f, 0:2 * TR], ACT.Relu, bias=b1c[:, f:f + 1])
                        last.then_inc(s["h_ready"], 1)
                    if "D" in st:
                        t = st["D"]
                        n = LNQ["D", t]
                        with act.If(i < NB - 1):
                            std(n)
                        with act.If(i > NB - 2):
                            act.wait_ge(s["std"], nb + n)
                            act.sem_inc(s["std"], 1)
                            act.wait_ge(s["fin_x"], t + 1)
                            act.activation(fsd[:, t % 2:t % 2 + 1], fmv[:, t % 2, 1:2], ACT.Sqrt, bias=eps[0:TR]
                                           ).then_inc(s["fin_std"], 1)
                    if "E" in st:
                        t = st["E"]
                        n = LNQ["D", t]
                        with act.If(i < NB - 1):
                            act_lnT(act, nb + n, (n + NT) % 2, yT_hi[:, :, t * TR:(t + 1) * TR])
                        with act.If(i > NB - 2):
                            act.wait_ge(s["lnT_ready"], nb + n)
                            act.sem_inc(s["lnT_ready"], 1)

            def y_evac(T, j):
                act.wait_ge(s["y_ps"], T * JW + j + 1)
                act.activation(Y[:, j % 2], bank(j % 2), ACT.Copy).then_inc(s["y_sb"], 1)

            def yT_copy(T, j):
                act.wait_ge(s["y_t"], T * JW + j + 1)
                src = bank(2 + j % 2).rearrange("p (k n b) -> p k b n", k=KC, b=BS)
                for k in range(KC):
                    last = act.activation(YT[:, k, :, j * WD:(j + 1) * WD], src[:, k], ACT.Copy)
                last.then_inc(s["yT_sb"], 1)

            def rel_std(T):
                act.wait_ge(s["rg_stats"], T + 1)
                act.activation(sd[:, 0:1], mv[:, 0, 1:2], ACT.Sqrt, bias=eps[0:TR]).then_inc(s["rg_std"], 1)

            def tile(T, before):
                y_evac(T, 0)
                if before is not None:
                    yT_copy(before, JW - 1)
                for j in range(1, JW):
                    y_evac(T, j)
                    if j == 1 and before is not None:
                        act.wait_ge(s["rel_ps"], before + 1)
                    yT_copy(T, j - 1)
                    if j == 2 and before is not None:
                        rel_std(before)

            tile(0, None)
            with act.Fori(0, NT - 1) as T:
                tile(T + 1, T)
            yT_copy(NT - 1, JW - 1)
            rel_std(NT - 1)

        @block.tensor
        def _(pe):
            def mm(o_, l_, r_, start=True, stop=True):
                return pe.matmul(o_, l_, r_, start=start, stop=stop)

            pe.sem_inc(s["oh_used"], CU)
            pe.wait_ge(s["iotas"], 1)
            pe.wait_ge(s["edge_rows"], 1)
            for a in range(4):
                for h in range(2):
                    c = (2 * a + h) * P
                    last = pe.transpose(ps[:, c:c + HALF], erow[:, a, h, :], ident[0:HALF, 0:HALF])
            last.then_inc(s["edge_cols_ps"], 1)
            pe.wait_ge(s["cond_in"], 80)
            pe.wait_ge(s["cond_emb"], 2)
            pe.wait_ge(s["edge_cols"], 1)
            for c0, cn in CHUNKS:
                last = mm(ps_s[0:CD, c0:c0 + cn], fw1, emb[:, c0:c0 + cn])
            last.then_inc(s["cond_h1"], 1)
            for k, W in enumerate((CW, RW)):
                pe.wait_ge(s["win_count"], k + 1)
                pe.wait_ge(s["tri_ready"], 1)
                mm(bank(7)[0:W, 4 + k:5 + k], tri2[0:W, 0:W], tc_[0:W, 8 + k:9 + k])
                mm(bank(7)[0:W, 6 + k:7 + k], tri2[0:W, 0:W], tc_[0:W, 11:12])
                mm(bank(7)[0:W, k:k + 1], tri[0:W, 0:W], tc_[0:W, 8 + k:9 + k]).then_inc(s["win_prefix"], 1)
            pe.wait_ge(s["cond_h"], 1)
            for c0, cn in CHUNKS:
                last = mm(ps_t[0:CD, c0:c0 + cn], fw2, hh[:, c0:c0 + cn])
            last.then_inc(s["cond_c"], 1)
            pe.wait_ge(s["tab_in"], 32)
            pe.wait_ge(s["ct_ready"], 1)
            with pe.Fori(0, CW // 2) as wp:
                for b2 in range(2):
                    w = 2 * wp + b2
                    u0 = pe.value_load(tabc[0:1, ds(TW * w + 1, 1)], min_val=0, max_val=CW * CH)
                    nu = pe.value_load(tabc[0:1, ds(TW * w + 2, 1)], min_val=0, max_val=CW * CH)
                    pe.wait_ge(s["cnt_relu"], w + 1)
                    pe.wait_ge(s["cnt_neg"], w + 1)
                    for b in range(3):
                        mm(bank(3 * b2 + b)[0:TR], zeros[:, 0:TR], zeros[:, :], True, False)
                    with pe.Fori(0, nu) as k_:
                        for j in range(CU):
                            pe.wait_ge(s["oh_ready"], CU * u0 + CU * k_ + j + 1)
                            for t in range(NT):
                                last = mm(bank(3 * b2, 3)[0:TR, t * P:t * P + TR], OS[:, j, t * TR:(t + 1) * TR],
                                          OD[:, j, 0:TR], False, False)
                            last.then_inc(s["oh_used"], 1)
                    for b in range(3):
                        last = mm(bank(3 * b2 + b)[0:TR], zeros[:, 0:TR], zeros[:, :], False, True)
                    last.then_inc(s["cnt_done"], 1)

            pe.wait_ge(s["bias_done"], 1)

            def cond_mm(n, t, j, banks=(ps_sc, ps_bi)):
                for b, dst in enumerate(banks):
                    last = mm(dst[0:TR, :], condS[0:KK, t * TR:(t + 1) * TR], stack[0:KK, j + b, :])
                last.then_inc(s["cond_ps"], 1)

            def y_transpose(n, slot, bk):
                pe.wait_ge(s["y_ready"], n + 1)
                for k in range(KC):
                    last = pe.transpose(ps_tt[bk][:, k * P:k * P + TR], ybuf[0:TR, slot, k * P:(k + 1) * P],
                                        ident[0:TR, 0:TR])
                last.then_inc(s["ln_t"], 1)

            pe.wait_ge(s["condS_in"], 16 * len(COND_PART))
            pe.wait_ge(s["mlpw_in"], 16)
            def first_transposed(n):
                if n >= 2:
                    pe.wait_ge(s["y_low"], n - 1)
                y_transpose(n, n % 4, n % 2)

            for n in range(NT):
                if n >= 2:
                    pe.wait_ge(s["y_ready"], n - 1)
                cond_mm(n, n, 4, FIRST_LN[n % 2])
                if n:
                    first_transposed(n - 1)
            first_transposed(NT - 1)

            with pe.Fori(0, NB) as i:
                def project(o_, m, b):
                    t0, tn = YCHUNKS[b]
                    for k in range(KC):
                        hi = yT_hi[:, k, t0 * TR:(t0 + tn) * TR]
                        lo = yT_lo[:, t0 // 2:(t0 + tn) // 2, k, :]
                        mm(o_, w_hi[:, m, k, :], hi, k == 0, False)
                        mm(o_, w_hi[:, m, k, :], lo, False, False)
                        last = mm(o_, w_lo[:, m, k, :], hi, False, k == KC - 1)
                    return last

                def kq_proj(g, n):
                    m, dst = ((1, ps_s), (0, ps_t))[n]
                    if n == 0:
                        pe.wait_ge(s["w_split"], 2 * g + 1)
                    for b in range(len(YCHUNKS)):
                        last = project(dst[:, 512 * b:512 * b + YCHUNKS[b][1] * TR], m, b)
                        if n == 1 and b == 0:
                            last.then_inc(s["proj"], 1)
                    last.then_inc(s["proj"], 1)

                def v_transposes(g, b):
                    pe.wait_ge(s["vT_ready"], 3 * g + b + 1)
                    t0, tn = YCHUNKS[b]
                    for t in range(tn):
                        last = pe.transpose(ps_v[b][0:TR, t, :], vT[:, (t0 + t) * TR:(t0 + t + 1) * TR], ident[:, :])
                    last.then_inc(s["v_t"], 1)

                def head(g, last_head):
                    pe.wait_ge(s["proj_lo"], 3 * g + 3)
                    for a in range(NT + 3):
                        if a < NT:
                            t = a
                            if t:
                                pe.wait_ge(s["scored"], NT * g + t)
                            for p, (q_, k_) in enumerate(((qk_hi, qk_lo), (qk_hi, qk_hi), (qk_lo, qk_hi))):
                                for c0, cn in CHUNKS:
                                    last = mm(ps_s[0:TR, c0:c0 + cn], q_[:, 0, t * TR:(t + 1) * TR], k_[:, 1, c0:c0 + cn],
                                              p == 0, p == 2)
                            last.then_inc(s["qk"], 1)
                        if 0 <= a - 2 < NT:
                            t = a - 2
                            q, u = divmod(t, 2)
                            pe.wait_ge(s["rden_ready"], NT * g + t + 1)
                            if u == 0 and q >= 1:
                                pe.wait_ge(s["r_ready"], NP * g + q)
                            pe.transpose(ps_r[:, 0, u * TR:(u + 1) * TR], rden[:, t:t + 1].broadcast_to([TR, P]),
                                         ident[0:TR, 0:TR]).then_inc(s["r_ps"], 1)
                        if a == 0:
                            pe.wait_ge(s["w_split"], 2 * g + 2)
                            pe.wait_ge(s["proj_lo"], 3 * g + 4)
                            project(ps_vT[0], 2, 0).then_inc(s["vproj"], 1)
                            project(ps_vT[1], 2, 1).then_inc(s["vproj"], 1)
                            v_transposes(g, 0)
                            v_transposes(g, 1)
                        if a == 2:
                            v_transposes(g, 2)
                        if 0 <= a - 3 < NT:
                            q, half = divmod(a - 3, 2)
                            if a == 3:
                                pe.wait_ge(s["v_ready"], 3 * g + 4)
                            if half == 0:
                                pe.wait_ge(s["pt_ready"], NT * g + 2 * q + 2)
                                if q >= 1:
                                    pe.wait_ge(s["ot_ready"], NP * g + q)
                            for k in range(half * NP, (half + 1) * NP):
                                last = mm(ps_o[:, 0, 0:2 * TR], V[0:TR, k, :], PT[0:TR, q % 2, k, :],
                                          k == 0, k == NT - 1)
                            if half:
                                last.then_inc(s["pv"], 1)
                        if 0 <= a - 1 < NT:
                            t = a - 1
                            q, u = divmod(t, 2)
                            pe.wait_ge(s["exped"], NT * g + t + 1)
                            if t:
                                pe.wait_ge(s["pt_ready"], NT * g + t)
                            for k in range(NT):
                                last = pe.transpose(ps_t3[0:TR, k, 0:TR], S[0:TR, t % 2, k * TR:(k + 1) * TR],
                                                    ident[0:TR, 0:TR])
                            last.then_inc(s["probs_t"], 1)
                        if a == 1:
                            pe.wait_ge(s["v_ready"], 3 * g + 2)
                            project(ps_vT[2], 2, 2).then_inc(s["vproj"], 1)
                        if not last_head and a == NT:
                            kq_proj(g + 1, 0)
                        if not last_head and a == NT + 1:
                            pe.wait_ge(s["pt_ready"], NT * g + NT)
                            kq_proj(g + 1, 1)
                pe.wait_ge(s["y_low"], NT * (i + 1))
                for n in range(2):
                    kq_proj(i * NH, n)
                with pe.Fori(0, NH - 1) as h:
                    head(i * NH + h, False)
                head(i * NH + NH - 1, True)
                nb = ln_base(i)
                pe.wait_ge(s["mlpw_in"], 80 * i + 96)
                pe.wait_ge(s["ot_ready"], NP * NH * i + NP * NH)

                def out_mm(n, t, lhs, w, j):
                    if n >= 2:
                        pe.wait_ge(s["x_added"], NLN * i + n - 1)
                    dst = ps_a[n % 2][0:TR, :]
                    mm(dst, condS[0:KK, t * TR:(t + 1) * TR], stack[0:KK, j, :], True, False)
                    for k in range(KC):
                        last = mm(dst, lhs(k), w[:, k, :], False, k == KC - 1)
                    last.then_inc(s["wo_ps"], 1)

                def scale_bias(kind, t, j):
                    n = LNQ[kind, t]
                    pe.wait_ge(s["y_ready"], nb + n)
                    cond_mm(nb + n, t, j)

                def transposed(kind, t):
                    n = LNQ[kind, t]
                    pe.wait_ge(s["lnT_ready"], nb + n - 1)
                    if KIND.get(n - 2, "A") in range(NT):
                        pe.wait_ge(s["y_low"], NT * (i + 1) + KIND[n - 2] + 1)
                    y_transpose(nb + n, (n + NT) % 4, (n + NT) % 2)

                for st in STEPS:
                    st = dict(st)
                    if "A" in st:
                        t = st["A"]
                        out_mm(LNQ["A", t], t, lambda k: OT[:, k, t * TR:(t + 1) * TR], Wo, 0)
                    if "B" in st:
                        transposed("A", st["B"])
                    if "A" in st:
                        scale_bias("A", st["A"], 2)
                    if "C" in st:
                        q = st["C"]
                        pe.wait_ge(s["lnT_ready"], nb + LNQ["A", 2 * q + 1] + 1)
                        if q:
                            pe.wait_ge(s["h_ready"], NP * i + q)
                        for f in range(KC):
                            for k in range(KC):
                                last = mm(ps_h[:, f, 0:2 * TR], W1[:, k, f * P:(f + 1) * P], y2T[:, k, :], k == 0, k == KC - 1)
                        last.then_inc(s["w1_ps"], 1)
                    if "D" in st:
                        t = st["D"]
                        if t % 2 == 0:
                            pe.wait_ge(s["h_ready"], NP * i + t // 2 + 1)
                        out_mm(LNQ["D", t], t, lambda k: hT[:, k, (t % 2) * TR:(t % 2 + 1) * TR], W2, 1)
                    with pe.If(i < NB - 1):
                        if "E" in st:
                            transposed("D", st["E"])
                        if "D" in st:
                            scale_bias("D", st["D"], 4)
                    with pe.If(i > NB - 2):
                        for kind, name in (("E", "ln_t"), ("D", "cond_ps")):
                            if kind in st:
                                pe.wait_ge(s[name], nb + LNQ["D", st[kind]])
                                pe.sem_inc(s[name], 1)

            pe.wait_ge(s["base_in"], 16 * (BS + 1))

            def transposes(T, j, wait_bank):
                w = T * JW + j
                pe.wait_ge(s["y_sb"], w + 1)
                if wait_bank is not None:
                    pe.wait_ge(s["yT_sb"], wait_bank)
                for k in range(KC):
                    last = pe.transpose(bank(2 + j % 2)[:, k * P:(k + 1) * P], Y[:, j % 2, k * P:(k + 1) * P],
                                        ident[:, :])
                last.then_inc(s["y_t"], 1)

            def entries(T, j):
                return entry(pe, T * JW + j, UNITS), entry(pe, T * JW + j, FOURTH, 1)

            def window(T, j, nu, fourth, wait_bank):
                w = T * JW + j
                st = j % NS
                bk = bank(j % 2)
                if wait_bank is not None:
                    pe.wait_ge(s["y_sb"], wait_bank)
                pe.wait_ge(s["rg_coef"], w + 1)
                pe.wait_ge(s["rg_in%d" % st], 16 * (RU - 1) * (T * (JW // NS) + j // NS + 1))
                mm(bk, CO[:, st, 0, :], G[:, st, 0, :], True, False)
                with pe.If(fourth):
                    fourths = entry(pe, w, FOURTHS_BEFORE)
                    pe.wait_ge(s["rg_4th%d" % st], 16 * fourths + 16)
                    mm(bk, CO[:, st, RU - 1, :], G[:, st, RU - 1, :], False, False)
                for c in range(1, RU - 1):
                    last = mm(bk, CO[:, st, c, :], G[:, st, c, :], False, False)
                last.then_inc(s["rg_used"], 1)
                with pe.If(nu > 1), pe.Fori(1, nu) as k_:
                    before = entry(pe, w, BEFORE)
                    set_before = entry(pe, w, SET_BEFORE)
                    pe.wait_ge(s["rg_xcoef"], before + k_ + 1)
                    pe.wait_ge(s["rg_xin%d" % st], 16 * RU * (set_before + k_))
                    for c in range(RU):
                        last = mm(bk, CO[:, st, c, :], G[:, st, c, :], False, False)
                    last.then_inc(s["rg_used"], 1)
                mm(bk[:, 0:16], zeros[:, 0:P], zeros[:, 0:16], False, True).then_inc(s["y_ps"], 1)

            def times_bases(T):
                pe.wait_ge(s["yT_sb"], JW * T + JW)
                pe.wait_ge(s["rel_read"], T + 1)
                for b in range(BS):
                    for k in range(KC):
                        last = mm(bank(4)[0:TR, :], YT[:, k, b, 0:TR], bases[:, b, k, :], b + k == 0,
                                  b == BS - 1 and k == KC - 1)
                last.then_inc(s["rel_ps"], 1)

            def tile(T, before):
                later = before is not None
                regs = entries(T, 0)
                if later:
                    transposes(before, JW - 2, before * JW + JW - 3)
                window(T, 0, *regs, before * JW + JW - 1 if later else None)
                regs = entries(T, 1)
                if later:
                    transposes(before, JW - 1, before * JW + JW - 2)
                    times_bases(before)
                for j in range(1, JW):
                    window(T, j, *regs, T * JW + j - 1 if later or j >= 2 else None)
                    if j < JW - 1:
                        regs = entries(T, j + 1)
                        transposes(T, j - 1, T * JW + j - 2 if later or j >= 3 else None)

            tile(0, None)
            with pe.Fori(0, NT - 1) as T:
                tile(T + 1, T)
            transposes(NT - 1, JW - 2, NT * JW - 3)
            transposes(NT - 1, JW - 1, NT * JW - 2)
            times_bases(NT - 1)

        @block.vector
        def _(dve):
            ch = Chain(dve, s["dve_pro"])
            dve.sem_inc(s["cnt_neg"], 2)
            dve.sem_inc(s["dve_cnt"], 2)
            dve.sem_inc(s["v_ready"], 1)
            dve.sem_inc(s["proj_lo"], 1)
            dve.sem_inc(s["rel_read"], 1)
            dve.sem_inc(s["rg_xcoef"], 1)
            dve.sem_inc(s["out_done"], 16)
            nload = sum(1 + ((min(E, (h + 1) * HALF * P) - h * HALF * P) % P != 0) for h in range(2)) * 4
            dve.wait_ge(s["edge_in"], 16 * nload)
            dve.tensor_copy(erow[:, 0:3], erow_i[:, :]).then_inc(s["edge_rows"], 1)
            dve.wait_ge(s["edge_rows"], 1)
            dve.tensor_reduce(cmm[0:HALF, 0, :], erow[:, 1], AX.X, ALU.min)
            dve.tensor_reduce(cmm[0:HALF, 1, :], erow[:, 1], AX.X, ALU.max).then_inc(s["chunk_mm"], 1)
            dve.wait_ge(s["edge_cols_ps"], 1)
            dve.wait_ge(s["iotas"], 1)
            for a in range(4):
                ch(dve.tensor_copy(ed[:, a, 0:CH].rearrange("p (h c) -> p h c", h=2),
                                   ps[:, 2 * a * P:2 * (a + 1) * P].rearrange("p (h c) -> p h c", c=P)[:, :, 0:HALF]))
            dve.sem_inc(s["edge_cols"], 1)
            ch(dve.tensor_scalar(par[:, :], par[:, :], NS - 1, None, ALU.bitwise_and))
            ch(dve.tensor_copy(tri2[:, :], par[:, :]))
            ch(dve.tensor_scalar(tri2[:, :], tri2[:, :], 0.5, None, ALU.is_lt))
            dve.tensor_tensor(tri2[:, :], tri2[:, :], tri[:, :], ALU.mult).then_inc(s["tri_ready"], 1)
            dve.wait_ge(s["cond_in"], 80)
            ch(dve.tensor_copy(fr, fri))
            ch(dve.tensor_scalar(fr, fr, 2.0 * math.pi / 16.0, None, ALU.mult))
            ch(dve.tensor_scalar(ph, nlb, fr, None, ALU.mult))
            ch(dve.tensor_scalar(nn, ph, 1.0 / (2.0 * math.pi), off1, ALU.mult, ALU.add))
            magic = 12582912.0
            ch(dve.tensor_scalar(nn, nn, magic, None, ALU.add))
            ch(dve.tensor_scalar(nn, nn, magic, None, ALU.subtract))
            c1 = 6.28125
            c2 = float(int((2 * math.pi - c1) * 2 ** 21)) / 2 ** 21
            c3 = 2 * math.pi - c1 - c2
            for c in (c1, c2, c3):
                ch(dve.scalar_tensor_tensor(ph, nn, -c, ph, ALU.mult, ALU.add))
            ch(dve.tensor_scalar(ph, ph, off2, None, ALU.add))
            ch(dve.tensor_scalar(ph, ph, -3.1415925, 3.1415925, ALU.max, ALU.min))
            ch(dve.tensor_scalar(nb1, fb1, -1.0, None, ALU.mult))
            dve.sem_inc(s["cond_emb"], 1)
            dve.wait_ge(s["chunk_in"], 32)
            for k, (W, width, unit) in enumerate(((CW, TR, CU), (RW, WD, RU))):
                lo, hi = tc_[0:W, 0:1], tc_[0:W, 1:2]
                wi = tci[0:W, 15:16]
                first, last1, cnt = tc_[0:W, 2:3], tc_[0:W, 3:4], tc_[0:W, 8 + 2 * k:9 + 2 * k]
                ch(dve.tensor_copy(tc_[0:W, 4:5], wi))
                if k == 0:
                    ch(dve.tensor_scalar(lo, tc_[0:W, 4:5], float(TR), None, ALU.mult))
                else:
                    sh = JW.bit_length() - 1
                    assert 1 << sh == JW
                    ch(dve.tensor_scalar(tci[0:W, 14:15], wi, sh, None, ALU.logical_shift_right))
                    ch(dve.tensor_copy(tc_[0:W, 5:6], tci[0:W, 14:15]))
                    ch(dve.tensor_scalar(tc_[0:W, 5:6], tc_[0:W, 5:6], float(TR - WD * JW), None, ALU.mult))
                    ch(dve.scalar_tensor_tensor(lo, tc_[0:W, 4:5], float(WD), tc_[0:W, 5:6], ALU.mult, ALU.add))
                ch(dve.tensor_scalar(hi, lo, float(width - 1), None, ALU.add))
                ch(dve.tensor_scalar(tA[0:W], cmB[0:W, 1, :], lo, None, ALU.is_ge))
                ch(dve.scalar_tensor_tensor(tA[0:W], cmB[0:W, 0, :], hi, tA[0:W], ALU.is_le, ALU.mult))
                ch(dve.scalar_tensor_tensor(tB[0:W], tA[0:W], -1000.0, tI[0:W], ALU.mult, ALU.add))
                ch(dve.tensor_reduce(first, tB[0:W], AX.X, ALU.min))
                ch(dve.tensor_scalar(first, first, 1000.0, float(CH), ALU.add, ALU.min))
                ch(dve.tensor_scalar(tB[0:W], tI[0:W], 1.0, None, ALU.add))
                ch(dve.tensor_tensor(tB[0:W], tB[0:W], tA[0:W], ALU.mult))
                ch(dve.tensor_reduce(last1, tB[0:W], AX.X, ALU.max))
                ch(dve.tensor_tensor(last1, last1, first, ALU.subtract))
                ch(dve.tensor_scalar(last1, last1, 1.0, float(unit - 1), ALU.max, ALU.add))
                ch(dve.tensor_copy(tci[0:W, 14:15], last1))
                ch(dve.tensor_scalar(tci[0:W, 14:15], tci[0:W, 14:15], unit.bit_length() - 1, None, ALU.logical_shift_right))
                ch(dve.tensor_copy(cnt, tci[0:W, 14:15]))
                ch(dve.tensor_scalar(tc_[0:W, 11:12], last1, 2 * unit - 1.5, None, ALU.is_ge))
                if k == 1:
                    ch(dve.tensor_scalar(tc_[0:W, 9:10], cnt, 1.0, None, ALU.subtract))
                dve.sem_inc(s["win_count"], 1)
                dve.wait_ge(s["win_prefix"], k + 1)
                ch(dve.tensor_copy(tc_[0:W, 5:6], bank(7)[0:W, k:k + 1]))
                ch(dve.tensor_copy(tc_[0:W, 6:7], cnt))
                if k == 1:
                    dve.wait_ge(s["tab_out"], 16)
                o5 = TW * k
                dve.tensor_copy(tci[0:W, o5:o5 + 1], first)
                dve.tensor_copy(tci[0:W, o5 + 3:o5 + 4], bank(7)[0:W, 4 + k:5 + k])
                dve.tensor_copy(tci[0:W, o5 + 4:o5 + 5], tc_[0:W, 11:12])
                dve.tensor_copy(tci[0:W, o5 + 5:o5 + 6], bank(7)[0:W, 6 + k:7 + k])
                ch(dve.tensor_copy(tci[0:W, o5 + 1:o5 + 3], tc_[0:W, 5:7]))
                dve.sem_inc(s["win_tab"], 1)
            dve.wait_ge(s["cond_e"], 1)
            ch(dve.tensor_scalar(ez, ez, 1.0, None, ALU.add))
            ch(dve.reciprocal(ez, ez))
            dve.scalar_tensor_tensor(hh, ps_s[0:CD, 0:N], fb1, ez, ALU.add, ALU.mult).then_inc(s["cond_h"], 1)
            dve.wait_ge(s["cond_c"], 1)
            dve.tensor_scalar(ct[0:CD], ps_t[0:CD, 0:N], fb2, None, ALU.add).then_inc(s["ct_ready"], 1)
            dve.wait_ge(s["tab_in"], 32)
            def onehots(w):
                first = dve.value_load(tabc[0:1, ds(TW * w, 1)], min_val=0, max_val=CH)
                u0 = dve.value_load(tabc[0:1, ds(TW * w + 1, 1)], min_val=0, max_val=CW * CH)
                nu = dve.value_load(tabc[0:1, ds(TW * w + 2, 1)], min_val=0, max_val=CW * CH)
                with dve.Fori(0, nu) as k_:
                    for j in range(CU):
                        c = nc.s_assert_within(first + CU * k_ + j, 0, CHP - 1)
                        dve.wait_ge(s["oh_used"], CU * u0 + CU * k_ + j + 1)
                        dve.tensor_scalar(OS[:, j, :], iota16[:, 0:N], ed[:, 0, ds(c, 1)], None, ALU.is_equal)
                        dve.tensor_scalar(OD[:, j, 0:TR], iota16[:, ds(w * TR, TR)], ed[:, 1, ds(c, 1)], None,
                                          ALU.is_equal).then_inc(s["oh_ready"], 1)

            def bias(w, b):
                Lw = Lb[:, :, ds(w * TR, TR)]
                dve.wait_ge(s["cnt_relu"], w + 3)
                dve.tensor_scalar(Lw, counts(b), 0.5, NEG, ALU.is_lt, ALU.mult).then_inc(s["cnt_neg"], 1)
                dve.wait_ge(s["cnt_ln"], w + 1)
                dve.wait_ge(s["cnt_neg"], w + 3)
                dve.scalar_tensor_tensor(Lw, lnt[:, b], 1.0 / SCALE, Lw, ALU.mult, ALU.add
                                         ).then_inc(s["dve_cnt"], 1)
                dve.wait_ge(s["dve_cnt"], w + 3)

            onehots(0)
            with dve.Fori(0, CW // 2 - 1) as wp:
                for b in range(2):
                    onehots(2 * wp + b + 1)
                    bias(2 * wp + b, b)
            onehots(CW - 1)
            for b in range(2):
                bias(CW - 2 + b, b)
            dve.sem_inc(s["bias_done"], 1)

            def layer_norm(n, r, t, c, add=None, banks=None):
                scale, shift = banks or (ps_sc, ps_bi)
                x_ = xs[:, t, :]
                if add is not None:
                    dve.tensor_tensor(x_, x_, add, ALU.add).then_inc(s["x_added"], 1)
                    dve.wait_ge(s["x_added"], c)
                r4, r2 = r % 4, r % 2
                ins = dve.bn_stats(st6[:, r4, :], x_)
                ins.then_inc(s["dve_ln"], 1)
                dve.wait_ge(s["dve_ln"], 5 * n + 1)
                dve.sem_inc(s["gate"], 1)
                dve.bn_aggr(mv[:, r4, :], st6[:, r4, :]).then_inc(s["stats"], 1)
                dve.wait_ge(s["std"], n + 1)
                dve.reciprocal(rstd[:, r4:r4 + 1], sd[:, r4:r4 + 1]).then_inc(s["dve_ln"], 1)
                dve.wait_ge(s["dve_ln"], 5 * n + 2)
                dve.tensor_scalar(xnb[0:TR, r2], x_, mv[:, r4, 0:1], rstd[:, r4:r4 + 1], ALU.subtract, ALU.mult
                                  ).then_inc(s["dve_ln"], 1)
                dve.wait_ge(s["dve_ln"], 5 * n + 3)
                dve.wait_ge(s["cond_ps"], n + 1)
                dve.scalar_tensor_tensor(xnb[0:TR, r2], scale[0:TR, :], 1.0, xnb[0:TR, r2], ALU.add, ALU.mult
                                         ).then_inc(s["dve_ln"], 1)
                dve.wait_ge(s["dve_ln"], 5 * n + 4)
                dve.tensor_tensor(ybuf[0:TR, r4], shift[0:TR, :], xnb[0:TR, r2], ALU.add).then_inc(s["y_ready"], 1)
                dve.sem_inc(s["dve_ln"], 1)

            def y_low(n, t, bk):
                dve.wait_ge(s["lnT_ready"], n + 1)
                dve.tensor_tensor(y_lo(t), ps_tt[bk][:, 0:KC * P].rearrange("p (k c) -> p k c", k=KC)[:, :, 0:TR],
                                  yT_hi[:, :, t * TR:(t + 1) * TR].bitcast(F32), ALU.subtract).then_inc(s["y_low"], 1)

            def split_weights(g, m, name, per):
                dve.wait_ge(s[name], per * (g + 1))
                dve.tensor_copy(w_hi[:, m], wqkv[:, m]).then_inc(s["w_hi"], 1)
                dve.wait_ge(s["w_hi"], 2 * g + 1 + m.start // 2)
                dve.tensor_tensor(w_lo[:, m], wqkv[:, m], w_hi[:, m].bitcast(F32), ALU.subtract
                                  ).then_inc(s["w_split"], 1)

            def split_qk(g):
                split_weights(g, slice(0, 2), "wqk_in", 64)

            def split_v(g):
                split_weights(g, slice(2, 3), "wv_in", 32)

            def around_blocks(t):
                ch2 = Chain(dve, s["dve_fin"], 3 * t)
                dve.wait_ge(s["x0_in%d" % (t % 4)], 16 * (t // 4 + 1))
                ch2(dve.tensor_tensor(xsum[:, t % 2], xs[:, t, :], x0t[:, t % 4], ALU.add))
                ch2(dve.bn_stats(fst6[:, t % 2, :], xsum[:, t % 2]))
                dve.bn_aggr(fmv[:, t % 2, :], fst6[:, t % 2, :]).then_inc(s["fin_x"], 1)
                dve.wait_ge(s["fin_std"], t + 1)
                ch2(dve.reciprocal(frstd[:, t % 2:t % 2 + 1], fsd[:, t % 2:t % 2 + 1]))
                dve.tensor_scalar(xs[:, t, :], xsum[:, t % 2], fmv[:, t % 2, 0:1], frstd[:, t % 2:t % 2 + 1],
                                  ALU.subtract, ALU.mult).then_inc(s["x1_ready"], 1)
                dve.wait_ge(s["x1_ready"], t + 1)

            dve.wait_ge(s["mlpw_in"], 16)
            split_qk(0)
            split_v(0)
            dve.wait_ge(s["x_in"], 16)
            for n in range(NT):
                if n >= 4:
                    dve.wait_ge(s["ln_t"], n - 3)
                layer_norm(n, n, n, None, banks=FIRST_LN[n % 2])
                if n:
                    y_low(n - 1, n - 1, (n - 1) % 2)
            y_low(NT - 1, NT - 1, (NT - 1) % 2)

            def kq_low(g, n):
                dve.wait_ge(s["proj_ev"], 3 * g + n + 2)
                for m, src, c in kq_pieces(n):
                    last = dve.scalar_tensor_tensor(qk_lo[:, m, c], src, bqk[:, m:m + 1], qk_hi[:, m, c].bitcast(F32),
                                                    ALU.add, ALU.subtract)
                last.then_inc(s["proj_lo"], 1)

            with dve.Fori(0, NB) as i:
                def v_evac(g, b):
                    t0, tn = YCHUNKS[b]
                    dve.wait_ge(s["v_t"], 3 * g + b + 1)
                    dve.tensor_copy(V[0:TR, t0:t0 + tn], ps_v[b][0:TR]).then_inc(s["v_ready"], 1)

                def head(g, h, last):
                    for a in range(NT + 3):
                        if a == 3 and not last:
                            split_qk(g + 1)
                        if a == 5 and not last:
                            split_v(g + 1)
                        if a == NT + 2 and not last:
                            kq_low(g + 1, 0)
                            kq_low(g + 1, 1)
                        if a < NT:
                            t = a
                            dve.wait_ge(s["qk"], NT * g + t + 1)
                            if t >= 2:
                                dve.wait_ge(s["probs_t"], NT * g + t - 1)
                            dve.sem_inc(s["gate"], 1)
                            dve.tensor_tensor_reduce(out=S[0:TR, t % 2], in0=ps_s[0:TR, 0:N], in1=Lb[:, t, :],
                                                     scale=1.0, scalar=-3.0e38, op0=ALU.add, op1=ALU.max,
                                                     accum_out=mx[:, t:t + 1]).then_inc(s["scored"], 1)
                            dve.wait_ge(s["scored"], NT * g + t + 1)
                            dve.tensor_scalar(nmx[:, t:t + 1], mx[:, t:t + 1], -SCALE, 1.0e20, ALU.mult, ALU.min
                                              ).then_inc(s["negmax"], 1)
                        if a == 0:
                            v_evac(g, 0)
                            v_evac(g, 1)
                        if a == 2:
                            v_evac(g, 2)
                        if 0 <= a - 1 < NT:
                            t = a - 1
                            dve.wait_ge(s["exped"], NT * g + t + 1)
                            dve.scalar_tensor_tensor(rrec[:, t:t + 1], mx[:, t:t + 1], NEG / 2, den[:, t:t + 1],
                                                     ALU.is_lt, ALU.add).then_inc(s["dve_head"], 1)
                            dve.wait_ge(s["dve_head"], NT * g + t + 1)
                            dve.reciprocal(rden[:, t:t + 1], rrec[:, t:t + 1]).then_inc(s["rden_ready"], 1)
                        if a >= 4 and a % 2 == 0:
                            q = (a - 4) // 2
                            dve.wait_ge(s["pv"], NP * g + q + 1)
                            dve.wait_ge(s["r_ready"], NP * g + q + 1)
                            dve.tensor_tensor(OT[:, ds(h, 1), q * 2 * TR:(q + 1) * 2 * TR].rearrange("p o c -> p (o c)"),
                                              ps_o[:, 0, 0:2 * TR], rb[:, :], ALU.mult
                                              ).then_inc(s["ot_ready"], 1)
                    if not last:
                        kq_low(g + 1, 2)

                for n in range(3):
                    kq_low(i * NH, n)
                with dve.Fori(0, NH - 1) as h:
                    head(i * NH + h, h, False)
                head(i * NH + NH - 1, NH - 1, True)
                nb = ln_base(i)
                dve.wait_ge(s["x_in"], 16 * (i + 2))
                for st in STEPS:
                    for kind, t in st:
                        if kind == "E":
                            n = LNQ["D", t]
                            with dve.If(i < NB - 1):
                                if t % 2 == 0:
                                    for j in (t, t + 1):
                                        dve.wait_ge(s["x_out%d" % (j % 4)],
                                                    16 * (len(range(j % 4, NT, 4)) * (i + 1) + j // 4 + 1))
                                y_low(nb + n, t, (n + NT) % 2)
                                if t == NT - 3:
                                    split_qk(i * NH + NH)
                                    split_v(i * NH + NH)
                            with dve.If(i > NB - 2):
                                dve.wait_ge(s["y_low"], NT * (i + 1) + t)
                                dve.sem_inc(s["y_low"], 1)
                        if kind in "AD":
                            n = LNQ[kind, t]
                            dve.wait_ge(s["wo_ps"], NLN * i + n + 1)
                            dve.wait_ge(s["ln_t"], nb + n - 3)
                            if kind == "A":
                                layer_norm(nb + n, n + NT, t, NLN * i + n + 1, add=ps_a[n % 2][0:TR, :])
                                continue
                            dve.sem_inc(s["gate"], 1)
                            with dve.If(i < NB - 1):
                                layer_norm(nb + n, n + NT, t, NLN * i + n + 1, add=ps_a[n % 2][0:TR, :])
                            with dve.If(i > NB - 2):
                                dve.tensor_tensor(xs[:, t, :], xs[:, t, :], ps_a[n % 2][0:TR, :], ALU.add
                                                  ).then_inc(s["x_added"], 1)
                                for name, per in (("stats", 1), ("y_ready", 1), ("dve_ln", 5)):
                                    dve.wait_ge(s[name], per * (nb + n))
                                    dve.sem_inc(s[name], per)
                                dve.wait_ge(s["x_added"], NLN * i + n + 1)
                                around_blocks(t)

            dve.wait_ge(s["base_in"], 16 * (BS + 1))
            dve.wait_ge(s["x1_ready"], NT)
            dve.wait_ge(s["coef_done"], CH // CG)

            def coefficients(w, lo, st, c, oh):
                ohx, cox = ("dve_rg", "rg_coef") if oh == 0 else ("dve_rgx", "rg_xcoef")
                return (dve.tensor_tensor(OH[:, oh], iota16[:, ds(lo, WD)].unsqueeze(1).broadcast_to([P, RU, WD]),
                                          ed[:, 1, ds(c, RU)].unsqueeze(2).broadcast_to([P, RU, WD]),
                                          ALU.is_equal).then_inc(s[ohx], 1),
                        lambda: dve.tensor_tensor(CO[:, st].rearrange("p j (n b) -> p j n b", b=BS),
                                                  OH[:, oh].unsqueeze(3).broadcast_to([P, RU, WD, BS]),
                                                  coef[:, ds(c, RU), :].unsqueeze(2).broadcast_to([P, RU, WD, BS]),
                                                  ALU.mult).then_inc(s[cox], 1))[1]

            def window(T, j, used):
                w = T * JW + j
                st = j % NS
                lo = T * TR + j * WD
                first = entry(dve, w, FIRST, CH)
                nu = entry(dve, w, UNITS)
                if used is not None:
                    dve.wait_ge(s["y_ps"], used)
                if not (isinstance(w, int) and w == 0):
                    dve.wait_ge(s["rg_coef"], w)
                multiply = coefficients(w, lo, st, first, 0)
                dve.wait_ge(s["dve_rg"], w + 1)
                multiply()
                with dve.If(nu > 1), dve.Fori(1, nu) as k_:
                    c = nc.s_assert_within(first + RU * k_, 0, CH)
                    before = entry(dve, w, BEFORE)
                    dve.wait_ge(s["rg_used"], before + w + k_)
                    dve.wait_ge(s["rg_xcoef"], before + k_)
                    multiply = coefficients(w, lo, st, c, 1)
                    dve.wait_ge(s["dve_rgx"], before + k_)
                    multiply()

            def finish(T):
                ch3 = Chain(dve, s["dve_rgt"], 5 * T)
                dve.wait_ge(s["rel_ps"], T + 1)
                dve.tensor_tensor(ln0, xs[:, ds(T, 1), :].rearrange("p o d -> p (o d)"), bank(4)[0:TR, :],
                                  ALU.add).then_inc(s["rel_read"], 1)
                dve.wait_ge(s["rel_read"], T + 2)
                ch3(dve.tensor_tensor(ln0, ln0, hb, ALU.add))
                ch3(dve.bn_stats(st6[:, 0, :], ln0))
                dve.sem_inc(s["gate"], 1)
                ch3(dve.bn_aggr(mv[:, 0, :], st6[:, 0, :]))
                dve.sem_inc(s["rg_stats"], 1)
                dve.wait_ge(s["rg_std"], T + 1)
                ch3(dve.reciprocal(rstd[:, 0:1], sd[:, 0:1]))
                dve.wait_ge(s["out_done"], 16 * T + 16)
                dve.tensor_scalar(fo[:, 0], ln0, mv[:, 0, 0:1], rstd[:, 0:1],
                                  ALU.subtract, ALU.mult).then_inc(s["out_ready"], 1)
                dve.sem_inc(s["dve_rgt"], 1)
                dve.wait_ge(s["out_ready"], T + 1)

            for j in range(JW):
                window(0, j, j - NS + 1 if j >= NS else None)
            with dve.Fori(0, NT - 1) as T:
                for j in range(JW):
                    window(T + 1, j, T * JW + JW + j - NS + 1)
                    if j == NS - 1:
                        finish(T)
            finish(NT - 1)


_INS = ["x", "src", "dst", "edge_type_32", "edge_weight1", "node_vec1",
        "L0_gnn_f_w1", "L0_gnn_f_b1", "L0_gnn_f_w2", "L0_gnn_f_b2", "L0_gnn_s1_w", "L0_gnn_s1_b", "L0_gnn_b1_w",
        "L0_gnn_b1_b", "L0_gnn_wq", "L0_gnn_bq", "L0_gnn_wk", "L0_gnn_bk", "L0_gnn_wv", "L0_gnn_bv", "L0_gnn_wo",
        "L0_gnn_bo", "L0_gnn_s2_w", "L0_gnn_s2_b", "L0_gnn_b2_w", "L0_gnn_b2_b", "L0_gnn_m_w1", "L0_gnn_m_b1",
        "L0_gnn_m_w2", "L0_gnn_m_b2", "L1_gnn_bases", "L1_gnn_w_comp", "L1_gnn_h_bias"]


def kernel(**inputs):
    import numpy as np
    import concourse.bacc as bacc
    from concourse.bass_utils import run_bass_kernel_spmd

    nc = bacc.Bacc("TRN2", target_bir_lowering=False, num_devices=1)
    arrays, aps = {}, {}
    for name in _INS:
        a = np.ascontiguousarray(inputs[name])
        arrays["in_" + name] = a
        aps[name] = nc.dram_tensor("in_" + name, a.shape, mybir.dt.from_np(a.dtype), kind="ExternalInput").ap()
    out = nc.dram_tensor("out", inputs["x"].shape, F32, kind="ExternalOutput").ap()
    graph_kernel(nc, aps, out)
    r = run_bass_kernel_spmd(nc, [arrays], core_ids=[0])
    return r.results[0]["out"]
```
